# Optimizing a Trainium2 kernel written in Bass

```python
import numpy as np
import jax
import jax.numpy as jnp

def _softmax(x, axis=-1):
    return jax.nn.softmax(x, axis=axis)

def _gelu(x):
    return jax.nn.gelu(x, approximate=True)

def _silu(x):
    return jax.nn.silu(x)

def _sigmoid(x):
    return jax.nn.sigmoid(x)

def _layernorm(x, axis=-1, eps=1e-05):
    m = jnp.mean(x, axis=axis, keepdims=True)
    v = jnp.var(x, axis=axis, keepdims=True)
    return (x - m) / jnp.sqrt(v + eps)

def _scatter_add(tgt, idx, src, axis=0):
    return tgt.at[idx].add(src)

def _segment_sum(src, seg, n):
    return jax.ops.segment_sum(src, seg, n)
kernel_name = 'mk_seq_preln_d1_jaxref_r4_4ca510'

def setup_inputs(seed: int=0):
    np.random.seed(seed)
    _w = jnp.asarray

    def _L0_attn_setup():
        import jax, jax.numpy as jnp
        import numpy as np
        NUM_HEADS = 16
        HIDDEN = 256
        HEAD_DIM = HIDDEN // NUM_HEADS
        GROUP_SIZE = 64

        def _attention(q, k, v, head_dim):
            scores = jnp.einsum('bghqd,bghkd->bghqk', q, k) / head_dim ** 0.5
            w = jax.nn.softmax(scores, axis=-1)
            return jnp.einsum('bghqk,bghkd->bghqd', w, v)
        key = jax.random.key(seed)
        k1, k2, k3 = jax.random.split(key, 3)
        hidden_states = jax.random.normal(k1, (2, 2048, HIDDEN), dtype=jnp.float32)
        w_qkv = jax.random.normal(k2, (3 * HIDDEN, HIDDEN), dtype=jnp.float32) * 0.02
        b_qkv = jax.random.normal(k3, (3 * HIDDEN,), dtype=jnp.float32) * 0.02
        return {'hidden_states': hidden_states, 'w_qkv': w_qkv, 'b_qkv': b_qkv}
    _L0_attn_in = _L0_attn_setup()

    def _L0_ffn_setup():
        import jax, jax.numpy as jnp
        import numpy as np
        EPS = 1e-05

        def _layernorm(x, w, b):
            mu = jnp.mean(x, axis=-1, keepdims=True)
            var = jnp.mean((x - mu) ** 2, axis=-1, keepdims=True)
            return (x - mu) * jax.lax.rsqrt(var + EPS) * w + b

        def _rope_tables(T, D, base=10000.0):
            inv_freq = 1.0 / base ** (jnp.arange(0, D, 2, dtype=jnp.float32) / D)
            t = jnp.arange(T, dtype=jnp.float32)
            freqs = jnp.einsum('i,j->ij', t, inv_freq)
            emb = jnp.concatenate([freqs, freqs], axis=-1)
            return (jnp.cos(emb), jnp.sin(emb))

        def _rotate_half(x):
            x1, x2 = (x[..., :x.shape[-1] // 2], x[..., x.shape[-1] // 2:])
            return jnp.concatenate([-x2, x1], axis=-1)

        def _attn(x, ln_w, ln_b, conv_w, attn_w, proj_w, n_head):
            B, T, C = x.shape
            D = C // n_head
            h = _layernorm(x, ln_w, ln_b)
            hc = jnp.transpose(h, (0, 2, 1))
            hc = jnp.pad(hc, ((0, 0), (0, 0), (2, 0)))
            hc = jax.lax.conv_general_dilated(hc, conv_w, window_strides=(1,), padding='VALID', dimension_numbers=('NCH', 'OIH', 'NCH'), feature_group_count=C)
            h = jnp.transpose(hc, (0, 2, 1))
            qkv = h @ attn_w
            q, k, v = jnp.split(qkv, 3, axis=-1)
            q = q.reshape(B, T, n_head, D)
            k = k.reshape(B, T, n_head, D)
            v = v.reshape(B, T, n_head, D)
            cos, sin = _rope_tables(T, D)
            cos = cos[None, :, None, :]
            sin = sin[None, :, None, :]
            q = q * cos + _rotate_half(q) * sin
            k = k * cos + _rotate_half(k) * sin
            scores = jnp.einsum('bqhd,bkhd->bhqk', q, k) / jnp.sqrt(jnp.float32(D))
            causal = jnp.tril(jnp.ones((T, T), dtype=bool))
            scores = jnp.where(causal, scores, jnp.float32(-1e+30))
            p = jax.nn.softmax(scores, axis=-1)
            y = jnp.einsum('bhqk,bkhd->bqhd', p, v).reshape(B, T, C)
            return y @ proj_w

        def _moe(x, ln_w, ln_b, router_w, expert_wv, expert_proj):
            h = _layernorm(x, ln_w, ln_b)
            logits = h @ router_w
            expert_idx = jnp.argmax(logits, axis=-1)
            E = router_w.shape[-1]
            out = jnp.zeros_like(x)
            for e in range(E):
                gv = h @ expert_wv[e]
                gate_raw, value = jnp.split(gv, 2, axis=-1)
                y = gate_raw * jax.nn.sigmoid(gate_raw) * value @ expert_proj[e]
                out = out + jnp.where((expert_idx == e)[..., None], y, 0.0)
            return out
        C, H, E, B, T = (256, 16, 4, 4, 256)
        Dff = 4 * C
        key = jax.random.key(seed)
        ks = jax.random.split(key, 8)
        s = 0.02
        return {'x': jax.random.normal(ks[0], (B, T, C), dtype=jnp.float32), 'ln1_w': jnp.ones((C,), jnp.float32), 'ln1_b': jnp.zeros((C,), jnp.float32), 'ln2_w': jnp.ones((C,), jnp.float32), 'ln2_b': jnp.zeros((C,), jnp.float32), 'conv_w': jax.random.normal(ks[1], (C, 1, 3), dtype=jnp.float32) * 0.1, 'attn_w': jax.random.normal(ks[2], (C, 3 * C), dtype=jnp.float32) * s, 'proj_w': jax.random.normal(ks[3], (C, C), dtype=jnp.float32) * s, 'router_w': jax.random.normal(ks[4], (C, E), dtype=jnp.float32) * s, 'expert_wv': jax.random.normal(ks[5], (E, C, 2 * Dff), dtype=jnp.float32) * s, 'expert_proj': jax.random.normal(ks[6], (E, Dff, C), dtype=jnp.float32) * s}
    _L0_ffn_in = _L0_ffn_setup()
    _d = {'L0_attn_hidden_states': _L0_attn_in['hidden_states'], 'L0_attn_w_qkv': _L0_attn_in['w_qkv'], 'L0_attn_b_qkv': _L0_attn_in['b_qkv'], 'L0_ffn_ln1_w': _L0_ffn_in['ln1_w'], 'L0_ffn_ln1_b': _L0_ffn_in['ln1_b'], 'L0_ffn_ln2_w': _L0_ffn_in['ln2_w'], 'L0_ffn_ln2_b': _L0_ffn_in['ln2_b'], 'L0_ffn_conv_w': _L0_ffn_in['conv_w'], 'L0_ffn_attn_w': _L0_ffn_in['attn_w'], 'L0_ffn_proj_w': _L0_ffn_in['proj_w'], 'L0_ffn_router_w': _L0_ffn_in['router_w'], 'L0_ffn_expert_wv': _L0_ffn_in['expert_wv'], 'L0_ffn_expert_proj': _L0_ffn_in['expert_proj']}
    _x0 = _d['L0_attn_hidden_states']
    _d['L0_attn_hidden_states'] = jax.random.normal(jax.random.fold_in(jax.random.key(seed), 1), (2, 2048, 256), dtype=_x0.dtype)
    del _x0
    return _d

def reference(L0_attn_hidden_states, L0_attn_w_qkv, L0_attn_b_qkv, L0_ffn_ln1_w, L0_ffn_ln1_b, L0_ffn_ln2_w, L0_ffn_ln2_b, L0_ffn_conv_w, L0_ffn_attn_w, L0_ffn_proj_w, L0_ffn_router_w, L0_ffn_expert_wv, L0_ffn_expert_proj):

    def _L0_attn_ref(hidden_states, w_qkv, b_qkv):
        import jax, jax.numpy as jnp
        import numpy as np
        NUM_HEADS = 16
        HIDDEN = 256
        HEAD_DIM = HIDDEN // NUM_HEADS
        GROUP_SIZE = 64

        def _attention(q, k, v, head_dim):
            scores = jnp.einsum('bghqd,bghkd->bghqk', q, k) / head_dim ** 0.5
            w = jax.nn.softmax(scores, axis=-1)
            return jnp.einsum('bghqk,bghkd->bghqd', w, v)
        b, n, _ = hidden_states.shape
        h, d, G = (NUM_HEADS, HEAD_DIM, GROUP_SIZE)
        ng = n // G
        half = G // 2
        qkv = hidden_states @ w_qkv.T + b_qkv
        qkv = qkv.reshape(b, n, 3, h, d).transpose(2, 0, 3, 1, 4)
        q, k, v = (qkv[0], qkv[1], qkv[2])

        def grp(x):
            return x.reshape(b, h, ng, G, d).transpose(0, 2, 1, 3, 4)
        q, k, v = (grp(q), grp(k), grp(v))
        q1, q2 = (q[:, :, :, :half], q[:, :, :, half:])
        k1, k2 = (k[:, :, :, :half], k[:, :, :, half:])
        v1, v2 = (v[:, :, :, :half], v[:, :, :, half:])
        q2 = jnp.roll(q2, -half, axis=2)
        k2 = jnp.roll(k2, -half, axis=2)
        v2 = jnp.roll(v2, -half, axis=2)
        out1 = _attention(q1, k1, v1, d)
        out2 = _attention(q2, k2, v2, d)
        out = jnp.concatenate([out1, out2], axis=3)
        out = jnp.concatenate([out[:, :, :, :half], jnp.roll(out[:, :, :, half:], half, axis=2)], axis=3)
        out = out.transpose(0, 2, 1, 3, 4).reshape(b, n, h * d)
        return out

    def _L0_ffn_ref(x, ln1_w, ln1_b, ln2_w, ln2_b, conv_w, attn_w, proj_w, router_w, expert_wv, expert_proj):
        import jax, jax.numpy as jnp
        import numpy as np
        EPS = 1e-05

        def _layernorm(x, w, b):
            mu = jnp.mean(x, axis=-1, keepdims=True)
            var = jnp.mean((x - mu) ** 2, axis=-1, keepdims=True)
            return (x - mu) * jax.lax.rsqrt(var + EPS) * w + b

        def _rope_tables(T, D, base=10000.0):
            inv_freq = 1.0 / base ** (jnp.arange(0, D, 2, dtype=jnp.float32) / D)
            t = jnp.arange(T, dtype=jnp.float32)
            freqs = jnp.einsum('i,j->ij', t, inv_freq)
            emb = jnp.concatenate([freqs, freqs], axis=-1)
            return (jnp.cos(emb), jnp.sin(emb))

        def _rotate_half(x):
            x1, x2 = (x[..., :x.shape[-1] // 2], x[..., x.shape[-1] // 2:])
            return jnp.concatenate([-x2, x1], axis=-1)

        def _attn(x, ln_w, ln_b, conv_w, attn_w, proj_w, n_head):
            B, T, C = x.shape
            D = C // n_head
            h = _layernorm(x, ln_w, ln_b)
            hc = jnp.transpose(h, (0, 2, 1))
            hc = jnp.pad(hc, ((0, 0), (0, 0), (2, 0)))
            hc = jax.lax.conv_general_dilated(hc, conv_w, window_strides=(1,), padding='VALID', dimension_numbers=('NCH', 'OIH', 'NCH'), feature_group_count=C)
            h = jnp.transpose(hc, (0, 2, 1))
            qkv = h @ attn_w
            q, k, v = jnp.split(qkv, 3, axis=-1)
            q = q.reshape(B, T, n_head, D)
            k = k.reshape(B, T, n_head, D)
            v = v.reshape(B, T, n_head, D)
            cos, sin = _rope_tables(T, D)
            cos = cos[None, :, None, :]
            sin = sin[None, :, None, :]
            q = q * cos + _rotate_half(q) * sin
            k = k * cos + _rotate_half(k) * sin
            scores = jnp.einsum('bqhd,bkhd->bhqk', q, k) / jnp.sqrt(jnp.float32(D))
            causal = jnp.tril(jnp.ones((T, T), dtype=bool))
            scores = jnp.where(causal, scores, jnp.float32(-1e+30))
            p = jax.nn.softmax(scores, axis=-1)
            y = jnp.einsum('bhqk,bkhd->bqhd', p, v).reshape(B, T, C)
            return y @ proj_w

        def _moe(x, ln_w, ln_b, router_w, expert_wv, expert_proj):
            h = _layernorm(x, ln_w, ln_b)
            logits = h @ router_w
            expert_idx = jnp.argmax(logits, axis=-1)
            E = router_w.shape[-1]
            out = jnp.zeros_like(x)
            for e in range(E):
                gv = h @ expert_wv[e]
                gate_raw, value = jnp.split(gv, 2, axis=-1)
                y = gate_raw * jax.nn.sigmoid(gate_raw) * value @ expert_proj[e]
                out = out + jnp.where((expert_idx == e)[..., None], y, 0.0)
            return out
        n_head = 16
        x = x + _attn(x, ln1_w, ln1_b, conv_w, attn_w, proj_w, n_head)
        x = x + _moe(x, ln2_w, ln2_b, router_w, expert_wv, expert_proj)
        return x
    x = L0_attn_hidden_states
    x = x + _L0_attn_ref(_layernorm(x, axis=-1), L0_attn_w_qkv, L0_attn_b_qkv)
    x = x + _L0_ffn_ref(_layernorm(x, axis=-1), L0_ffn_ln1_w, L0_ffn_ln1_b, L0_ffn_ln2_w, L0_ffn_ln2_b, L0_ffn_conv_w, L0_ffn_attn_w, L0_ffn_proj_w, L0_ffn_router_w, L0_ffn_expert_wv, L0_ffn_expert_proj)
    return x

_drawn_inputs = setup_inputs


def setup_inputs(seed=0):
    import zlib

    import numpy as np

    out = dict(_drawn_inputs(seed))
    spreads = {'L0_ffn_ln1_w': (1.0, 0.6),
     'L0_ffn_ln1_b': (0.0, 0.8),
     'L0_ffn_ln2_w': (1.0, 0.6),
     'L0_ffn_ln2_b': (0.0, 0.8)}
    factors = {'L0_ffn_conv_w': 8.0,
     'L0_ffn_attn_w': 8.0,
     'L0_ffn_proj_w': 8.0,
     'L0_ffn_router_w': 3.443,
     'L0_ffn_expert_wv': 2.947,
     'L0_ffn_expert_proj': 2.955}
    for name, (base, spread) in spreads.items():
        noise = np.random.default_rng([zlib.crc32(name.encode()), seed]).standard_normal(out[name].shape)
        drawn = base * np.exp(spread * noise) if base else spread * noise
        out[name] = jnp.asarray(drawn.astype(out[name].dtype))
    for name, factor in factors.items():
        out[name] = (out[name] * factor).astype(out[name].dtype)
    return out
```

```python
import concourse.bass as bass
from concourse import mybir
from contextlib import ExitStack

FP32 = mybir.dt.float32
BF16 = mybir.dt.bfloat16
ALU = mybir.AluOpType
ACT = mybir.ActivationFunctionType
AX = mybir.AxisListType

B = 2
T = 2048
C = 256
P = 128
NT = T // P
CH = C // P
H = 16
D = C // H
HG = 4
NG = H // HG
QC = 512
NC = T // QC
TC = QC // P
NTERM = 6
KR = NTERM * D
MROW = KR
VW = D + 1
NP = 8
HD = 32
ONES2 = 1.0019378662109375
E4 = 4
F = 4 * C
NE = B * NT + E4 - 1
EPS = 1e-5
TERMS = [[0, 0, 1, 1, 0, 2], [0, 1, 0, 1, 2, 0]]



class Phase:

    def __init__(self, nc, ctx, tag):
        self.nc, self.ctx, self.tag = nc, ctx, tag

    def sb(self, name, shape, dt):
        return self.ctx.enter_context(self.nc.sbuf_tensor(name + self.tag, shape, dt))

    def sem(self, name):
        return self.ctx.enter_context(self.nc.semaphore(name + self.tag))


def attention_phase(nc, PS, causal, src, add, w_dram, bias, ln_w, ln_b, conv_w, rope_c, rope_s,
                    mask_qk, mask_kq, identf, identb, m_dram, y_out, x_out, h_out):
    ctx = ExitStack()
    with ctx:
        ph = Phase(nc, ctx, "B" if causal else "A")
        sb, sem = ph.sb, ph.sem

        W = sb("W", [P, CH, 3 * C], FP32)
        XY = sb("XY", [P, NT, C], FP32)
        partsT = sb("partsT", [P, 3, 2, CH, T], BF16)
        stk = sb("stk", [P, 2, 2, HG, T], BF16)
        arena = sb("arena", [P, CH * (T + 2)], FP32)
        hT = arena[:, :].rearrange("p (c t) -> p c t", c=CH)
        PR = arena[:, 0:NP * QC].rearrange("p (n q) -> p n q", n=NP)
        if causal:
            AD = stk[:, 0, :, :, :].rearrange("p a b t -> p (a b t)").bitcast(FP32)[:, 0:NT * C].rearrange("p (n c) -> p n c", c=C)
            hc = stk[:, 1, :, :, :].rearrange("p a b t -> p (a b t)").bitcast(FP32)[:, 0:CH * T].rearrange("p (c t) -> p c t", c=CH)
        V = sb("V", [P, NT, H, VW], FP32)
        hn = sb("hn", [P, 2, C], FP32)
        qk = sb("qk", [P, 2, 2 * C], FP32)
        r1 = sb("r1", [P, 2, 2 * C], FP32)
        parts = sb("parts", [P, 2, 3, 2 * C], BF16)
        OT = sb("OT", [P, 2, QC], FP32)
        ra = OT[:, 0, :]
        rb = OT[:, 1, :]
        IDF = sb("IDF", [P, P], FP32)
        IDB = sb("IDB", [P, P], BF16)
        ZB = sb("ZB", [P, P], BF16)
        MQK = sb("MQK", [P, P], BF16)
        MKQ = sb("MKQ", [P, P], BF16)
        st = sb("st", [P, NT, 6], FP32)
        mv = sb("mv", [P, NT, 2], FP32)
        ve = sb("ve", [P, NT], FP32)
        sd = sb("sd", [P, NT], FP32)
        rs = sb("rs", [P, NT], FP32)
        mx = sb("mx", [P, HG * NT, 2], FP32)
        mm = sb("mm", [P, HG * NT], FP32)
        nmb = sb("nmb", [P, HG * NT], BF16)
        nmr = sb("nmr", [HG * NT, P], BF16)
        rden = sb("rden", [P, TC, HG], FP32)
        if causal:
            RC = sb("RC", [P, NT, 2, D], FP32)
            RS = sb("RS", [P, NT, 2, D], FP32)
            LW = sb("LW", [P, CH], FP32)
            LB = sb("LB", [P, CH], FP32)
            CW = sb("CW", [P, CH, 3], FP32)
        else:
            BI = sb("BI", [P, 3 * C], FP32)
            BQ = sb("BQ", [P, C], FP32)
        proj_in = hc if causal else hT[:, :, 2:T + 2]
        pT = [PS[:, i, 0:CH * P].rearrange("p (c t) -> p c t", c=CH) for i in (0, 1)]
        pQ = [PS[:, i, :] for i in (2, 3)]
        pV = [PS[:, i, 0:C] for i in (4, 5)]
        pP = [PS[:, i, :].bitcast(BF16)[:, 0:6 * P].rearrange("p (n t) -> p n t", n=6) for i in (6, 7)]
        pM = [PS[:, i:i + 2, :].rearrange("p a b -> p (a b)") for i in (0, 2)]
        pS = [PS[:, i, :] for i in (4, 5)]
        pO = PS[:, 6, :]
        pX = PS[:, 7, :]

        consts = sem("consts")
        rows = sem("rows")
        zeroed = sem("zeroed")
        dch = sem("dch")
        ach = sem("ach")
        sum_ready = sem("sum_ready")
        var_ready = sem("var_ready")
        sd_ready = sem("sd_ready")
        hn_ready = sem("hn_ready")
        tp_done = sem("tp_done")
        ht_ready = sem("ht_ready")
        hc_ready = sem("hc_ready")
        qkv_done = sem("qkv_done")
        v_ready = sem("v_ready")
        qk_ready = sem("qk_ready")
        hi_ready = sem("hi_ready")
        r1_ready = sem("r1_ready")
        mid_ready = sem("mid_ready")
        lo_ready = sem("lo_ready")
        pt_done = sem("pt_done")
        partsT_ready = sem("partsT_ready")
        x_stored = sem("x_stored")
        stk_loaded = [sem("stk_loaded0"), sem("stk_loaded1")]
        mx_scored = sem("mx_scored")
        mx_taken = sem("mx_taken")
        nm_ready = sem("nm_ready")
        nmr_ready = sem("nmr_ready")
        m_stored = sem("m_stored")
        m_loaded = sem("m_loaded")
        s_done = sem("s_done")
        e_done = sem("e_done")
        pv_done = sem("pv_done")
        ot_ready = sem("ot_ready")
        x_done = sem("x_done")
        y_ready = sem("y_ready")
        y_stored = sem("y_stored")

        LQ = 5 if causal else 1
        LP = LQ + 2
        N_CONST = 16 * (10 if causal else 6)
        N_LOAD = 2 * NTERM * HG
        E = HG if causal else 1
        if causal:
            STEPS = [(c, kt, max(0, kt - TC * c) * P) for c in range(NC) for kt in range(TC * (c + 1))]
        else:
            STEPS = [(c, TC * c + i, i * P) for c in range(NC) for i in range(TC)]
        NS = len(STEPS)
        LAST = [max(s for s in range(NS) if STEPS[s][0] == c) for c in range(NC)]
        if causal:
            UNITS = [(j, i, k0, min(2 * QC, P * (i + 1) - k0))
                     for j in range(HG) for i in range(NT) for k0 in range(0, P * (i + 1), 2 * QC)]
        else:
            UNITS = [(0, i, P * i, P) for i in range(NT)]
        NU = len(UNITS)
        PVLAG = 1 if causal else 2
        NX = NC + 1

        def due(s):
            return range(NU * s // NS, NU * (s + 1) // NS) if s < NS else ()

        block = ctx.enter_context(nc.Block())

        @block.sync
        def _(sp):
            sp.dma_start(W[:, :, :], w_dram).then_inc(consts, 16)
            sp.dma_start(IDF[:, :], identf).then_inc(consts, 16)
            sp.dma_start(IDB[:, :], identb).then_inc(consts, 16)
            sp.dma_start(MQK[:, :], mask_qk).then_inc(consts, 16)
            sp.dma_start(MKQ[:, :], mask_kq).then_inc(consts, 16)
            if causal:
                sp.dma_start(RC[:, :, :, :], rope_c).then_inc(consts, 16)
                sp.dma_start(RS[:, :, :, :], rope_s).then_inc(consts, 16)
                sp.dma_start(LW[:, :], ln_w).then_inc(consts, 16)
                sp.dma_start(LB[:, :], ln_b).then_inc(consts, 16)
                sp.dma_start(CW[:, :, :], conv_w).then_inc(consts, 16)
            else:
                sp.dma_start(BI[:, :], bias).then_inc(consts, 16)
            for b in range(B):
                if b:
                    sp.wait_ge(y_stored, 16 * NT * b)
                    sp.wait_ge(s_done, E * NS * NG * b)
                sp.dma_start(XY[:, :, :], src(b)).then_inc(rows, 16)
                if causal:
                    sp.dma_start(AD[:, :, :], add(b)).then_inc(rows, 16)
                    sp.wait_ge(sum_ready, b + 1)
                    sp.dma_start(x_out(b), XY[:, :, :]).then_inc(x_stored, 16)
                    sp.wait_ge(var_ready, 2 * b + 2)
                    sp.dma_start(h_out(b), AD[:, :, :]).then_inc(x_stored, 16)
                sp.wait_ge(partsT_ready, NT * (b + 1))
                if causal:
                    sp.wait_ge(x_stored, 32 * (b + 1))
                for g in range(NG):
                    if g >= 2 or b:
                        sp.wait_ge(s_done, E * NS * (NG * b + g - 1))
                    for a in range(2):
                        for n in range(NTERM):
                            for j in range(HG):
                                half, row = divmod((HG * g + j) * D, P)
                                sp.dma_start(stk[n * D:(n + 1) * D, g % 2, a, j, :],
                                             partsT[row:row + D, TERMS[a][n], a, half, :])\
                                  .then_inc(stk_loaded[g % 2], 16)
                sp.wait_ge(y_ready, NC * NG * (b + 1))
                for i in range(NT):
                    sp.dma_start(y_out(b, i), XY[:, i, :] if causal else XY[:, i, :].rearrange("p (h d) -> p h d", h=H))\
                      .then_inc(y_stored, 16)
            sp.wait_ge(y_stored, 16 * NT * B)
            if causal:
                sp.wait_ge(x_stored, 32 * B)

        @block.gpsimd
        def _(pool):
            pool.memset(ZB[:, :], 0.0).then_inc(zeroed, 1)
            pool.memset(V[:, :, :, :], 1.0).then_inc(zeroed, 1)
            for b in range(B):
                if causal:
                    pool.wait_ge(zeroed, 2 + 3 * b)
                    if b:
                        pool.wait_ge(pv_done, NS * NG * b)
                    pool.memset(hT[:, :, 0:2], 0.0).then_inc(zeroed, 1)
                for i in range(NT):
                    n = NT * b + i
                    pool.wait_ge(hi_ready, n + 1)
                    pool.tensor_tensor(r1[:, n % 2, :], qk[:, n % 2, :], parts[:, n % 2, 0, :], ALU.subtract)\
                        .then_inc(r1_ready, 1)
                    pool.wait_ge(mid_ready, n + 1)
                    pool.tensor_tensor(parts[:, n % 2, 2, :], r1[:, n % 2, :], parts[:, n % 2, 1, :], ALU.subtract)\
                        .then_inc(lo_ready, 1)
                if causal or b == 0:
                    pool.wait_ge(qkv_done, NT * (b + 1))
                    if causal:
                        pool.wait_ge(x_stored, 32 * (b + 1))
                    pool.wait_ge(lo_ready, NT * (b + 1))
                    for par in range(2):
                        if par:
                            pool.wait_ge(zeroed, 2 + (3 * b + 2 if causal else 1))
                        pool.memset(stk[MROW:MROW + 1, par, 1, :, :].rearrange("p b t -> p (b t)").bitcast(FP32),
                                    ONES2).then_inc(zeroed, 1)
                for g in range(NG):
                    pool.wait_ge(nmr_ready, NG * b + g + 1)
                    pool.dma_start(m_dram[NG * b + g], nmr[:, :]).then_inc(m_stored, 16)
                    if g >= 2 or b:
                        pool.wait_ge(s_done, E * NS * (NG * b + g - 1))
                    pool.wait_ge(m_stored, 16 * (NG * b + g + 1))
                    pool.dma_start(stk[MROW:MROW + 1, g % 2, 0, :, :].rearrange("a j t -> a (j t)"),
                                   m_dram[NG * b + g].rearrange("r s -> (r s)").unsqueeze(0)).then_inc(m_loaded, 16)

        @block.scalar
        def _(act):
            def evacuate(b, i):
                n = NT * b + i
                act.wait_ge(tp_done, n + 1)
                for c in range(CH):
                    dst = hT[:, c, 2 + i * P:2 + (i + 1) * P]
                    if causal:
                        last = act.activation(dst, pT[n % 2][:, c, :], ACT.Identity, scale=LW[:, c:c + 1], bias=LB[:, c:c + 1])
                    else:
                        last = act.activation(dst, pT[n % 2][:, c, :], ACT.Copy)
                last.then_inc(ht_ready, 1)

            def high(b, i):
                n = NT * b + i
                if causal:
                    act.wait_ge(qkv_done, n + 1)
                    act.activation(V[:, i, :, 0:D], pV[n % 2].rearrange("p (h d) -> p h d", h=H), ACT.Copy).then_inc(v_ready, 1)
                act.wait_ge(qk_ready, n + 1)
                if n >= 2:
                    act.wait_ge(pt_done, n - 1)
                act.activation(parts[:, n % 2, 0, :], qk[:, n % 2, :], ACT.Copy).then_inc(hi_ready, 1)

            def middle(b, i):
                n = NT * b + i
                act.wait_ge(r1_ready, n + 1)
                act.activation(parts[:, n % 2, 1, :], r1[:, n % 2, :], ACT.Copy).then_inc(mid_ready, 1)

            act.wait_ge(consts, N_CONST)
            act.wait_ge(zeroed, 2)
            for b in range(B):
                for k in range(2 if causal else 1):
                    m = (2 if causal else 1) * b + k + 1
                    act.wait_ge(var_ready, m)
                    act.activation(sd[:, :], ve[:, :], ACT.Sqrt).then_inc(sd_ready, 1)
                if b:
                    act.wait_ge(pv_done, NS * NG * b)
                for s in range(NT + LQ + 1):
                    if s < NT:
                        evacuate(b, s)
                    if 0 <= s - LQ < NT:
                        high(b, s - LQ)
                    if 0 <= s - LQ - 1 < NT:
                        middle(b, s - LQ - 1)
                for g in range(NG):
                    for s, (c, kt, off) in enumerate(STEPS):
                        for j in range(E):
                            n = E * (NS * (NG * b + g) + s) + j
                            act.wait_ge(s_done, n + 1)
                            if n >= NP:
                                act.wait_ge(pv_done, (n - NP) // E + 1)
                            w = slice(off, QC) if causal else slice(0, QC)
                            act.activation(PR[:, n % NP, w], pS[n % 2][:, w], ACT.Exp).then_inc(e_done, 1)

        @block.vector
        def _(dve):
            chain = [0]

            def link(ins):
                chain[0] += 1
                ins.then_inc(dch, 1)
                dve.wait_ge(dch, chain[0])

            def statistics(rows_, k):
                for i in range(NT):
                    last = dve.bn_stats(st[:, i, :], rows_[:, i, :])
                link(last)
                for i in range(NT):
                    last = dve.bn_aggr(mv[:, i, :], st[:, i, :])
                link(last)
                dve.tensor_scalar(ve[:, :], mv[:, :, 1], EPS, None, ALU.add).then_inc(var_ready, 1)
                dve.wait_ge(sd_ready, k)
                link(dve.reciprocal(rs[:, :], sd[:, :]))

            def normalise(b, i):
                n = NT * b + i
                if n >= 2:
                    dve.wait_ge(tp_done, n - 1)
                dve.tensor_scalar(hn[:, n % 2, :], (AD if causal else XY)[:, i, :], mv[:, i, 0:1], rs[:, i:i + 1],
                                  ALU.subtract, ALU.mult).then_inc(hn_ready, 1)

            def convolve(b, k):
                dve.wait_ge(ht_ready, NT * b + TC * (k + 1))
                if k == 0:
                    dve.wait_ge(zeroed, 2 + 3 * b + 1)
                for tap in range(3):
                    for c in range(CH):
                        dst = hc[:, c, k * QC:(k + 1) * QC]
                        past = hT[:, c, k * QC + tap:(k + 1) * QC + tap]
                        if tap == 0:
                            last = dve.tensor_scalar(dst, past, CW[:, c, 0:1], None, ALU.mult)
                        else:
                            last = dve.scalar_tensor_tensor(out=dst, in0=past, scalar=CW[:, c, tap:tap + 1], in1=dst,
                                                            op0=ALU.mult, op1=ALU.add)
                    if tap < 2:
                        link(last)
                last.then_inc(hc_ready, 1)

            def rotate(b, i):
                n = NT * b + i
                dve.wait_ge(qkv_done, n + 1)
                if n >= 2:
                    dve.wait_ge(r1_ready, n - 1)
                s = pQ[n % 2]
                if causal:
                    if n:
                        dve.wait_ge(qk_ready, n)
                    s4 = s.rearrange("p (a h d) -> p a h d", a=2, h=H)
                    ra4 = ra.rearrange("p (a h d) -> p a h d", a=2, h=H)
                    rb4 = rb.rearrange("p (a h d) -> p a h d", a=2, h=H)
                    half = D // 2
                    for lo in (0, half):
                        hi = half - lo
                        dve.tensor_tensor(rb4[:, :, :, lo:lo + half], s4[:, :, :, hi:hi + half],
                                          RS[:, i, :, lo:lo + half].unsqueeze(2).broadcast_to([P, 2, H, half]), ALU.mult)
                    link(dve.tensor_tensor(ra4, s4, RC[:, i, :, :].unsqueeze(2).broadcast_to([P, 2, H, D]), ALU.mult))
                    dve.tensor_tensor(qk[:, n % 2, :], ra, rb, ALU.add).then_inc(qk_ready, 1)
                else:
                    dve.scalar_tensor_tensor(out=qk[:, n % 2, 0:C], in0=s[:, 0:C], scalar=D ** -0.5,
                                             in1=BQ[:, :], op0=ALU.mult, op1=ALU.add)
                    dve.tensor_tensor(qk[:, n % 2, C:2 * C], s[:, C:2 * C], BI[:, C:2 * C], ALU.add)
                    dve.tensor_tensor(V[:, i, :, 0:D], pV[n % 2].rearrange("p (h d) -> p h d", h=H),
                                      BI[:, 2 * C:3 * C].rearrange("p (h d) -> p h d", h=H), ALU.add).then_inc(qk_ready, 1)

            def parts_out(b, i):
                n = NT * b + i
                dve.wait_ge(pt_done, n + 1)
                if b and i == 0:
                    for par in range(2):
                        dve.wait_ge(stk_loaded[par], 16 * N_LOAD * (NG // 2) * b)
                dst = partsT[:, :, :, :, i * P:(i + 1) * P].rearrange("p a q c t -> p (a q c) t")
                dve.tensor_copy(dst[:, 0:6, :], pP[0])
                dve.tensor_copy(dst[:, 6:12, :], pP[1]).then_inc(partsT_ready, 1)

            def take_max(b, g, u):
                j, i, k0, w = UNITS[u]
                n = NU * (NG * b + g) + u
                dve.wait_ge(mx_scored, n + 1)
                if causal:
                    dve.reduce_max(mx[:, NT * j + i, k0 // (2 * QC):k0 // (2 * QC) + 1], pM[n % 2][:, 0:w], AX.X)\
                       .then_inc(mx_taken, 1)
                else:
                    dve.reduce_max(mx[:, i:i + NT * (HG - 1) + 1:NT, 0], pM[n % 2][:, 0:HG * P].rearrange("p (j k) -> p j k", j=HG),
                                   AX.X).then_inc(mx_taken, 1)

            def maxima_out(b, g):
                dve.wait_ge(mx_taken, NU * (NG * b + g + 1))
                link(dve.tensor_tensor(mm[:, :], mx[:, :, 0], mx[:, :, 1], ALU.max))
                dve.tensor_scalar(nmb[:, :], mm[:, :], -1.0, None, ALU.mult).then_inc(nm_ready, 1)
                dve.wait_ge(x_done, NX * (NG * b + g) + 1)
                if g or b:
                    dve.wait_ge(m_stored, 16 * (NG * b + g))
                dve.tensor_copy(nmr[:, :], pX.bitcast(BF16)[0:HG * NT, 0:P]).then_inc(nmr_ready, 1)

            def results_out(b, g, c):
                n = NC * (NG * b + g) + c
                dve.wait_ge(pv_done, NS * (NG * b + g) + LAST[c] + 1)
                dve.tensor_copy(OT[:, n % 2, :], pO).then_inc(ot_ready, 1)

            def divide(b, g, c):
                dve.wait_ge(x_done, NX * (NG * b + g) + 2 + c)
                x = pX.rearrange("p (i j w) -> p i j w", i=TC, j=HG)
                link(dve.reciprocal(rden[:, :, :], x[:, :, :, D]))
                for i in range(TC):
                    last = dve.tensor_tensor(XY[:, TC * c + i, HG * D * g:HG * D * (g + 1)].rearrange("p (j d) -> p j d", j=HG),
                                             x[:, i, :, 0:D], rden[:, i, :].unsqueeze(2).broadcast_to([P, HG, D]), ALU.mult)
                last.then_inc(y_ready, 1)

            dve.memset(mx[:, :, :], -3.0e38)
            dve.wait_ge(consts, N_CONST)
            dve.wait_ge(zeroed, 2)
            if not causal:
                link(dve.tensor_scalar(BQ[:, :], BI[:, 0:C], D ** -0.5, None, ALU.mult))
            for b in range(B):
                if causal:
                    dve.wait_ge(rows, 32 * (b + 1))
                    for i in range(NT):
                        last = dve.tensor_tensor(XY[:, i, :], XY[:, i, :], AD[:, i, :], ALU.add)
                    last.then_inc(sum_ready, 1)
                    dve.wait_ge(sum_ready, b + 1)
                    statistics(XY, 2 * b + 1)
                    for i in range(NT):
                        last = dve.tensor_scalar(AD[:, i, :], XY[:, i, :], mv[:, i, 0:1], rs[:, i:i + 1],
                                                 ALU.subtract, ALU.mult)
                    link(last)
                    statistics(AD, 2 * b + 2)
                else:
                    dve.wait_ge(rows, 16 * (b + 1))
                    statistics(XY, b + 1)
                if b:
                    dve.wait_ge(pv_done, NS * NG * b)
                for s in range(NT + LP):
                    if s < NT:
                        normalise(b, s)
                    if causal and s % TC == 0 and 0 < s <= NT:
                        convolve(b, s // TC - 1)
                    if 0 <= s - LQ < NT:
                        rotate(b, s - LQ)
                    if 0 <= s - LP < NT:
                        parts_out(b, s - LP)
                if causal:
                    dve.wait_ge(x_stored, 32 * (b + 1))
                for u in range(NU):
                    take_max(b, 0, u)
                maxima_out(b, 0)
                for g in range(NG):
                    for s in range(NS + PVLAG + 1):
                        for c in range(NC):
                            if s == LAST[c] + PVLAG:
                                results_out(b, g, c)
                            if s == LAST[c] + PVLAG + 1:
                                divide(b, g, c)
                        if g + 1 < NG:
                            for u in due(s):
                                take_max(b, g + 1, u)
                    if g + 1 < NG:
                        maxima_out(b, g + 1)

        @block.tensor
        def _(pe):
            def transpose_rows(b, i):
                n = NT * b + i
                pe.wait_ge(hn_ready, n + 1)
                if n >= 2:
                    pe.wait_ge(ht_ready, n - 1)
                for c in range(CH):
                    last = pe.transpose(pT[n % 2][:, c, :], hn[:, n % 2, c * P:(c + 1) * P], IDF[:, :])
                last.then_inc(tp_done, 1)

            def project(b, i):
                n = NT * b + i
                if causal:
                    pe.wait_ge(hc_ready, NC * b + i // TC + 1)
                else:
                    pe.wait_ge(ht_ready, n + 1)
                if n >= 2:
                    pe.wait_ge(qk_ready, n - 1)
                    if causal:
                        pe.wait_ge(v_ready, n - 1)
                for c in range(CH):
                    pe.matmul(pQ[n % 2], proj_in[:, c, i * P:(i + 1) * P], W[:, c, 0:2 * C], start=(c == 0), stop=(c == CH - 1))
                for c in range(CH):
                    last = pe.matmul(pV[n % 2], proj_in[:, c, i * P:(i + 1) * P], W[:, c, 2 * C:3 * C],
                                     start=(c == 0), stop=(c == CH - 1))
                last.then_inc(qkv_done, 1)

            def transpose_parts(b, i):
                n = NT * b + i
                pe.wait_ge(lo_ready, n + 1)
                if n:
                    pe.wait_ge(partsT_ready, n)
                for k in range(12):
                    a, f = divmod(k, 4)
                    last = pe.transpose(pP[k // 6][:, k % 6, :], parts[:, n % 2, a, f * P:(f + 1) * P], IDB[:, :])
                last.then_inc(pt_done, 1)

            def score_max(b, g, u):
                j, i, k0, w = UNITS[u]
                n = NU * (NG * b + g) + u
                if u == 0:
                    pe.wait_ge(stk_loaded[g % 2], 16 * N_LOAD * ((NG // 2) * b + g // 2 + 1))
                if n >= 2:
                    pe.wait_ge(mx_taken, n - 1)
                if causal:
                    for k in range(k0, k0 + w, QC):
                        m = min(QC, k0 + w - k)
                        diagonal = k + m == P * (i + 1)
                        o = pM[n % 2][:, k - k0:k - k0 + m]
                        last = pe.matmul(o, stk[0:KR, g % 2, 0, j, i * P:(i + 1) * P], stk[0:KR, g % 2, 1, j, k:k + m],
                                         start=True, stop=not diagonal)
                        if diagonal:
                            last = pe.matmul(o[:, m - P:m], IDB[:, :], MQK[:, :], start=False, stop=True)
                else:
                    for j in range(HG):
                        o = pM[n % 2][:, j * P:(j + 1) * P]
                        pe.matmul(o, stk[0:KR, g % 2, 0, j, i * P:(i + 1) * P], stk[0:KR, g % 2, 1, j, i * P:(i + 1) * P],
                                  start=True, stop=False)
                        last = pe.matmul(o, IDB[:, :], MQK[:, :], start=False, stop=True)
                last.then_inc(mx_scored, 1)

            def maxima(b, g):
                pe.wait_ge(nm_ready, NG * b + g + 1)
                pe.transpose(pX.bitcast(BF16)[0:HG * NT, 0:P], nmb[:, :], IDB[:, :]).then_inc(x_done, 1)

            def score(b, g, s):
                c, kt, off = STEPS[s]
                if s == 0:
                    pe.wait_ge(m_loaded, 16 * (NG * b + g + 1))
                for e in range(E):
                    n = E * (NS * (NG * b + g) + s) + e
                    if n >= 2:
                        pe.wait_ge(e_done, n - 1)
                    if causal:
                        last = pe.matmul(pS[n % 2][:, off:QC], stk[0:KR + 1, g % 2, 1, e, kt * P:(kt + 1) * P],
                                         stk[0:KR + 1, g % 2, 0, e, c * QC + off:(c + 1) * QC],
                                         start=True, stop=kt < TC * c)
                        if kt >= TC * c:
                            last = pe.matmul(pS[n % 2][:, off:off + P], IDB[:, :], MKQ[:, :], start=False, stop=True)
                    else:
                        for j in range(HG):
                            o = pS[n % 2][:, j * P:(j + 1) * P]
                            pe.matmul(o, stk[0:KR + 1, g % 2, 1, j, kt * P:(kt + 1) * P],
                                      stk[0:KR + 1, g % 2, 0, j, kt * P:(kt + 1) * P], start=True, stop=False)
                            last = pe.matmul(o, IDB[:, :], MKQ[:, :], start=False, stop=True)
                    last.then_inc(s_done, 1)

            def weigh(b, g, s):
                c, kt, off = STEPS[s]
                n = NS * (NG * b + g) + s
                pe.wait_ge(e_done, E * (n + 1))
                if s == 0 or STEPS[s - 1][0] != c:
                    pe.wait_ge(ot_ready, NC * (NG * b + g) + c)
                for j in range(HG):
                    if causal:
                        pr = PR[:, (E * n + j) % NP, off:QC]
                        o = pO[HD * j:HD * j + VW, off:QC]
                        first, end = kt == 0, s == LAST[c]
                    else:
                        pr = PR[:, n % NP, j * P:(j + 1) * P]
                        o = pO[HD * j:HD * j + VW, off:off + P]
                        first, end = True, True
                    last = pe.matmul(o, V[:, kt, HG * g + j, :], pr, start=first, stop=end)
                last.then_inc(pv_done, 1)

            def transpose_results(b, g, c):
                n = NC * (NG * b + g) + c
                pe.wait_ge(ot_ready, n + 1)
                if c:
                    pe.wait_ge(y_ready, n)
                else:
                    pe.wait_ge(nmr_ready, NG * b + g + 1)
                for i in range(TC):
                    last = pe.transpose(pX[:, i * P:(i + 1) * P], OT[:, n % 2, i * P:(i + 1) * P], IDF[:, :])
                last.then_inc(x_done, 1)

            pe.wait_ge(consts, N_CONST)
            pe.wait_ge(zeroed, 2)
            for b in range(B):
                if b:
                    pe.wait_ge(y_ready, NC * NG * b)
                    pe.wait_ge(mx_taken, NU * NG * b)
                for s in range(NT + LP):
                    if s < NT:
                        transpose_rows(b, s)
                    if 0 <= s - LQ < NT:
                        project(b, s - LQ)
                    if 0 <= s - LP < NT:
                        transpose_parts(b, s - LP)
                pe.wait_ge(partsT_ready, NT * (b + 1))
                pe.matmul(pO, ZB[:, :], partsT[:, 0, 0, 0, 0:QC], start=True, stop=True)
                for u in range(NU):
                    score_max(b, 0, u)
                maxima(b, 0)
                pe.wait_ge(zeroed, 2 + (3 * (b + 1) if causal else 2))
                for g in range(NG):
                    for s in range(NS + PVLAG + 1):
                        if s < NS:
                            score(b, g, s)
                        if 0 <= s - PVLAG < NS:
                            weigh(b, g, s - PVLAG)
                        for c in range(NC):
                            if s == LAST[c] + PVLAG + 1:
                                transpose_results(b, g, c)
                        if g + 1 < NG:
                            for u in due(s):
                                score_max(b, g + 1, u)
                    if g + 1 < NG:
                        pe.wait_ge(y_ready, NC * (NG * b + g + 1))
                        maxima(b, g + 1)


def router_phase(nc, PS, mem, yB, y0d, x1d, projw, rw, ln2w, ln2b, identf, xs_dram):
    ctx = ExitStack()
    with ctx:
        ph = Phase(nc, ctx, "C")
        sb, sem = ph.sb, ph.sem
        N = B * NT
        RES, H2, LG = mem.RES, mem.H2, mem.LG
        PW = sb("PW", [P, CH, C], FP32)
        RW = sb("RW", [P, CH, E4], FP32)
        LNW = sb("LNW", [P, C], FP32)
        LNB = sb("LNB", [P, C], FP32)
        zeros = sb("zeros", [P, C], FP32)
        yt = sb("yt", [P, 2, C], FP32)
        y0t = sb("y0t", [P, 2, C], FP32)
        x1t = sb("x1t", [P, 2, C], FP32)
        yT = sb("yT", [P, 2, CH, P], FP32)
        hh = sb("hh", [P, 2, C], FP32)
        hw = sb("hw", [P, C], FP32)
        st = sb("st", [P, 6], FP32)
        mv = sb("mv", [P, N, 2], FP32)
        ve = sb("ve", [P, N], FP32)
        sd = sb("sd", [P, N], FP32)
        rs = sb("rs", [P, N], FP32)
        pT = [PS[:, i, 0:C].rearrange("p (c t) -> p c t", c=CH) for i in (0, 1)]
        pP = [PS[:, i, 0:C] for i in (2, 3)]
        pL = [PS[:, i, 0:E4] for i in (4, 5)]
        consts = sem("consts")
        zeroed = sem("zeroed")
        y_loaded = [sem(f"y_loaded{i}") for i in range(2)]
        y0_loaded = [sem(f"y0_loaded{i}") for i in range(2)]
        x1_loaded = [sem(f"x1_loaded{i}") for i in range(2)]
        t_done = sem("t_done")
        T_ready = sem("T_ready")
        p_done = sem("p_done")
        dch = sem("dch")
        y1_ready = sem("y1_ready")
        sd_ready = sem("sd_ready")
        var_ready = sem("var_ready")
        h_ready = sem("h_ready")
        kept = sem("kept")
        l_done = sem("l_done")
        l_ready = sem("l_ready")
        res_ready = sem("res_ready")
        block = ctx.enter_context(nc.Block())

        @block.sync
        def _(sp):
            sp.dma_start(mem.IDF[:, :], identf).then_inc(consts, 16)
            sp.dma_start(PW[:, :, :], projw).then_inc(consts, 16)
            sp.dma_start(RW[:, :, :], rw).then_inc(consts, 16)
            sp.dma_start(LNW[:, :], ln2w).then_inc(consts, 16)
            sp.dma_start(LNB[:, :], ln2b).then_inc(consts, 16)
            for n in range(N):
                if n >= 2:
                    sp.wait_ge(t_done, n - 1)
                sp.dma_start(yt[:, n % 2, :], yB[n]).then_inc(y_loaded[n % 2], 16)
                if n >= 2:
                    sp.wait_ge(y1_ready, n - 1)
                sp.dma_start(y0t[:, n % 2, :], y0d[n]).then_inc(y0_loaded[n % 2], 16)
            for n in range(N):
                if n >= 2:
                    sp.wait_ge(res_ready, n - 1)
                sp.dma_start(x1t[:, n % 2, :], x1d[n]).then_inc(x1_loaded[n % 2], 16)

        @block.gpsimd
        def _(pool):
            pool.memset(zeros[:, :], 0.0).then_inc(zeroed, 1)
            pool.wait_ge(zeroed, 1)
            pool.dma_start(xs_dram, zeros[:, :].unsqueeze(1).broadcast_to([P, NE, C])).then_inc(mem.xs_zeroed, 16)
            for n in range(N):
                pool.wait_ge(h_ready, n + 1)
                pool.tensor_copy(H2[:, n, :], hh[:, n % 2, :]).then_inc(kept, 1)
                pool.wait_ge(x1_loaded[n % 2], 16 * (n // 2 + 1))
                pool.tensor_tensor(RES[:, n, :], RES[:, n, :], x1t[:, n % 2, :], ALU.add).then_inc(res_ready, 1)

        @block.scalar
        def _(act):
            for dst, s in mem.loads:
                act.dma_start(dst, s).then_inc(mem.loaded, 16)
            for n in range(2 * N):
                if n == N:
                    act.wait_ge(var_ready, 1)
                    act.activation(sd[:, :], ve[:, :], ACT.Sqrt).then_inc(sd_ready, 1)
                act.wait_ge(t_done, n + 1)
                if n >= 2:
                    if n - 2 < N:
                        act.wait_ge(p_done, n - 1)
                    else:
                        act.wait_ge(l_done, n - 2 - N + 1)
                act.activation(yT[:, n % 2, :, :], pT[n % 2], ACT.Copy).then_inc(T_ready, 1)

        @block.vector
        def _(dve):
            chain = [0]

            def link(ins):
                chain[0] += 1
                ins.then_inc(dch, 1)
                dve.wait_ge(dch, chain[0])

            dve.wait_ge(consts, 80)
            for n in range(N):
                dve.wait_ge(p_done, n + 1)
                dve.wait_ge(y0_loaded[n % 2], 16 * (n // 2 + 1))
                dve.tensor_tensor(RES[:, n, :], pP[n % 2], y0t[:, n % 2, :], ALU.add).then_inc(y1_ready, 1)
                dve.wait_ge(y1_ready, n + 1)
                link(dve.bn_stats(st[:, :], RES[:, n, :]))
                link(dve.bn_aggr(mv[:, n, :], st[:, :]))
            dve.tensor_scalar(ve[:, :], mv[:, :, 1], EPS, None, ALU.add).then_inc(var_ready, 1)
            dve.wait_ge(sd_ready, 1)
            link(dve.reciprocal(rs[:, :], sd[:, :]))

            def logits_out(n):
                dve.wait_ge(l_done, n + 1)
                dve.tensor_copy(LG[:, n, :], pL[n % 2]).then_inc(l_ready, 1)

            for n in range(N):
                if n >= 2:
                    dve.wait_ge(t_done, N + n - 1)
                    dve.wait_ge(kept, n - 1)
                link(dve.tensor_scalar(hh[:, n % 2, :], RES[:, n, :], mv[:, n, 0:1], rs[:, n:n + 1], ALU.subtract, ALU.mult))
                link(dve.tensor_tensor(hw[:, :], hh[:, n % 2, :], LNW[:, :], ALU.mult))
                dve.tensor_tensor(hh[:, n % 2, :], hw[:, :], LNB[:, :], ALU.add).then_inc(h_ready, 1)
                dve.wait_ge(h_ready, n + 1)
                if n:
                    logits_out(n - 1)
            logits_out(N - 1)

        @block.tensor
        def _(pe):
            def transposes(n):
                m = n % N
                src = yt if n < N else hh
                if n < N:
                    pe.wait_ge(y_loaded[n % 2], 16 * (n // 2 + 1))
                else:
                    pe.wait_ge(h_ready, m + 1)
                if n >= 2:
                    pe.wait_ge(T_ready, n - 1)
                for c in range(CH):
                    last = pe.transpose(pT[n % 2][:, c, :], src[:, n % 2, c * P:(c + 1) * P], mem.IDF[:, :])
                last.then_inc(t_done, 1)

            def project(n):
                pe.wait_ge(T_ready, n + 1)
                if n >= 2:
                    pe.wait_ge(y1_ready, n - 1)
                for c in range(CH):
                    last = pe.matmul(pP[n % 2], yT[:, n % 2, c, :], PW[:, c, :], start=(c == 0), stop=(c == CH - 1))
                last.then_inc(p_done, 1)

            def route(n):
                pe.wait_ge(T_ready, N + n + 1)
                if n >= 2:
                    pe.wait_ge(l_ready, n - 1)
                for c in range(CH):
                    last = pe.matmul(pL[n % 2], yT[:, n % 2, c, :], RW[:, c, :], start=(c == 0), stop=(c == CH - 1))
                last.then_inc(l_done, 1)

            pe.wait_ge(consts, 80)
            transposes(0)
            for n in range(1, N + 1):
                if n < N:
                    transposes(n)
                project(n - 1)
            transposes(N)
            for n in range(1, N + 1):
                if n < N:
                    transposes(N + n)
                route(n - 1)


def expert_phase(nc, PS, mem, xs_dram, xs_tiles, ys_tiles, ys_dram, out):
    ctx = ExitStack()
    with ctx:
        ph = Phase(nc, ctx, "D")
        sb, sem = ph.sb, ph.sem
        N = B * NT
        RES, H2, LG, WV, WP = mem.RES, mem.H2, mem.LG, mem.WV, mem.WP
        mxl = sb("mxl", [P, N], FP32)
        ge = sb("ge", [P, N, E4], FP32)
        oh = sb("oh", [P, E4, N], FP32)
        ohT = oh[:, :, :].rearrange("p e n -> p n e")
        oh2 = oh[:, :, :].rearrange("p e n -> p (e n)")
        inc_ = sb("inc_", [P, E4, N], FP32)
        tot = sb("tot", [P, E4, N], FP32)
        inc2 = inc_[:, :, :].rearrange("p e n -> p (e n)")
        tot2 = tot[:, :, :].rearrange("p e n -> p (e n)")
        ni = sb("ni", [P, E4], mybir.dt.int32)
        nf = sb("nf", [P, E4], FP32)
        ts = sb("ts", [P, E4], FP32)
        base = sb("base", [P, E4], FP32)
        slotf = sb("slotf", [P, N], FP32)
        slot = sb("slot", [P, N], mybir.dt.uint32)
        cmp_ = sb("cmp_", [1, NE, E4 - 1], FP32)
        eidf = sb("eidf", [1, NE], FP32)
        eid = sb("eid", [1, NE], mybir.dt.int32)
        xs = sb("xs", [P, 2, C], FP32)
        xT = sb("xT", [P, 2, CH, P], FP32)
        sg = sb("sg", [P, F], FP32)
        u = sb("u", [P, F], FP32)
        uT = sb("uT", [P, 2, F // P, P], FP32)
        yo = sb("yo", [P, 2, C], FP32)
        NGB = 4
        gt = sb("gt", [P, NGB, C], FP32)
        pG = PS[:, 0:4, :].rearrange("p a b -> p (a b)")
        pU = PS[:, 4:6, :].rearrange("p a (b t) -> p (a b) t", t=P)
        pX = PS[:, 6, 0:C].rearrange("p (c t) -> p c t", c=CH)
        pD = PS[:, 7, 0:C]
        pA = PS[:, 0, 0:E4 * N]
        pB = PS[:, 1, 0:E4 * N]
        dch = sem("dch")
        oh_ready = sem("oh_ready")
        cnt_done = sem("cnt_done")
        slot_ready = sem("slot_ready")
        eid_ready = sem("eid_ready")
        scattered = sem("scattered")
        xs_loaded = [sem(f"xs_loaded{i}") for i in range(2)]
        x_tr = sem("x_tr")
        xt_ready = sem("xt_ready")
        gate_done = sem("gate_done")
        g_done = sem("g_done")
        silu_done = sem("silu_done")
        u_ready = sem("u_ready")
        ut_done = sem("ut_done")
        ut_ready = sem("ut_ready")
        d_done = sem("d_done")
        yo_ready = sem("yo_ready")
        ys_stored = [sem(f"ys_stored{i}") for i in range(2)]
        gathered = [sem(f"gathered{i}") for i in range(NGB)]
        o_ready = sem("o_ready")
        o_stored = [sem(f"o_stored{i}") for i in range(NGB)]
        block = ctx.enter_context(nc.Block())

        @block.sync
        def _(sp):
            sp.wait_ge(scattered, 16 * N)
            for j in range(NE):
                if j >= 2:
                    sp.wait_ge(x_tr, j - 1)
                sp.dma_start(xs[:, j % 2, :], xs_tiles[j]).then_inc(xs_loaded[j % 2], 16)
            for n in range(N):
                sp.wait_ge(o_ready, n + 1)
                sp.dma_start(out[n], gt[:, n % NGB, :]).then_inc(o_stored[n % NGB], 16)
            for i in range(NGB):
                sp.wait_ge(o_stored[i], 16 * (N // NGB))

        @block.gpsimd
        def _(pool):
            pool.wait_ge(slot_ready, 1)
            pool.wait_ge(mem.xs_zeroed, 16)
            for n in range(N):
                pool.indirect_dma_start(xs_dram, bass.IndirectOffsetOnAxis(ap=slot[:, n:n + 1], axis=0),
                                        H2[:, n, :], None).then_inc(scattered, 16)
            for j in range(NE):
                pool.wait_ge(yo_ready, j + 1)
                pool.dma_start(ys_tiles[j], yo[:, j % 2, :]).then_inc(ys_stored[j % 2], 16)
            for i in range(2):
                pool.wait_ge(ys_stored[i], 16 * ((NE - i + 1) // 2))
            for n in range(N):
                if n >= NGB:
                    pool.wait_ge(o_stored[n % NGB], 16 * (n // NGB))
                pool.indirect_dma_start(gt[:, n % NGB, :], None, ys_dram,
                                        bass.IndirectOffsetOnAxis(ap=slot[:, n:n + 1], axis=0)).then_inc(gathered[n % NGB], 16)

        @block.scalar
        def _(act):
            for j in range(NE):
                act.wait_ge(gate_done, j + 1)
                if j:
                    act.wait_ge(u_ready, j)
                act.activation(sg[:, :], pG[:, 0:F], ACT.Silu).then_inc(silu_done, 1)
                act.wait_ge(ut_done, j + 1)
                if j >= 2:
                    act.wait_ge(d_done, j - 1)
                act.activation(uT[:, j % 2, :, :], pU, ACT.Copy).then_inc(ut_ready, 1)

        @block.vector
        def _(dve):
            chain = [0]

            def link(ins):
                chain[0] += 1
                ins.then_inc(dch, 1)
                dve.wait_ge(dch, chain[0])

            dve.wait_ge(mem.loaded, 16 * mem.n_loads)
            link(dve.reduce_max(mxl[:, :], LG[:, :, :], AX.X))
            link(dve.tensor_tensor(ge[:, :, :], LG[:, :, :], mxl[:, :].unsqueeze(2).broadcast_to([P, N, E4]), ALU.is_ge))
            link(dve.tensor_tensor(ge[:, :, :], ge[:, :, :], mem.RANK[:, :].unsqueeze(1).broadcast_to([P, N, E4]), ALU.mult))
            link(dve.reduce_max(mxl[:, :], ge[:, :, :], AX.X))
            dve.tensor_tensor(ohT, ge[:, :, :], mxl[:, :].unsqueeze(2).broadcast_to([P, N, E4]), ALU.is_equal).then_inc(oh_ready, 1)
            dve.wait_ge(cnt_done, 1)
            link(dve.tensor_copy(tot2, pB))
            link(dve.tensor_tensor_scan(inc2, mem.RESET[:, :], tot2, 0.0, ALU.mult, ALU.add))
            link(dve.tensor_scalar(nf[:, :], inc_[:, :, N - 1], float(P - 1), None, ALU.add))
            link(dve.tensor_copy(ni[:, :], nf[:, :]))
            link(dve.tensor_scalar(ni[:, :], ni[:, :], 7, None, ALU.logical_shift_right))
            link(dve.tensor_copy(nf[:, :], ni[:, :]))
            link(dve.tensor_tensor_scan(ts[:, :], mem.ONE[:, 0:E4], nf[:, :], 0.0, ALU.mult, ALU.add))
            link(dve.tensor_tensor(ts[:, :], ts[:, :], nf[:, :], ALU.subtract))
            link(dve.tensor_scalar(base[:, :], ts[:, :], float(P), None, ALU.mult))
            link(dve.tensor_tensor(inc2, inc2, tot2, ALU.subtract))
            link(dve.tensor_tensor(inc2, inc2, pA, ALU.add))
            link(dve.tensor_tensor(inc_[:, :, :], inc_[:, :, :], base[:, :].unsqueeze(2).broadcast_to([P, E4, N]), ALU.add))
            link(dve.tensor_tensor(inc2, inc2, oh2, ALU.mult))
            link(dve.reduce_sum(slotf[:, :], inc_[:, :, :].rearrange("p e n -> p n e"), AX.X))
            dve.tensor_copy(slot[:, :], slotf[:, :]).then_inc(slot_ready, 1)
            link(dve.tensor_tensor(cmp_[:, :, :], mem.TILE[:, :].unsqueeze(2).broadcast_to([1, NE, E4 - 1]),
                                   ts[0:1, 1:E4].unsqueeze(1).broadcast_to([1, NE, E4 - 1]), ALU.is_ge))
            link(dve.reduce_sum(eidf[:, :], cmp_[:, :, :], AX.X))
            dve.tensor_copy(eid[:, :], eidf[:, :]).then_inc(eid_ready, 1)

            def xT_out(j):
                dve.wait_ge(x_tr, j + 1)
                if j >= 2:
                    dve.wait_ge(g_done, j - 1)
                dve.tensor_copy(xT[:, j % 2, :, :], pX).then_inc(xt_ready, 1)

            def y_out(j):
                dve.wait_ge(d_done, j + 1)
                if j >= 2:
                    dve.wait_ge(ys_stored[j % 2], 16 * (j // 2))
                dve.tensor_copy(yo[:, j % 2, :], pD).then_inc(yo_ready, 1)

            xT_out(0)
            for j in range(NE):
                dve.wait_ge(silu_done, j + 1)
                dve.wait_ge(g_done, j + 1)
                if j:
                    dve.wait_ge(ut_done, j)
                dve.tensor_tensor(u[:, :], sg[:, :], pG[:, F:2 * F], ALU.mult).then_inc(u_ready, 1)
                if j + 1 < NE:
                    xT_out(j + 1)
                if j:
                    y_out(j - 1)
            y_out(NE - 1)
            for n in range(N):
                dve.wait_ge(gathered[n % NGB], 16 * (n // NGB + 1))
                dve.tensor_tensor(gt[:, n % NGB, :], gt[:, n % NGB, :], RES[:, n, :], ALU.add).then_inc(o_ready, 1)

        @block.tensor
        def _(pe):
            pe.wait_ge(mem.loaded, 16 * mem.n_loads)
            pe.wait_ge(oh_ready, 1)
            pe.matmul(pA, mem.LOWER[:, :], oh2, start=True, stop=True)
            pe.matmul(pB, mem.ONE[:, :], oh2, start=True, stop=True).then_inc(cnt_done, 1)

            def rows_in(j):
                pe.wait_ge(xs_loaded[j % 2], 16 * (j // 2 + 1))
                if j:
                    pe.wait_ge(xt_ready, j)
                for c in range(CH):
                    last = pe.transpose(pX[:, c, :], xs[:, j % 2, c * P:(c + 1) * P], mem.IDF[:, :])
                last.then_inc(x_tr, 1)

            def up(j, e):
                pe.wait_ge(xt_ready, j + 1)
                for k in range(2 * F // QC):
                    if j and k == 0:
                        pe.wait_ge(silu_done, j)
                    if j and k == F // QC:
                        pe.wait_ge(u_ready, j)
                    for c in range(CH):
                        last = pe.matmul(pG[:, k * QC:(k + 1) * QC], xT[:, j % 2, c, :],
                                         WV[:, bass.ds(e * (CH * 2 * F) + c * 2 * F + k * QC, QC)],
                                         start=(c == 0), stop=(c == CH - 1))
                    if k == F // QC - 1:
                        last.then_inc(gate_done, 1)
                last.then_inc(g_done, 1)

            def hidden(j):
                pe.wait_ge(u_ready, j + 1)
                if j:
                    pe.wait_ge(ut_ready, j)
                for f in range(F // P):
                    last = pe.transpose(pU[:, f, :], u[:, f * P:(f + 1) * P], mem.IDF[:, :])
                last.then_inc(ut_done, 1)

            def down(j, e):
                pe.wait_ge(ut_ready, j + 1)
                if j:
                    pe.wait_ge(yo_ready, j)
                for f in range(F // P):
                    last = pe.matmul(pD, uT[:, j % 2, f, :], WP[:, bass.ds(e * (F // P * C) + f * C, C)],
                                     start=(f == 0), stop=(f == F // P - 1))
                last.then_inc(d_done, 1)

            pe.wait_ge(eid_ready, 1)
            rows_in(0)
            before = None
            for j in range(NE):
                e = pe.value_load(eid[0:1, j:j + 1], min_val=0, max_val=E4 - 1)
                up(j, e)
                if j + 1 < NE:
                    rows_in(j + 1)
                if j:
                    down(j - 1, before)
                hidden(j)
                before = e
            down(NE - 1, before)


class Memory:
    pass


def expert_layer(nc, PS, yB, y0d, x1d, projw, rw, ln2w, ln2b, wv, wp, rank, reset, lower, tiles, one, identf, xs_rows, ys_rows, out):
    ctx = ExitStack()
    with ctx:
        ph = Phase(nc, ctx, "M")
        mem = Memory()
        N = B * NT
        mem.RES = ph.sb("RES", [P, N, C], FP32)
        mem.H2 = ph.sb("H2", [P, N, C], FP32)
        mem.LG = ph.sb("LG", [P, N, E4], FP32)
        mem.WV = ph.sb("WV", [P, E4 * CH * 2 * F], FP32)
        mem.WP = ph.sb("WP", [P, E4 * F * C // P], FP32)
        mem.IDF = ph.sb("IDF", [P, P], FP32)
        mem.RANK = ph.sb("RANK", [P, E4], FP32)
        mem.RESET = ph.sb("RESET", [P, E4 * N], FP32)
        mem.LOWER = ph.sb("LOWER", [P, P], FP32)
        mem.ONE = ph.sb("ONE", [P, P], FP32)
        mem.TILE = ph.sb("TILE", [1, NE], FP32)
        mem.loaded = ph.sem("loaded")
        mem.xs_zeroed = ph.sem("xs_zeroed")
        loads = [(mem.RANK[:, :], rank), (mem.RESET[:, :], reset), (mem.LOWER[:, :], lower),
                 (mem.ONE[:, :], one), (mem.TILE[:, :], tiles)]
        step = CH * 2 * F
        loads += [(mem.WV[:, e * step:(e + 1) * step].rearrange("p (c n) -> p c n", c=CH), wv[e]) for e in range(E4)]
        step = F * C // P
        loads += [(mem.WP[:, e * step:(e + 1) * step].rearrange("p (f n) -> p f n", n=C), wp[e]) for e in range(E4)]
        mem.n_loads = len(loads)
        mem.loads = loads

        def tiled(t):
            return t.rearrange("(n p) c -> n p c", p=P)

        xs_view = xs_rows.rearrange("(n p) c -> p n c", p=P)
        router_phase(nc, PS, mem, tiled(yB), tiled(y0d), tiled(x1d), projw, rw, ln2w, ln2b, identf, xs_view)
        expert_phase(nc, PS, mem, xs_rows, tiled(xs_rows), tiled(ys_rows), ys_rows, tiled(out))


def build(nc, x, wA, bA, ln1w, ln1b, cw, wB, ropec, ropes, mqk, mkq, bqk, identf, identb, projw, rw, ln2w, ln2b, wv, wp, rank, reset, lower, tiles, one, mA, mB, att, x1d, y0d, yB, xs, ys, out):
    with ExitStack() as ctx:
        PS = ctx.enter_context(nc.psum_tensor("PS", [P, 8, QC], FP32))

        def batch(t):
            r = t.rearrange("(b i p) c -> b p i c", b=B, p=P)
            return lambda b: r[b]

        attv = att.rearrange("r c -> (r c)").rearrange("(b h t d) -> b t h d", b=B, h=H, d=D)
        rowsv = yB.rearrange("(b i p) c -> b i p c", b=B, p=P)
        attention_phase(nc, PS, False, batch(x), None, wA, bA, None, None, None, None, None, bqk, bqk, identf, identb, mA,
                        lambda b, i: attv[b, i * P:(i + 1) * P], None, None)
        attention_phase(nc, PS, True, batch(x), batch(att), wB, None, ln1w, ln1b, cw, ropec, ropes, mqk, mkq, identf, identb, mB,
                        lambda b, i: rowsv[b, i], batch(x1d), batch(y0d))
        expert_layer(nc, PS, yB, y0d, x1d, projw, rw, ln2w, ln2b, wv, wp, rank, reset, lower, tiles, one, identf, xs, ys, out)


def kernel(**inputs):
    import ml_dtypes
    import numpy as np
    import concourse.bacc as bacc
    from concourse.bass_utils import run_bass_kernel_spmd as run

    def lay(name):
        return np.ascontiguousarray(inputs[name])

    def halves(w):
        return np.ascontiguousarray(w.reshape(CH, P, -1).transpose(1, 0, 2))

    def col(v):
        return np.ascontiguousarray(v.reshape(CH, P).T)

    inv = (1.0 / (10000.0 ** (np.arange(0, D, 2, dtype=np.float32) / np.float32(D)))).astype(np.float32)
    ang = (np.arange(T, dtype=np.float32)[:, None] * inv[None]).astype(np.float32)
    cos = np.concatenate([np.cos(ang)] * 2, -1).astype(np.float32)
    sin = np.concatenate([-np.sin(ang), np.sin(ang)], -1).astype(np.float32)

    def table(t):
        t = np.stack([t * np.float32(D ** -0.5), t], 1)
        return np.ascontiguousarray(t.reshape(NT, P, 2, D).transpose(1, 0, 2, 3).astype(np.float32))

    neg = np.float32(-1e30)
    r = np.arange(P)
    qk_mask = np.where(r[None] <= r[:, None], np.float32(0), neg)
    block_mask = np.where(r[None] // 32 == r[:, None] // 32, np.float32(0), neg)
    bf = ml_dtypes.bfloat16
    wq = lay("L0_attn_w_qkv")
    arrays = {
        "x": lay("L0_attn_hidden_states").reshape(B * T, C),
        "wA": halves(np.ascontiguousarray(wq.T)),
        "bA": np.ascontiguousarray(np.broadcast_to(lay("L0_attn_b_qkv")[None], (P, 3 * C))),
        "ln1w": col(lay("L0_ffn_ln1_w")), "ln1b": col(lay("L0_ffn_ln1_b")),
        "cw": halves(lay("L0_ffn_conv_w").reshape(C, 3)),
        "wB": halves(lay("L0_ffn_attn_w")),
        "ropec": table(cos), "ropes": table(sin),
        "mqk": qk_mask.astype(bf), "mkq": np.ascontiguousarray(qk_mask.T).astype(bf), "bqk": block_mask.astype(bf),
        "identf": np.eye(P, dtype=np.float32), "identb": np.eye(P, dtype=np.float32).astype(bf),
    }
    N = B * NT
    arrays.update({
        "projw": halves(lay("L0_ffn_proj_w")), "rw": halves(lay("L0_ffn_router_w")),
        "ln2w": np.ascontiguousarray(np.broadcast_to(lay("L0_ffn_ln2_w")[None], (P, C))),
        "ln2b": np.ascontiguousarray(np.broadcast_to(lay("L0_ffn_ln2_b")[None], (P, C))),
        "wv": np.ascontiguousarray(lay("L0_ffn_expert_wv").reshape(E4, CH, P, 2 * F).transpose(0, 2, 1, 3)),
        "wp": np.ascontiguousarray(lay("L0_ffn_expert_proj").reshape(E4, F // P, P, C).transpose(0, 2, 1, 3)),
        "rank": np.ascontiguousarray(np.broadcast_to(np.arange(E4, 0, -1, dtype=np.float32)[None], (P, E4))),
        "reset": np.ascontiguousarray(np.broadcast_to((np.arange(E4 * N) % N != 0).astype(np.float32)[None], (P, E4 * N))),
        "lower": (r[:, None] < r[None]).astype(np.float32),
        "tiles": np.arange(NE, dtype=np.float32)[None],
        "one": np.ones((P, P), np.float32),
    })
    nc = bacc.Bacc("TRN2", target_bir_lowering=False, num_devices=1)
    args = [nc.dram_tensor(k + "_dram", a.shape, mybir.dt.from_np(a.dtype), kind="ExternalInput").ap() for k, a in arrays.items()]
    for k in ("mA", "mB"):
        args.append(nc.dram_tensor(k + "_dram", (B * NG, HG * NT, P), BF16, kind="Internal").ap())
    for k, rows in (("att", B * T), ("x1d", B * T), ("y0d", B * T), ("yB", B * T), ("xs", NE * P), ("ys", NE * P)):
        args.append(nc.dram_tensor(k + "_dram", (rows, C), FP32, kind="Internal").ap())
    o = nc.dram_tensor("out_dram", (B * T, C), FP32, kind="ExternalOutput").ap()
    args.append(o)
    build(nc, *args)
    res = run(nc, [{k + "_dram": a for k, a in arrays.items()}], core_ids=[0])
    return res.results[0]["out_dram"].reshape(B, T, C)
```

```python
import concourse.bass as bass
from concourse import mybir
from contextlib import ExitStack

FP32 = mybir.dt.float32
BF16 = mybir.dt.bfloat16
ALU = mybir.AluOpType
ACT = mybir.ActivationFunctionType
AX = mybir.AxisListType

B = 2
T = 2048
C = 256
P = 128
NT = T // P
CH = C // P
H = 16
D = C // H
HG = 4
NG = H // HG
QC = 512
NC = T // QC
TC = QC // P
NTERM = 6
VW = D + 1
NP = 12
HD = 32
ONES2 = 1.0019378662109375
E4 = 4
F = 4 * C
NE = B * NT + E4 - 1
EPS = 1e-5
LEAD_A = 14
LEAD_B = 21
TERMS = [[0, 0, 1, 1, 0, 2], [0, 1, 0, 1, 2, 0]]
NMAX = 4
HALF_ROWS = NMAX * D
FIRST_ROW = [0, HALF_ROWS]
REST_ROW = [HALF_ROWS, 0]
M_ROW = [HALF_ROWS + (NTERM - NMAX) * D, (NTERM - NMAX) * D]
ROWS = [M_ROW[0] + 1, P]
N = B * NT



class Phase:

    def __init__(self, nc, ctx, tag):
        self.nc, self.ctx, self.tag = nc, ctx, tag

    def sb(self, name, shape, dt):
        return self.ctx.enter_context(self.nc.sbuf_tensor(name + self.tag, shape, dt))

    def sem(self, name):
        return self.ctx.enter_context(self.nc.semaphore(name + self.tag))


def project_phase(nc, PS, V, causal, src, add, w_dram, bias, ln_w, ln_b, conv_w, rope_c, rope_s, identf, identb,
                  pt, x_out, h_out):
    ctx = ExitStack()
    with ctx:
        ph = Phase(nc, ctx, "PB" if causal else "PA")
        sb, sem = ph.sb, ph.sem

        W = sb("W", [P, CH, 3 * C], FP32)
        X = sb("X", [P, N, C], FP32)
        hT = sb("hT", [P, CH, B, T + 2], FP32)
        hn = sb("hn", [P, 2, C], FP32)
        qk = sb("qk", [P, 2, 2 * C], FP32)
        r1 = sb("r1", [P, 2, 2 * C], FP32)
        parts = sb("parts", [P, 2, 3, 2 * C], BF16)
        PB = sb("PB", [P, 2, 12, QC], BF16)
        IDF = sb("IDF", [P, P], FP32)
        IDB = sb("IDB", [P, P], BF16)
        st = sb("st", [P, N, 6], FP32)
        mv = sb("mv", [P, N, 2], FP32)
        ve = sb("ve", [P, N], FP32)
        sd = sb("sd", [P, N], FP32)
        rs = sb("rs", [P, N], FP32)
        if causal:
            AD = sb("AD", [P, N, C], FP32)
            hc = sb("hc", [P, 2, CH, QC], FP32)
            ra = sb("ra", [P, 2, 2 * C], FP32)
            rb = sb("rb", [P, 2, 2 * C], FP32)
            RC = sb("RC", [P, NT, 2, D], FP32)
            RS = sb("RS", [P, NT, 2, D], FP32)
            LW = sb("LW", [P, CH], FP32)
            LB = sb("LB", [P, CH], FP32)
            CW = sb("CW", [P, CH, 3], FP32)
        else:
            BI = sb("BI", [P, 3 * C], FP32)
            BQ = sb("BQ", [P, C], FP32)
        pT = [PS[:, i, 0:CH * P].rearrange("p (c t) -> p c t", c=CH) for i in (0, 1)]
        pQ = [PS[:, i, :] for i in (2, 3)]
        pV = [PS[:, i, 0:C] for i in (4, 5)]
        pP = [PS[:, i, :].bitcast(BF16)[:, 0:6 * P].rearrange("p (n t) -> p n t", n=6) for i in (6, 7)]

        consts = sem("consts")
        rows = [sem(f"rows{b}") for b in range(B)]
        zeroed = sem("zeroed")
        dch = sem("dch")
        sum_ready = sem("sum_ready")
        var_ready = sem("var_ready")
        sd_ready = sem("sd_ready")
        y0_ready = sem("y0_ready")
        hn_ready = sem("hn_ready")
        tp_done = sem("tp_done")
        ht_ready = sem("ht_ready")
        hc_ready = sem("hc_ready")
        qkv_done = sem("qkv_done")
        v_ready = sem("v_ready")
        ro_ready = sem("ro_ready")
        qk_ready = sem("qk_ready")
        hi_ready = sem("hi_ready")
        r1_ready = sem("r1_ready")
        mid_ready = sem("mid_ready")
        lo_ready = sem("lo_ready")
        pt_done = sem("pt_done")
        pbd_ready = sem("pbd_ready")
        pba_ready = sem("pba_ready")
        pt_stored = [sem(f"pt_stored{i}") for i in range(2)]
        x_stored = sem("x_stored")

        LQ = 5 if causal else 1
        LP = LQ + 2
        N_CONST = 16 * (8 if causal else 4)

        block = ctx.enter_context(nc.Block())

        @block.sync
        def _(sp):
            for b in range(B):
                for c in range(NC):
                    t = slice(TC * c, TC * (c + 1))
                    sp.dma_start(X[:, NT * b + TC * c:NT * b + TC * (c + 1), :], src(b)[:, t, :]).then_inc(rows[b], 16)
                    if causal:
                        sp.dma_start(AD[:, NT * b + TC * c:NT * b + TC * (c + 1), :], add(b)[:, t, :]).then_inc(rows[b], 16)
            if causal:
                for b in range(B):
                    sp.wait_ge(sum_ready, b + 1)
                    sp.dma_start(x_out(b), X[:, NT * b:NT * (b + 1), :]).then_inc(x_stored, 16)
                sp.wait_ge(y0_ready, 1)
                for b in range(B):
                    sp.dma_start(h_out(b), AD[:, NT * b:NT * (b + 1), :]).then_inc(x_stored, 16)
            for k in range(N // TC):
                b, c = divmod(k, NC)
                sp.wait_ge(pbd_ready, TC * (k + 1))
                sp.wait_ge(pba_ready, TC * (k + 1))
                sp.dma_start(pt[b].rearrange("n p t -> p n t")[:, :, c * QC:(c + 1) * QC], PB[:, k % 2, :, :])\
                  .then_inc(pt_stored[k % 2], 16)
            for i in range(2):
                sp.wait_ge(pt_stored[i], 16 * (N // TC // 2))
            if causal:
                sp.wait_ge(x_stored, 32 * B)

        @block.gpsimd
        def _(pool):
            pool.memset(hT[:, :, :, 0:2], 0.0).then_inc(zeroed, 1)
            pool.memset(V[:, :, :, D:VW], 1.0).then_inc(zeroed, 1)
            pool.wait_ge(zeroed, 2)
            if causal:
                for b in range(B):
                    t = slice(NT * b, NT * (b + 1))
                    pool.wait_ge(rows[b], 16 * 2 * NC)
                    pool.tensor_tensor(X[:, t, :], X[:, t, :], AD[:, t, :], ALU.add).then_inc(sum_ready, 1)

            def total(n):
                pool.wait_ge(ro_ready, n + 1)
                if n >= 2:
                    pool.wait_ge(hi_ready, n - 1)
                    pool.wait_ge(r1_ready, n - 1)
                pool.tensor_tensor(qk[:, n % 2, :], ra[:, n % 2, :], rb[:, n % 2, :], ALU.add).then_inc(qk_ready, 1)

            if causal:
                total(0)
            for n in range(N):
                pool.wait_ge(hi_ready, n + 1)
                if n >= 2:
                    pool.wait_ge(mid_ready, n - 1)
                    pool.wait_ge(lo_ready, n - 1)
                pool.tensor_tensor(r1[:, n % 2, :], qk[:, n % 2, :], parts[:, n % 2, 0, :], ALU.subtract)\
                    .then_inc(r1_ready, 1)
                if causal and n + 1 < N:
                    total(n + 1)
                pool.wait_ge(mid_ready, n + 1)
                pool.tensor_tensor(parts[:, n % 2, 2, :], r1[:, n % 2, :], parts[:, n % 2, 1, :], ALU.subtract)\
                    .then_inc(lo_ready, 1)

        @block.scalar
        def _(act):
            act.dma_start(IDF[:, :], identf).then_inc(consts, 16)
            act.dma_start(IDB[:, :], identb).then_inc(consts, 16)
            act.dma_start(W[:, :, :], w_dram).then_inc(consts, 16)
            if causal:
                act.dma_start(RC[:, :, :, :], rope_c).then_inc(consts, 16)
                act.dma_start(RS[:, :, :, :], rope_s).then_inc(consts, 16)
                act.dma_start(LW[:, :], ln_w).then_inc(consts, 16)
                act.dma_start(LB[:, :], ln_b).then_inc(consts, 16)
                act.dma_start(CW[:, :, :], conv_w).then_inc(consts, 16)
            else:
                act.dma_start(BI[:, :], bias).then_inc(consts, 16)

            def evacuate(n):
                b, i = divmod(n, NT)
                act.wait_ge(tp_done, n + 1)
                t = slice(2 + i * P, 2 + (i + 1) * P)
                if causal:
                    for c in range(CH):
                        last = act.activation(hT[:, c, b, t], pT[n % 2][:, c, :], ACT.Identity,
                                              scale=LW[:, c:c + 1], bias=LB[:, c:c + 1])
                else:
                    last = act.activation(hT[:, :, b, t], pT[n % 2], ACT.Copy)
                last.then_inc(ht_ready, 1)

            def high(n):
                if causal:
                    act.wait_ge(qkv_done, n + 1)
                    act.activation(V[:, n, :, 0:D], pV[n % 2].rearrange("p (h d) -> p h d", h=H), ACT.Copy).then_inc(v_ready, 1)
                act.wait_ge(qk_ready, n + 1)
                if n >= 2:
                    act.wait_ge(pt_done, n - 1)
                act.activation(parts[:, n % 2, 0, :], qk[:, n % 2, :], ACT.Copy).then_inc(hi_ready, 1)

            def middle(n):
                act.wait_ge(r1_ready, n + 1)
                act.activation(parts[:, n % 2, 1, :], r1[:, n % 2, :], ACT.Copy).then_inc(mid_ready, 1)

            def parts_out(n):
                k, i = divmod(n, TC)
                act.wait_ge(pt_done, n + 1)
                if k >= 2:
                    act.wait_ge(pt_stored[k % 2], 16 * (k // 2))
                act.activation(PB[:, k % 2, 6:12, i * P:(i + 1) * P], pP[1], ACT.Copy).then_inc(pba_ready, 1)

            act.wait_ge(consts, N_CONST)
            for k in range(2 if causal else 1):
                act.wait_ge(var_ready, k + 1)
                act.activation(sd[:, :], ve[:, :], ACT.Sqrt).then_inc(sd_ready, 1)
            act.wait_ge(zeroed, 2)
            for s in range(N + LP + 1):
                if s < N:
                    evacuate(s)
                if 0 <= s - LQ < N:
                    high(s - LQ)
                if 0 <= s - LQ - 1 < N:
                    middle(s - LQ - 1)
                if 0 <= s - LP < N:
                    parts_out(s - LP)

        @block.vector
        def _(dve):
            chain = [0]

            def link(ins):
                chain[0] += 1
                ins.then_inc(dch, 1)
                dve.wait_ge(dch, chain[0])

            def statistics(rows_, k, arrival):
                for b in range(B):
                    arrival(b)
                    for i in range(NT * b, NT * (b + 1)):
                        last = dve.bn_stats(st[:, i, :], rows_[:, i, :])
                link(last)
                for i in range(N):
                    last = dve.bn_aggr(mv[:, i, :], st[:, i, :])
                link(last)
                dve.tensor_scalar(ve[:, :], mv[:, :, 1], EPS, None, ALU.add).then_inc(var_ready, 1)
                dve.wait_ge(sd_ready, k)
                link(dve.reciprocal(rs[:, :], sd[:, :]))

            def normalise(n):
                if n >= 2:
                    dve.wait_ge(tp_done, n - 1)
                dve.tensor_scalar(hn[:, n % 2, :], (AD if causal else X)[:, n, :], mv[:, n, 0:1], rs[:, n:n + 1],
                                  ALU.subtract, ALU.mult).then_inc(hn_ready, 1)

            def convolve(k):
                b, q = divmod(k, NC)
                dve.wait_ge(ht_ready, TC * (k + 1))
                if k >= 2:
                    dve.wait_ge(qkv_done, TC * (k - 1))
                for tap in range(3):
                    for c in range(CH):
                        dst = hc[:, k % 2, c, :]
                        past = hT[:, c, b, q * QC + tap:(q + 1) * QC + tap]
                        if tap == 0:
                            last = dve.tensor_scalar(dst, past, CW[:, c, 0:1], None, ALU.mult)
                        else:
                            last = dve.scalar_tensor_tensor(out=dst, in0=past, scalar=CW[:, c, tap:tap + 1], in1=dst,
                                                            op0=ALU.mult, op1=ALU.add)
                    if tap < 2:
                        link(last)
                last.then_inc(hc_ready, 1)

            def rotate(n):
                i = n % NT
                dve.wait_ge(qkv_done, n + 1)
                s = pQ[n % 2]
                if causal:
                    if n >= 2:
                        dve.wait_ge(qk_ready, n - 1)
                    s4 = s.rearrange("p (a h d) -> p a h d", a=2, h=H)
                    ra4 = ra[:, n % 2, :].rearrange("p (a h d) -> p a h d", a=2, h=H)
                    rb4 = rb[:, n % 2, :].rearrange("p (a h d) -> p a h d", a=2, h=H)
                    half = D // 2
                    for lo in (0, half):
                        hi = half - lo
                        dve.tensor_tensor(rb4[:, :, :, lo:lo + half], s4[:, :, :, hi:hi + half],
                                          RS[:, i, :, lo:lo + half].unsqueeze(2).broadcast_to([P, 2, H, half]), ALU.mult)
                    dve.tensor_tensor(ra4, s4, RC[:, i, :, :].unsqueeze(2).broadcast_to([P, 2, H, D]), ALU.mult)\
                       .then_inc(ro_ready, 1)
                else:
                    if n >= 2:
                        dve.wait_ge(r1_ready, n - 1)
                    dve.scalar_tensor_tensor(out=qk[:, n % 2, 0:C], in0=s[:, 0:C], scalar=D ** -0.5,
                                             in1=BQ[:, :], op0=ALU.mult, op1=ALU.add)
                    dve.tensor_tensor(qk[:, n % 2, C:2 * C], s[:, C:2 * C], BI[:, C:2 * C], ALU.add)
                    dve.tensor_tensor(V[:, n, :, 0:D], pV[n % 2].rearrange("p (h d) -> p h d", h=H),
                                      BI[:, 2 * C:3 * C].rearrange("p (h d) -> p h d", h=H), ALU.add).then_inc(qk_ready, 1)

            def parts_out(n):
                k, i = divmod(n, TC)
                dve.wait_ge(pt_done, n + 1)
                if k >= 2:
                    dve.wait_ge(pt_stored[k % 2], 16 * (k // 2))
                dve.tensor_copy(PB[:, k % 2, 0:6, i * P:(i + 1) * P], pP[0]).then_inc(pbd_ready, 1)

            dve.wait_ge(consts, N_CONST)
            dve.wait_ge(zeroed, 2)
            if not causal:
                link(dve.tensor_scalar(BQ[:, :], BI[:, 0:C], D ** -0.5, None, ALU.mult))
                statistics(X, 1, lambda b: dve.wait_ge(rows[b], 16 * NC))
            else:
                statistics(X, 1, lambda b: dve.wait_ge(sum_ready, b + 1))
                for n in range(N):
                    last = dve.tensor_scalar(AD[:, n, :], X[:, n, :], mv[:, n, 0:1], rs[:, n:n + 1],
                                             ALU.subtract, ALU.mult)
                last.then_inc(y0_ready, 1)
                dve.wait_ge(y0_ready, 1)
                statistics(AD, 2, lambda b: None)
            for s in range(N + LP):
                if s < N:
                    normalise(s)
                if causal and s % TC == 0 and 0 < s <= N:
                    convolve(s // TC - 1)
                if 0 <= s - LQ < N:
                    rotate(s - LQ)
                if 0 <= s - LP < N:
                    parts_out(s - LP)

        @block.tensor
        def _(pe):
            def transpose_rows(n):
                pe.wait_ge(hn_ready, n + 1)
                if n >= 2:
                    pe.wait_ge(ht_ready, n - 1)
                for c in range(CH):
                    last = pe.transpose(pT[n % 2][:, c, :], hn[:, n % 2, c * P:(c + 1) * P], IDF[:, :])
                last.then_inc(tp_done, 1)

            def project(n):
                k, i = divmod(n, TC)
                if causal:
                    pe.wait_ge(hc_ready, k + 1)
                else:
                    pe.wait_ge(ht_ready, n + 1)
                if n >= 2:
                    pe.wait_ge(ro_ready if causal else qk_ready, n - 1)
                    if causal:
                        pe.wait_ge(v_ready, n - 1)

                def rows_of(c):
                    if causal:
                        return hc[:, k % 2, c, i * P:(i + 1) * P]
                    return hT[:, c, n // NT, 2 + (n % NT) * P:2 + (n % NT + 1) * P]

                for c in range(CH):
                    pe.matmul(pQ[n % 2], rows_of(c), W[:, c, 0:2 * C], start=(c == 0), stop=(c == CH - 1))
                for c in range(CH):
                    last = pe.matmul(pV[n % 2], rows_of(c), W[:, c, 2 * C:3 * C], start=(c == 0), stop=(c == CH - 1))
                last.then_inc(qkv_done, 1)

            def transpose_parts(n):
                pe.wait_ge(lo_ready, n + 1)
                if n:
                    pe.wait_ge(pbd_ready, n)
                    pe.wait_ge(pba_ready, n)
                for k in range(12):
                    a, f = divmod(k, 4)
                    last = pe.transpose(pP[k // 6][:, k % 6, :], parts[:, n % 2, a, f * P:(f + 1) * P], IDB[:, :])
                last.then_inc(pt_done, 1)

            pe.wait_ge(consts, N_CONST)
            pe.wait_ge(zeroed, 2)
            for s in range(N + LP):
                if s < N:
                    transpose_rows(s)
                if 0 <= s - LQ < N:
                    project(s - LQ)
                if 0 <= s - LP < N:
                    transpose_parts(s - LP)


def attend_phase(nc, PS, V, causal, pt, mask_q, mask_k, identf, identb, m_dram, y_out):
    ctx = ExitStack()
    with ctx:
        ph = Phase(nc, ctx, "TB" if causal else "TA")
        sb, sem = ph.sb, ph.sem
        GG = B * NG
        E = HG if causal else 1
        if causal:
            STEPS = [(c, kt, max(0, kt - TC * c) * P) for c in range(NC) for kt in range(TC * (c + 1))]
        else:
            STEPS = [(c, TC * c + i, i * P) for c in range(NC) for i in range(TC)]
        NS = len(STEPS)
        START = [min(s for s in range(NS) if STEPS[s][0] == c) for c in range(NC)]
        LAST = [max(s for s in range(NS) if STEPS[s][0] == c) for c in range(NC)]
        PVLAG = 2
        LEAD = LEAD_B if causal else LEAD_A
        if causal:
            PAIRS = [[(i, k, p) for i in range(TC) for k in range(c + 1) for p in range(HG // 2)] for c in range(NC)]
        else:
            PAIRS = [[(i, 0, 0) for i in range(0, TC, 2)] for c in range(NC)]

        beside = {}
        for g in range(GG):
            for c in range(NC):
                size = LAST[c] + 1 - START[c]
                at = NS * g + START[c] - LEAD
                for k, pair in enumerate(PAIRS[c]):
                    beside.setdefault(at + (k + 1) * size // len(PAIRS[c]), []).append(("scores", g, c, pair))
                beside.setdefault(at + size + 1, []).append(("maxima", g, c, None))
                beside.setdefault(NS * g + LAST[c] + PVLAG + 2, []).append(("results", g, c, None))
        FIRST, END = min(beside), max(beside) + 1
        order = [item for s in range(FIRST, END) for item in beside.get(s, ())]
        bank, n = {}, 0
        for item in order:
            bank[item] = n
            n += 2 if item[0] == "scores" else 1
        n_banks = n
        del n_banks

        stk = sb("stk", [P, 2, 2, HG, T], BF16)
        PR = sb("PR", [P, NP, QC], FP32)
        OT = sb("OT", [P, 2, QC], FP32)
        YO = sb("YO", [P, 4, TC, HG * D], FP32)
        IDF = sb("IDF", [P, P], FP32)
        IDB = sb("IDB", [P, P], BF16)
        ZB = sb("ZB", [P, QC], BF16)
        MQ = sb("MQ", [P, HG * P], BF16)
        MK = sb("MK", [P, HG * P], BF16)
        mx = sb("mx", [P, 2, HG * TC, NC], FP32)
        mm = sb("mm", [P, HG * TC], FP32)
        nmb = sb("nmb", [P, 2, HG * TC], BF16)
        nmr = sb("nmr", [HG * TC, 2, P], BF16)
        rden = sb("rden", [P, TC, HG], FP32)
        pM = [PS[:, i, :] for i in range(4)]
        pS = [PS[:, i, :] for i in (4, 5, 6)]
        pO = PS[:, 7, :]

        consts = sem("consts")
        zeroed = sem("zeroed")
        dch = sem("dch")
        stk_loaded = [sem(f"stk_loaded{i}") for i in range(2)]
        m_put = sem("m_put")
        m_got = sem("m_got")
        nm_ready = sem("nm_ready")
        nmr_ready = sem("nmr_ready")
        m_stored = sem("m_stored")
        m_loaded = sem("m_loaded")
        s_done = sem("s_done")
        e_done = sem("e_done")
        pv_done = sem("pv_done")
        ot_ready = sem("ot_ready")
        y_ready = sem("y_ready")
        y_stored = [sem(f"y_stored{i}") for i in range(4)]
        N_LOAD = 2 * NTERM * 2
        N_STORE = 1 if causal else HG

        block = ctx.enter_context(nc.Block())

        @block.sync
        def _(sp):
            def load_stacks(g):
                b, hg = divmod(g, NG)
                half, r0 = divmod(hg * HG * D, P)
                if g >= 2:
                    sp.wait_ge(s_done, E * NS * (g - 1))
                for a in range(2):
                    for n in range(NTERM):
                        rows = pt[b, 4 * TERMS[a][n] + 2 * a + half, r0:r0 + HG * D, :]\
                            .rearrange("(j x d) t -> x d j t", x=2, d=D)
                        for x in range(2):
                            r = FIRST_ROW[x] + n * D if n < NMAX else REST_ROW[x] + (n - NMAX) * D
                            sp.dma_start(stk[r:r + D, g % 2, a, x::2, :], rows[x]).then_inc(stk_loaded[g % 2], 16)

            sp.dma_start(IDB[:, :], identb).then_inc(consts, 16)
            sp.dma_start(MQ[:, :], mask_q).then_inc(consts, 16)
            load_stacks(0)
            sp.dma_start(MK[:, :], mask_k).then_inc(consts, 16)
            sp.dma_start(IDF[:, :], identf).then_inc(consts, 16)
            load_stacks(1)
            for n in range(NC * GG):
                g, c = divmod(n, NC)
                if c == NC - 1 and g + 2 < GG:
                    load_stacks(g + 2)
                sp.wait_ge(y_ready, n + 1)
                for j in range(N_STORE):
                    w = HG * D // N_STORE
                    sp.dma_start(y_out(g // NG, g % NG, c, j), YO[:, n % 4, :, j * w:(j + 1) * w]).then_inc(y_stored[n % 4], 16)
            for i in range(4):
                sp.wait_ge(y_stored[i], 16 * N_STORE * (NC * GG // 4))

        @block.gpsimd
        def _(pool):
            pool.memset(ZB[:, :], 0.0).then_inc(zeroed, 1)
            odd = slice(M_ROW[1], HALF_ROWS)
            view = stk[:, :, :, :, :].rearrange("p g a j t -> p (g a j t)").bitcast(FP32)\
                .rearrange("p (g a j t) -> p g a j t", g=2, a=2, j=HG)
            pool.wait_ge(zeroed, 1)
            for g in range(2):
                pool.memset(view[odd, g, :, 1::2, :], 0.0).then_inc(zeroed, 1)
                pool.wait_ge(zeroed, 2 + 3 * g)
                for x in range(2):
                    pool.memset(view[M_ROW[x]:M_ROW[x] + 1, g, 1, x::2, :], ONES2).then_inc(zeroed, 1)
                    pool.wait_ge(zeroed, 3 + 3 * g + x)
            for n in range(NC * GG):
                g, c = divmod(n, NC)
                pool.wait_ge(nmr_ready, n + 1)
                pool.dma_start(m_dram[n], nmr[:, n % 2, :]).then_inc(m_stored, 16)
                if g >= 2:
                    pool.wait_ge(s_done, E * NS * (g - 1))
                pool.wait_ge(m_stored, 16 * (n + 1))
                m = m_dram[n].rearrange("(j x i) s -> x j (i s)", x=2, i=TC)
                for x in range(2):
                    pool.dma_start(stk[M_ROW[x]:M_ROW[x] + 1, g % 2, 0, x::2, c * QC:(c + 1) * QC],
                                   m[x].unsqueeze(0)).then_inc(m_loaded, 16)

        @block.scalar
        def _(act):
            act.wait_ge(zeroed, 1)
            for s in range(NS * GG + PVLAG + 2):
                for e in range(E):
                    if s < NS * GG:
                        off = STEPS[s % NS][2] if causal else 0
                        n = E * s + e
                        act.wait_ge(s_done, n + 1)
                        if n >= NP:
                            act.wait_ge(pv_done, (n - NP) // E + 1)
                        act.activation(PR[:, n % NP, off:QC], pS[n % 3][:, off:QC], ACT.Exp).then_inc(e_done, 1)
                    if e == 0:
                        g, r = divmod(s - PVLAG - 1, NS)
                        if r in LAST and g >= 0:
                            n = NC * g + LAST.index(r)
                            act.wait_ge(pv_done, NS * g + r + 1)
                            if n >= 2:
                                act.wait_ge(m_got, bank["results", (n - 2) // NC, (n - 2) % NC, None] + 1)
                            act.activation(OT[:, n % 2, :], pO, ACT.Copy).then_inc(ot_ready, 1)

        @block.vector
        def _(dve):
            chain = [0]

            def link(ins):
                chain[0] += 1
                ins.then_inc(dch, 1)
                dve.wait_ge(dch, chain[0])

            def take_scores(g, c, pair, n):
                i, k, p = pair
                par = (NC * g + c) % 2
                for x in range(2):
                    dve.wait_ge(m_put, n + x + 1)
                    s = pM[(n + x) % 4]
                    if causal:
                        w = min(QC, P * (TC * c + i + 1) - QC * k)
                        dve.reduce_max(mx[:, par, TC * (2 * p + x) + i, k:k + 1], s[:, 0:w], AX.X).then_inc(m_got, 1)
                    else:
                        dst = mx[:, par, :, 0].rearrange("p (j x i) -> p x i j", x=2, i=TC)[:, x, i:i + 2, :]
                        dve.reduce_max(dst, s.rearrange("p (i j k) -> p i j k", i=2, j=2), AX.X).then_inc(m_got, 1)

            def take_maxima(g, c, n):
                dve.wait_ge(m_put, n + 1)
                q = NC * g + c
                if q >= 2:
                    dve.wait_ge(m_stored, 16 * (q - 1))
                dve.tensor_copy(nmr[:, q % 2, :], pM[n % 4].bitcast(BF16)[0:HG * TC, 0:P]).then_inc(nmr_ready, 1)
                dve.wait_ge(nmr_ready, q + 1)
                dve.sem_inc(m_got, 1)

            def maxima(g, c, n):
                q = NC * g + c
                dve.wait_ge(m_got, n)
                if causal:
                    link(dve.reduce_max(mm[:, :], mx[:, q % 2, :, 0:c + 1], AX.X))
                else:
                    link(dve.tensor_copy(mm[:, :], mx[:, q % 2, :, 0]))
                dve.tensor_scalar(nmb[:, q % 2, :], mm[:, :], -1.0, None, ALU.mult).then_inc(nm_ready, 1)
                dve.wait_ge(nm_ready, q + 1)

            def take_results(g, c, n):
                q = NC * g + c
                dve.wait_ge(m_put, n + 1)
                x = pM[n % 4].rearrange("p (i j w) -> p i j w", i=TC, j=HG)
                link(dve.reciprocal(rden[:, :, :], x[:, :, :, D]))
                if q >= 4:
                    dve.wait_ge(y_stored[q % 4], 16 * N_STORE * (q // 4))
                dve.tensor_tensor(YO[:, q % 4, :, :].rearrange("p i (j d) -> p i j d", j=HG), x[:, :, :, 0:D],
                                  rden[:, :, :].unsqueeze(3).broadcast_to([P, TC, HG, D]), ALU.mult).then_inc(y_ready, 1)
                dve.wait_ge(y_ready, q + 1)
                dve.sem_inc(m_got, 1)

            left = {}
            for kind, g, c, pair in order:
                if kind == "scores":
                    left[g, c] = left.get((g, c), 0) + 1
            for item in order:
                kind, g, c, pair = item
                if kind == "scores":
                    take_scores(g, c, pair, bank[item])
                    left[g, c] -= 1
                    if not left[g, c]:
                        maxima(g, c, bank[item] + 2)
                elif kind == "maxima":
                    take_maxima(g, c, bank[item])
                else:
                    take_results(g, c, bank[item])

        @block.tensor
        def _(pe):
            def score_max(g, c, pair, n):
                i, k, p = pair
                if n >= 3:
                    pe.wait_ge(m_got, n - 2)
                out = [pM[(n + x) % 4] for x in range(2)]
                if causal:
                    qt = TC * c + i
                    w = min(QC, P * (qt + 1) - QC * k)
                    diagonal = k == c
                    for x in range(2):
                        r = slice(FIRST_ROW[x], FIRST_ROW[x] + HALF_ROWS)
                        j = 2 * p + x
                        last = pe.matmul(out[x][:, 0:w], stk[r, g % 2, 0, j, qt * P:(qt + 1) * P],
                                         stk[r, g % 2, 1, j, k * QC:k * QC + w], start=True, stop=not diagonal)
                        if not diagonal:
                            last.then_inc(m_put, 1)
                    if diagonal:
                        for x in range(2):
                            pe.matmul(out[x][:, w - P:w], IDB[:, :], MQ[:, 0:P], start=False, stop=True).then_inc(m_put, 1)
                else:
                    for x in range(2):
                        pe.matmul(out[x], IDB[:, :], MQ[:, :], start=True, stop=False)
                    for k in range(4):
                        t, jj = divmod(k, 2)
                        qt = TC * c + i + t
                        for x in range(2):
                            r = slice(FIRST_ROW[x], FIRST_ROW[x] + HALF_ROWS)
                            last = pe.matmul(out[x][:, k * P:(k + 1) * P], stk[r, g % 2, 0, 2 * jj + x, qt * P:(qt + 1) * P],
                                             stk[r, g % 2, 1, 2 * jj + x, qt * P:(qt + 1) * P],
                                             start=False, stop=k == 3)
                            if k == 3:
                                last.then_inc(m_put, 1)

            def transposes(kind, g, c, n):
                q = NC * g + c
                if n >= 4:
                    pe.wait_ge(m_got, n - 3)
                if kind == "maxima":
                    pe.wait_ge(nm_ready, q + 1)
                    last = pe.transpose(pM[n % 4].bitcast(BF16)[0:HG * TC, 0:P], nmb[:, q % 2, :], IDB[:, :])
                else:
                    pe.wait_ge(ot_ready, q + 1)
                    for i in range(TC):
                        last = pe.transpose(pM[n % 4][:, i * P:(i + 1) * P], OT[:, q % 2, i * P:(i + 1) * P], IDF[:, :])
                last.then_inc(m_put, 1)

            def score(s, e):
                g, r = divmod(s, NS)
                c, kt, off = STEPS[r]
                n = E * s + e
                if e == 0 and r in START:
                    pe.wait_ge(m_loaded, 32 * (NC * g + c + 1))
                if n >= 3:
                    pe.wait_ge(e_done, n - 2)
                o = pS[n % 3]
                if causal:
                    rows = slice(0, ROWS[e % 2])
                    last = pe.matmul(o[:, off:QC], stk[rows, g % 2, 1, e, kt * P:(kt + 1) * P],
                                     stk[rows, g % 2, 0, e, c * QC + off:(c + 1) * QC], start=True, stop=kt < TC * c)
                    if kt >= TC * c:
                        last = pe.matmul(o[:, off:off + P], IDB[:, :], MK[:, 0:P], start=False, stop=True)
                else:
                    pe.matmul(o, IDB[:, :], MK[:, :], start=True, stop=False)
                    for j in range(HG):
                        rows = slice(0, ROWS[j % 2])
                        last = pe.matmul(o[:, j * P:(j + 1) * P], stk[rows, g % 2, 1, j, kt * P:(kt + 1) * P],
                                         stk[rows, g % 2, 0, j, kt * P:(kt + 1) * P], start=False, stop=j == HG - 1)
                last.then_inc(s_done, 1)

            def weigh(s):
                g, r = divmod(s, NS)
                b, hg = divmod(g, NG)
                c, kt, off = STEPS[r]
                pe.wait_ge(e_done, E * (s + 1))
                if r in START:
                    pe.wait_ge(ot_ready, NC * g + c)
                for j in range(HG):
                    if causal:
                        pr = PR[:, (E * s + j) % NP, off:QC]
                        o = pO[HD * j:HD * j + VW, off:QC]
                        first, end = kt == 0, r == LAST[c]
                    else:
                        pr = PR[:, s % NP, j * P:(j + 1) * P]
                        o = pO[HD * j:HD * j + VW, off:off + P]
                        first, end = True, True
                    last = pe.matmul(o, V[:, NT * b + kt, HG * hg + j, :], pr, start=first, stop=end)
                last.then_inc(pv_done, 1)

            pe.wait_ge(consts, 64)
            pe.wait_ge(zeroed, 7)
            pe.matmul(pO, ZB[:, 0:P], ZB[:, :], start=True, stop=True)
            loaded = set()
            for s in range(FIRST, max(END, NS * GG + PVLAG)):
                items = list(beside.get(s, ()))
                for e in range(E):
                    if 0 <= s < NS * GG:
                        score(s, e)
                    if e == min(1, E - 1) and 0 <= s - PVLAG < NS * GG:
                        weigh(s - PVLAG)
                    take = (len(items) + E - 1 - e) // (E - e)
                    for item in items[:take]:
                        kind, g, c, pair = item
                        if kind == "scores":
                            if g not in loaded:
                                loaded.add(g)
                                pe.wait_ge(stk_loaded[g % 2], 16 * N_LOAD * (g // 2 + 1))
                            score_max(g, c, pair, bank[item])
                        else:
                            transposes(kind, g, c, bank[item])
                    items = items[take:]


def router_phase(nc, PS, mem, yB, y0d, x1d, projw, rw, ln2w, ln2b, identf, xs_dram):
    ctx = ExitStack()
    with ctx:
        ph = Phase(nc, ctx, "C")
        sb, sem = ph.sb, ph.sem
        RES, H2, LG = mem.RES, mem.H2, mem.LG
        PW = sb("PW", [P, CH, C], FP32)
        RW = sb("RW", [P, CH, E4], FP32)
        LNW = sb("LNW", [P, C], FP32)
        LNB = sb("LNB", [P, C], FP32)
        zeros = sb("zeros", [P, C], FP32)
        yt = sb("yt", [P, 2, C], FP32)
        y0t = sb("y0t", [P, 2, C], FP32)
        x1t = sb("x1t", [P, 2, C], FP32)
        yT = sb("yT", [P, 2, CH, P], FP32)
        hh = sb("hh", [P, 2, C], FP32)
        hw = sb("hw", [P, C], FP32)
        st = sb("st", [P, 6], FP32)
        mv = sb("mv", [P, N, 2], FP32)
        ve = sb("ve", [P, N], FP32)
        sd = sb("sd", [P, N], FP32)
        rs = sb("rs", [P, N], FP32)
        pT = [PS[:, i, 0:C].rearrange("p (c t) -> p c t", c=CH) for i in (0, 1)]
        pP = [PS[:, i, 0:C] for i in (2, 3)]
        pL = [PS[:, i, 0:E4] for i in (4, 5)]
        consts = sem("consts")
        zeroed = sem("zeroed")
        y_loaded = [sem(f"y_loaded{i}") for i in range(2)]
        y0_loaded = [sem(f"y0_loaded{i}") for i in range(2)]
        x1_loaded = [sem(f"x1_loaded{i}") for i in range(2)]
        t_done = sem("t_done")
        T_ready = sem("T_ready")
        p_done = sem("p_done")
        dch = sem("dch")
        y1_ready = sem("y1_ready")
        sd_ready = sem("sd_ready")
        var_ready = sem("var_ready")
        h_ready = sem("h_ready")
        kept = sem("kept")
        l_done = sem("l_done")
        l_ready = sem("l_ready")
        res_ready = sem("res_ready")
        block = ctx.enter_context(nc.Block())

        @block.sync
        def _(sp):
            sp.dma_start(mem.IDF[:, :], identf).then_inc(consts, 16)
            sp.dma_start(PW[:, :, :], projw).then_inc(consts, 16)
            sp.dma_start(RW[:, :, :], rw).then_inc(consts, 16)
            sp.dma_start(LNW[:, :], ln2w).then_inc(consts, 16)
            sp.dma_start(LNB[:, :], ln2b).then_inc(consts, 16)
            for n in range(N):
                if n >= 2:
                    sp.wait_ge(t_done, n - 1)
                sp.dma_start(yt[:, n % 2, :], yB[n]).then_inc(y_loaded[n % 2], 16)
                if n >= 2:
                    sp.wait_ge(y1_ready, n - 1)
                sp.dma_start(y0t[:, n % 2, :], y0d[n]).then_inc(y0_loaded[n % 2], 16)
            for n in range(N):
                if n >= 2:
                    sp.wait_ge(res_ready, n - 1)
                sp.dma_start(x1t[:, n % 2, :], x1d[n]).then_inc(x1_loaded[n % 2], 16)

        @block.gpsimd
        def _(pool):
            pool.memset(zeros[:, :], 0.0).then_inc(zeroed, 1)
            pool.wait_ge(zeroed, 1)
            pool.dma_start(xs_dram, zeros[:, :].unsqueeze(1).broadcast_to([P, NE, C])).then_inc(mem.xs_zeroed, 16)
            for n in range(N):
                pool.wait_ge(h_ready, n + 1)
                pool.tensor_copy(H2[:, n, :], hh[:, n % 2, :]).then_inc(kept, 1)
                pool.wait_ge(x1_loaded[n % 2], 16 * (n // 2 + 1))
                pool.tensor_tensor(RES[:, n, :], RES[:, n, :], x1t[:, n % 2, :], ALU.add).then_inc(res_ready, 1)

        @block.scalar
        def _(act):
            for dst, s in mem.loads:
                act.dma_start(dst, s).then_inc(mem.loaded, 16)
            for n in range(2 * N):
                if n == N:
                    act.wait_ge(var_ready, 1)
                    act.activation(sd[:, :], ve[:, :], ACT.Sqrt).then_inc(sd_ready, 1)
                act.wait_ge(t_done, n + 1)
                if n >= 2:
                    if n - 2 < N:
                        act.wait_ge(p_done, n - 1)
                    else:
                        act.wait_ge(l_done, n - 2 - N + 1)
                act.activation(yT[:, n % 2, :, :], pT[n % 2], ACT.Copy).then_inc(T_ready, 1)

        @block.vector
        def _(dve):
            chain = [0]

            def link(ins):
                chain[0] += 1
                ins.then_inc(dch, 1)
                dve.wait_ge(dch, chain[0])

            dve.wait_ge(consts, 80)
            for n in range(N):
                dve.wait_ge(p_done, n + 1)
                dve.wait_ge(y0_loaded[n % 2], 16 * (n // 2 + 1))
                dve.tensor_tensor(RES[:, n, :], pP[n % 2], y0t[:, n % 2, :], ALU.add).then_inc(y1_ready, 1)
                dve.wait_ge(y1_ready, n + 1)
                link(dve.bn_stats(st[:, :], RES[:, n, :]))
                link(dve.bn_aggr(mv[:, n, :], st[:, :]))
            dve.tensor_scalar(ve[:, :], mv[:, :, 1], EPS, None, ALU.add).then_inc(var_ready, 1)
            dve.wait_ge(sd_ready, 1)
            link(dve.reciprocal(rs[:, :], sd[:, :]))

            def logits_out(n):
                dve.wait_ge(l_done, n + 1)
                dve.tensor_copy(LG[:, n, :], pL[n % 2]).then_inc(l_ready, 1)

            for n in range(N):
                if n >= 2:
                    dve.wait_ge(t_done, N + n - 1)
                    dve.wait_ge(kept, n - 1)
                link(dve.tensor_scalar(hh[:, n % 2, :], RES[:, n, :], mv[:, n, 0:1], rs[:, n:n + 1], ALU.subtract, ALU.mult))
                link(dve.tensor_tensor(hw[:, :], hh[:, n % 2, :], LNW[:, :], ALU.mult))
                dve.tensor_tensor(hh[:, n % 2, :], hw[:, :], LNB[:, :], ALU.add).then_inc(h_ready, 1)
                dve.wait_ge(h_ready, n + 1)
                if n:
                    logits_out(n - 1)
            logits_out(N - 1)

        @block.tensor
        def _(pe):
            def transposes(n):
                m = n % N
                src = yt if n < N else hh
                if n < N:
                    pe.wait_ge(y_loaded[n % 2], 16 * (n // 2 + 1))
                else:
                    pe.wait_ge(h_ready, m + 1)
                if n >= 2:
                    pe.wait_ge(T_ready, n - 1)
                for c in range(CH):
                    last = pe.transpose(pT[n % 2][:, c, :], src[:, n % 2, c * P:(c + 1) * P], mem.IDF[:, :])
                last.then_inc(t_done, 1)

            def project(n):
                pe.wait_ge(T_ready, n + 1)
                if n >= 2:
                    pe.wait_ge(y1_ready, n - 1)
                for c in range(CH):
                    last = pe.matmul(pP[n % 2], yT[:, n % 2, c, :], PW[:, c, :], start=(c == 0), stop=(c == CH - 1))
                last.then_inc(p_done, 1)

            def route(n):
                pe.wait_ge(T_ready, N + n + 1)
                if n >= 2:
                    pe.wait_ge(l_ready, n - 1)
                for c in range(CH):
                    last = pe.matmul(pL[n % 2], yT[:, n % 2, c, :], RW[:, c, :], start=(c == 0), stop=(c == CH - 1))
                last.then_inc(l_done, 1)

            pe.wait_ge(consts, 80)
            transposes(0)
            for n in range(1, N + 1):
                if n < N:
                    transposes(n)
                project(n - 1)
            transposes(N)
            for n in range(1, N + 1):
                if n < N:
                    transposes(N + n)
                route(n - 1)


def expert_phase(nc, PS, mem, xs_dram, xs_tiles, ys_tiles, ys_dram, out):
    ctx = ExitStack()
    with ctx:
        ph = Phase(nc, ctx, "D")
        sb, sem = ph.sb, ph.sem
        RES, H2, LG, WV, WP = mem.RES, mem.H2, mem.LG, mem.WV, mem.WP
        mxl = sb("mxl", [P, N], FP32)
        ge = sb("ge", [P, N, E4], FP32)
        oh = sb("oh", [P, E4, N], FP32)
        ohT = oh[:, :, :].rearrange("p e n -> p n e")
        oh2 = oh[:, :, :].rearrange("p e n -> p (e n)")
        inc_ = sb("inc_", [P, E4, N], FP32)
        tot = sb("tot", [P, E4, N], FP32)
        inc2 = inc_[:, :, :].rearrange("p e n -> p (e n)")
        tot2 = tot[:, :, :].rearrange("p e n -> p (e n)")
        ni = sb("ni", [P, E4], mybir.dt.int32)
        nf = sb("nf", [P, E4], FP32)
        ts = sb("ts", [P, E4], FP32)
        base = sb("base", [P, E4], FP32)
        slotf = sb("slotf", [P, N], FP32)
        slot = sb("slot", [P, N], mybir.dt.uint32)
        cmp_ = sb("cmp_", [1, NE, E4 - 1], FP32)
        eidf = sb("eidf", [1, NE], FP32)
        eid = sb("eid", [1, NE], mybir.dt.int32)
        xs = sb("xs", [P, 2, C], FP32)
        xT = sb("xT", [P, 2, CH, P], FP32)
        sg = sb("sg", [P, F], FP32)
        u = sb("u", [P, F], FP32)
        uT = sb("uT", [P, 2, F // P, P], FP32)
        yo = sb("yo", [P, 2, C], FP32)
        NGB = 4
        gt = sb("gt", [P, NGB, C], FP32)
        pG = PS[:, 0:4, :].rearrange("p a b -> p (a b)")
        pU = PS[:, 4:6, :].rearrange("p a (b t) -> p (a b) t", t=P)
        pX = PS[:, 6, 0:C].rearrange("p (c t) -> p c t", c=CH)
        pD = PS[:, 7, 0:C]
        pA = PS[:, 0, 0:E4 * N]
        pB = PS[:, 1, 0:E4 * N]
        dch = sem("dch")
        oh_ready = sem("oh_ready")
        cnt_done = sem("cnt_done")
        slot_ready = sem("slot_ready")
        eid_ready = sem("eid_ready")
        scattered = sem("scattered")
        xs_loaded = [sem(f"xs_loaded{i}") for i in range(2)]
        x_tr = sem("x_tr")
        xt_ready = sem("xt_ready")
        gate_done = sem("gate_done")
        g_done = sem("g_done")
        silu_done = sem("silu_done")
        u_ready = sem("u_ready")
        ut_done = sem("ut_done")
        ut_ready = sem("ut_ready")
        d_done = sem("d_done")
        yo_ready = sem("yo_ready")
        ys_stored = [sem(f"ys_stored{i}") for i in range(2)]
        gathered = [sem(f"gathered{i}") for i in range(NGB)]
        o_ready = sem("o_ready")
        o_stored = [sem(f"o_stored{i}") for i in range(NGB)]
        block = ctx.enter_context(nc.Block())

        @block.sync
        def _(sp):
            sp.wait_ge(scattered, 16 * N)
            for j in range(NE):
                if j >= 2:
                    sp.wait_ge(x_tr, j - 1)
                sp.dma_start(xs[:, j % 2, :], xs_tiles[j]).then_inc(xs_loaded[j % 2], 16)
            for n in range(N):
                sp.wait_ge(o_ready, n + 1)
                sp.dma_start(out[n], gt[:, n % NGB, :]).then_inc(o_stored[n % NGB], 16)
            for i in range(NGB):
                sp.wait_ge(o_stored[i], 16 * (N // NGB))

        @block.gpsimd
        def _(pool):
            pool.wait_ge(slot_ready, 1)
            pool.wait_ge(mem.xs_zeroed, 16)
            for n in range(N):
                pool.indirect_dma_start(xs_dram, bass.IndirectOffsetOnAxis(ap=slot[:, n:n + 1], axis=0),
                                        H2[:, n, :], None).then_inc(scattered, 16)
            for j in range(NE):
                pool.wait_ge(yo_ready, j + 1)
                pool.dma_start(ys_tiles[j], yo[:, j % 2, :]).then_inc(ys_stored[j % 2], 16)
            for i in range(2):
                pool.wait_ge(ys_stored[i], 16 * ((NE - i + 1) // 2))
            for n in range(N):
                if n >= NGB:
                    pool.wait_ge(o_stored[n % NGB], 16 * (n // NGB))
                pool.indirect_dma_start(gt[:, n % NGB, :], None, ys_dram,
                                        bass.IndirectOffsetOnAxis(ap=slot[:, n:n + 1], axis=0)).then_inc(gathered[n % NGB], 16)

        @block.scalar
        def _(act):
            for j in range(NE):
                act.wait_ge(gate_done, j + 1)
                if j:
                    act.wait_ge(u_ready, j)
                act.activation(sg[:, :], pG[:, 0:F], ACT.Silu).then_inc(silu_done, 1)
                act.wait_ge(ut_done, j + 1)
                if j >= 2:
                    act.wait_ge(d_done, j - 1)
                act.activation(uT[:, j % 2, :, :], pU, ACT.Copy).then_inc(ut_ready, 1)

        @block.vector
        def _(dve):
            chain = [0]

            def link(ins):
                chain[0] += 1
                ins.then_inc(dch, 1)
                dve.wait_ge(dch, chain[0])

            dve.wait_ge(mem.loaded, 16 * mem.n_loads)
            link(dve.reduce_max(mxl[:, :], LG[:, :, :], AX.X))
            link(dve.tensor_tensor(ge[:, :, :], LG[:, :, :], mxl[:, :].unsqueeze(2).broadcast_to([P, N, E4]), ALU.is_ge))
            link(dve.tensor_tensor(ge[:, :, :], ge[:, :, :], mem.RANK[:, :].unsqueeze(1).broadcast_to([P, N, E4]), ALU.mult))
            link(dve.reduce_max(mxl[:, :], ge[:, :, :], AX.X))
            dve.tensor_tensor(ohT, ge[:, :, :], mxl[:, :].unsqueeze(2).broadcast_to([P, N, E4]), ALU.is_equal).then_inc(oh_ready, 1)
            dve.wait_ge(cnt_done, 1)
            link(dve.tensor_copy(tot2, pB))
            link(dve.tensor_tensor_scan(inc2, mem.RESET[:, :], tot2, 0.0, ALU.mult, ALU.add))
            link(dve.tensor_scalar(nf[:, :], inc_[:, :, N - 1], float(P - 1), None, ALU.add))
            link(dve.tensor_copy(ni[:, :], nf[:, :]))
            link(dve.tensor_scalar(ni[:, :], ni[:, :], 7, None, ALU.logical_shift_right))
            link(dve.tensor_copy(nf[:, :], ni[:, :]))
            link(dve.tensor_tensor_scan(ts[:, :], mem.ONE[:, 0:E4], nf[:, :], 0.0, ALU.mult, ALU.add))
            link(dve.tensor_tensor(ts[:, :], ts[:, :], nf[:, :], ALU.subtract))
            link(dve.tensor_scalar(base[:, :], ts[:, :], float(P), None, ALU.mult))
            link(dve.tensor_tensor(inc2, inc2, tot2, ALU.subtract))
            link(dve.tensor_tensor(inc2, inc2, pA, ALU.add))
            link(dve.tensor_tensor(inc_[:, :, :], inc_[:, :, :], base[:, :].unsqueeze(2).broadcast_to([P, E4, N]), ALU.add))
            link(dve.tensor_tensor(inc2, inc2, oh2, ALU.mult))
            link(dve.reduce_sum(slotf[:, :], inc_[:, :, :].rearrange("p e n -> p n e"), AX.X))
            dve.tensor_copy(slot[:, :], slotf[:, :]).then_inc(slot_ready, 1)
            link(dve.tensor_tensor(cmp_[:, :, :], mem.TILE[:, :].unsqueeze(2).broadcast_to([1, NE, E4 - 1]),
                                   ts[0:1, 1:E4].unsqueeze(1).broadcast_to([1, NE, E4 - 1]), ALU.is_ge))
            link(dve.reduce_sum(eidf[:, :], cmp_[:, :, :], AX.X))
            dve.tensor_copy(eid[:, :], eidf[:, :]).then_inc(eid_ready, 1)

            def xT_out(j):
                dve.wait_ge(x_tr, j + 1)
                if j >= 2:
                    dve.wait_ge(g_done, j - 1)
                dve.tensor_copy(xT[:, j % 2, :, :], pX).then_inc(xt_ready, 1)

            def y_out(j):
                dve.wait_ge(d_done, j + 1)
                if j >= 2:
                    dve.wait_ge(ys_stored[j % 2], 16 * (j // 2))
                dve.tensor_copy(yo[:, j % 2, :], pD).then_inc(yo_ready, 1)

            xT_out(0)
            for j in range(NE):
                dve.wait_ge(silu_done, j + 1)
                dve.wait_ge(g_done, j + 1)
                if j:
                    dve.wait_ge(ut_done, j)
                dve.tensor_tensor(u[:, :], sg[:, :], pG[:, F:2 * F], ALU.mult).then_inc(u_ready, 1)
                if j + 1 < NE:
                    xT_out(j + 1)
                if j:
                    y_out(j - 1)
            y_out(NE - 1)
            for n in range(N):
                dve.wait_ge(gathered[n % NGB], 16 * (n // NGB + 1))
                dve.tensor_tensor(gt[:, n % NGB, :], gt[:, n % NGB, :], RES[:, n, :], ALU.add).then_inc(o_ready, 1)

        @block.tensor
        def _(pe):
            pe.wait_ge(mem.loaded, 16 * mem.n_loads)
            pe.wait_ge(oh_ready, 1)
            pe.matmul(pA, mem.LOWER[:, :], oh2, start=True, stop=True)
            pe.matmul(pB, mem.ONE[:, :], oh2, start=True, stop=True).then_inc(cnt_done, 1)

            def rows_in(j):
                pe.wait_ge(xs_loaded[j % 2], 16 * (j // 2 + 1))
                if j:
                    pe.wait_ge(xt_ready, j)
                for c in range(CH):
                    last = pe.transpose(pX[:, c, :], xs[:, j % 2, c * P:(c + 1) * P], mem.IDF[:, :])
                last.then_inc(x_tr, 1)

            def up(j, e):
                pe.wait_ge(xt_ready, j + 1)
                for k in range(2 * F // QC):
                    if j and k == 0:
                        pe.wait_ge(silu_done, j)
                    if j and k == F // QC:
                        pe.wait_ge(u_ready, j)
                    for c in range(CH):
                        last = pe.matmul(pG[:, k * QC:(k + 1) * QC], xT[:, j % 2, c, :],
                                         WV[:, bass.ds(e * (CH * 2 * F) + c * 2 * F + k * QC, QC)],
                                         start=(c == 0), stop=(c == CH - 1))
                    if k == F // QC - 1:
                        last.then_inc(gate_done, 1)
                last.then_inc(g_done, 1)

            def hidden(j):
                pe.wait_ge(u_ready, j + 1)
                if j:
                    pe.wait_ge(ut_ready, j)
                for f in range(F // P):
                    last = pe.transpose(pU[:, f, :], u[:, f * P:(f + 1) * P], mem.IDF[:, :])
                last.then_inc(ut_done, 1)

            def down(j, e):
                pe.wait_ge(ut_ready, j + 1)
                if j:
                    pe.wait_ge(yo_ready, j)
                for f in range(F // P):
                    last = pe.matmul(pD, uT[:, j % 2, f, :], WP[:, bass.ds(e * (F // P * C) + f * C, C)],
                                     start=(f == 0), stop=(f == F // P - 1))
                last.then_inc(d_done, 1)

            pe.wait_ge(eid_ready, 1)
            rows_in(0)
            before = None
            for j in range(NE):
                e = pe.value_load(eid[0:1, j:j + 1], min_val=0, max_val=E4 - 1)
                up(j, e)
                if j + 1 < NE:
                    rows_in(j + 1)
                if j:
                    down(j - 1, before)
                hidden(j)
                before = e
            down(NE - 1, before)


class Memory:
    pass


def expert_layer(nc, PS, yB, y0d, x1d, projw, rw, ln2w, ln2b, wv, wp, rank, reset, lower, tiles, one, identf, xs_rows, ys_rows, out):
    ctx = ExitStack()
    with ctx:
        ph = Phase(nc, ctx, "M")
        mem = Memory()
        mem.RES = ph.sb("RES", [P, N, C], FP32)
        mem.H2 = ph.sb("H2", [P, N, C], FP32)
        mem.LG = ph.sb("LG", [P, N, E4], FP32)
        mem.WV = ph.sb("WV", [P, E4 * CH * 2 * F], FP32)
        mem.WP = ph.sb("WP", [P, E4 * F * C // P], FP32)
        mem.IDF = ph.sb("IDF", [P, P], FP32)
        mem.RANK = ph.sb("RANK", [P, E4], FP32)
        mem.RESET = ph.sb("RESET", [P, E4 * N], FP32)
        mem.LOWER = ph.sb("LOWER", [P, P], FP32)
        mem.ONE = ph.sb("ONE", [P, P], FP32)
        mem.TILE = ph.sb("TILE", [1, NE], FP32)
        mem.loaded = ph.sem("loaded")
        mem.xs_zeroed = ph.sem("xs_zeroed")
        loads = [(mem.RANK[:, :], rank), (mem.RESET[:, :], reset), (mem.LOWER[:, :], lower),
                 (mem.ONE[:, :], one), (mem.TILE[:, :], tiles)]
        step = CH * 2 * F
        loads += [(mem.WV[:, e * step:(e + 1) * step].rearrange("p (c n) -> p c n", c=CH), wv[e]) for e in range(E4)]
        step = F * C // P
        loads += [(mem.WP[:, e * step:(e + 1) * step].rearrange("p (f n) -> p f n", n=C), wp[e]) for e in range(E4)]
        mem.n_loads = len(loads)
        mem.loads = loads

        def tiled(t):
            return t.rearrange("(n p) c -> n p c", p=P)

        xs_view = xs_rows.rearrange("(n p) c -> p n c", p=P)
        router_phase(nc, PS, mem, tiled(yB), tiled(y0d), tiled(x1d), projw, rw, ln2w, ln2b, identf, xs_view)
        expert_phase(nc, PS, mem, xs_rows, tiled(xs_rows), tiled(ys_rows), ys_rows, tiled(out))


def build(nc, x, wA, bA, ln1w, ln1b, cw, wB, ropec, ropes, mqk, mkq, bqk, identf, identb, projw, rw, ln2w, ln2b, wv, wp,
          rank, reset, lower, tiles, one, ptA, ptB, mA, mB, att, x1d, y0d, yB, xs, ys, out):
    with ExitStack() as ctx:
        PS = ctx.enter_context(nc.psum_tensor("PS", [P, 8, QC], FP32))

        def batch(t):
            r = t.rearrange("(b i p) c -> b p i c", b=B, p=P)
            return lambda b: r[b]

        att_heads = att.rearrange("r c -> (r c)").rearrange("(b g h c i s d) -> b g c h s i d", b=B, g=NG, h=HG, c=NC, i=TC, d=D)
        y_rows = yB.rearrange("(b c i s) (g w) -> b g c s i w", b=B, c=NC, i=TC, g=NG)
        with nc.sbuf_tensor("V", [P, N, H, VW], FP32) as V:
            project_phase(nc, PS, V, False, batch(x), None, wA, bA, None, None, None, None, None, identf, identb, ptA, None, None)
            attend_phase(nc, PS, V, False, ptA, bqk, bqk, identf, identb, mA, lambda b, g, c, j: att_heads[b, g, c, j])
            project_phase(nc, PS, V, True, batch(x), batch(att), wB, None, ln1w, ln1b, cw, ropec, ropes, identf, identb,
                          ptB, batch(x1d), batch(y0d))
            attend_phase(nc, PS, V, True, ptB, mqk, mkq, identf, identb, mB, lambda b, g, c, j: y_rows[b, g, c])
        expert_layer(nc, PS, yB, y0d, x1d, projw, rw, ln2w, ln2b, wv, wp, rank, reset, lower, tiles, one, identf, xs, ys, out)


def kernel(**inputs):
    import ml_dtypes
    import numpy as np
    import concourse.bacc as bacc
    from concourse.bass_utils import run_bass_kernel_spmd as run

    def lay(name):
        return np.ascontiguousarray(inputs[name])

    def halves(w):
        return np.ascontiguousarray(w.reshape(CH, P, -1).transpose(1, 0, 2))

    def col(v):
        return np.ascontiguousarray(v.reshape(CH, P).T)

    inv = (1.0 / (10000.0 ** (np.arange(0, D, 2, dtype=np.float32) / np.float32(D)))).astype(np.float32)
    ang = (np.arange(T, dtype=np.float32)[:, None] * inv[None]).astype(np.float32)
    cos = np.concatenate([np.cos(ang)] * 2, -1).astype(np.float32)
    sin = np.concatenate([-np.sin(ang), np.sin(ang)], -1).astype(np.float32)

    def table(t):
        t = np.stack([t * np.float32(D ** -0.5), t], 1)
        return np.ascontiguousarray(t.reshape(NT, P, 2, D).transpose(1, 0, 2, 3).astype(np.float32))

    neg = np.float32(-1e30)
    r = np.arange(P)
    qk_mask = np.where(r[None] <= r[:, None], np.float32(0), neg)
    block_mask = np.where(r[None] // 32 == r[:, None] // 32, np.float32(0), neg)
    bf = ml_dtypes.bfloat16
    wq = lay("L0_attn_w_qkv")
    arrays = {
        "x": lay("L0_attn_hidden_states").reshape(B * T, C),
        "wA": halves(np.ascontiguousarray(wq.T)),
        "bA": np.ascontiguousarray(np.broadcast_to(lay("L0_attn_b_qkv")[None], (P, 3 * C))),
        "ln1w": col(lay("L0_ffn_ln1_w")), "ln1b": col(lay("L0_ffn_ln1_b")),
        "cw": halves(lay("L0_ffn_conv_w").reshape(C, 3)),
        "wB": halves(lay("L0_ffn_attn_w")),
        "ropec": table(cos), "ropes": table(sin),
        "mqk": np.tile(qk_mask, (1, HG)).astype(bf), "mkq": np.tile(qk_mask.T, (1, HG)).astype(bf),
        "bqk": np.tile(block_mask, (1, HG)).astype(bf),
        "identf": np.eye(P, dtype=np.float32), "identb": np.eye(P, dtype=np.float32).astype(bf),
    }
    arrays.update({
        "projw": halves(lay("L0_ffn_proj_w")), "rw": halves(lay("L0_ffn_router_w")),
        "ln2w": np.ascontiguousarray(np.broadcast_to(lay("L0_ffn_ln2_w")[None], (P, C))),
        "ln2b": np.ascontiguousarray(np.broadcast_to(lay("L0_ffn_ln2_b")[None], (P, C))),
        "wv": np.ascontiguousarray(lay("L0_ffn_expert_wv").reshape(E4, CH, P, 2 * F).transpose(0, 2, 1, 3)),
        "wp": np.ascontiguousarray(lay("L0_ffn_expert_proj").reshape(E4, F // P, P, C).transpose(0, 2, 1, 3)),
        "rank": np.ascontiguousarray(np.broadcast_to(np.arange(E4, 0, -1, dtype=np.float32)[None], (P, E4))),
        "reset": np.ascontiguousarray(np.broadcast_to((np.arange(E4 * N) % N != 0).astype(np.float32)[None], (P, E4 * N))),
        "lower": (r[:, None] < r[None]).astype(np.float32),
        "tiles": np.arange(NE, dtype=np.float32)[None],
        "one": np.ones((P, P), np.float32),
    })
    nc = bacc.Bacc("TRN2", target_bir_lowering=False, num_devices=1)
    args = [nc.dram_tensor(k + "_dram", a.shape, mybir.dt.from_np(a.dtype), kind="ExternalInput").ap() for k, a in arrays.items()]
    for k in ("ptA", "ptB"):
        args.append(nc.dram_tensor(k + "_dram", (B, 12, P, T), BF16, kind="Internal").ap())
    for k in ("mA", "mB"):
        args.append(nc.dram_tensor(k + "_dram", (B * NG * NC, HG * TC, P), BF16, kind="Internal").ap())
    for k, rows in (("att", B * T), ("x1d", B * T), ("y0d", B * T), ("yB", B * T), ("xs", NE * P), ("ys", NE * P)):
        args.append(nc.dram_tensor(k + "_dram", (rows, C), FP32, kind="Internal").ap())
    o = nc.dram_tensor("out_dram", (B * T, C), FP32, kind="ExternalOutput").ap()
    args.append(o)
    build(nc, *args)
    res = run(nc, [{k + "_dram": a for k, a in arrays.items()}], core_ids=[0])
    return res.results[0]["out_dram"].reshape(B, T, C)
```

```python
import concourse.bass as bass
from concourse import mybir
from contextlib import ExitStack

FP32 = mybir.dt.float32
BF16 = mybir.dt.bfloat16
ALU = mybir.AluOpType
ACT = mybir.ActivationFunctionType
AX = mybir.AxisListType

B = 2
T = 2048
C = 256
P = 128
NT = T // P
CH = C // P
H = 16
D = C // H
HG = 4
NG = H // HG
QC = 512
NC = T // QC
TC = QC // P
NTERM = 6
VW = D + 1
NP = 12
HD = 32
ONES2 = 1.0019378662109375
E4 = 4
F = 4 * C
NE = B * NT + E4 - 1
EPS = 1e-5
LEAD_A = 27
LEAD_B = 21
TERMS = [[0, 0, 1, 1, 0, 2], [0, 1, 0, 1, 2, 0]]
NMAX = 4
HALF_ROWS = NMAX * D
FIRST_ROW = [0, HALF_ROWS]
REST_ROW = [HALF_ROWS, 0]
M_ROW = [HALF_ROWS + (NTERM - NMAX) * D, (NTERM - NMAX) * D]
ROWS = [M_ROW[0] + 1, P]
N = B * NT
XW = 2 * C + 1


class Phase:

    def __init__(self, nc, ctx, tag):
        self.nc, self.ctx, self.tag = nc, ctx, tag

    def sb(self, name, shape, dt):
        return self.ctx.enter_context(self.nc.sbuf_tensor(name + self.tag, shape, dt))

    def sem(self, name):
        return self.ctx.enter_context(self.nc.semaphore(name + self.tag))


def project_phase(nc, PS, V, causal, src, add, w_dram, bias, ln_w, ln_b, conv_w, rope_c, rope_s, identf, identb,
                  pt, x_out, h_out):
    ctx = ExitStack()
    with ctx:
        ph = Phase(nc, ctx, "PB" if causal else "PA")
        sb, sem = ph.sb, ph.sem

        W = sb("W", [P, CH, 3 * C], FP32)
        X = sb("X", [P, N, C], FP32)
        hT = sb("hT", [P, CH, B, T + 2], FP32)
        hn = sb("hn", [P, 4, C], FP32)
        qk = sb("qk", [P, 2, 2 * C], FP32)
        r1 = sb("r1", [P, 2, 2 * C], FP32)
        parts = sb("parts", [P, 4, 3, 2 * C], BF16)
        PB = sb("PB", [P, 2, 12, QC], BF16)
        IDF = sb("IDF", [P, P], FP32)
        IDB = sb("IDB", [P, P], BF16)
        st = sb("st", [P, N, 6], FP32)
        mv = sb("mv", [P, N, 2], FP32)
        ve = sb("ve", [P, N], FP32)
        sd = sb("sd", [P, N], FP32)
        rs = sb("rs", [P, N], FP32)
        if causal:
            AD = sb("AD", [P, N, C], FP32)
            hc = sb("hc", [P, 2, CH, QC], FP32)
            ra = sb("ra", [P, 2, 2 * C], FP32)
            rb = sb("rb", [P, 2, 2 * C], FP32)
            RC = sb("RC", [P, NT, 2, D], FP32)
            RS = sb("RS", [P, NT, 2, D], FP32)
            LW = sb("LW", [P, CH], FP32)
            LB = sb("LB", [P, CH], FP32)
            CW = sb("CW", [P, CH, 3], FP32)
        else:
            BI = sb("BI", [P, 3 * C], FP32)
            BQ = sb("BQ", [P, C], FP32)
        pT = [PS[:, i, 0:CH * P].rearrange("p (c t) -> p c t", c=CH) for i in (0, 1)]
        pQ = [PS[:, i, :] for i in (2, 3)]
        pV = [PS[:, i, 0:C] for i in (4, 5)]
        pP = [PS[:, i, :].bitcast(BF16)[:, 0:6 * P].rearrange("p (n t) -> p n t", n=6) for i in (6, 7)]

        consts = sem("consts")
        rows = [sem(f"rows{k}") for k in range(NC + 1)]
        zeroed = sem("zeroed")
        dch = sem("dch")
        sum_ready = sem("sum_ready") if causal else None
        var_ready = sem("var_ready")
        sd_ready = sem("sd_ready")
        y0_ready = sem("y0_ready") if causal else None
        hn_ready = sem("hn_ready")
        tp_done = sem("tp_done")
        ht_ready = sem("ht_ready")
        hc_ready = sem("hc_ready") if causal else None
        qkv_done = sem("qkv_done")
        v_ready = sem("v_ready") if causal else None
        ro_ready = sem("ro_ready") if causal else None
        qk_ready = sem("qk_ready")
        hi_ready = sem("hi_ready")
        r1_ready = sem("r1_ready")
        mid_ready = sem("mid_ready")
        lo_ready = sem("lo_ready")
        pt_done = sem("pt_done")
        pbd_ready = sem("pbd_ready")
        pba_ready = sem("pba_ready")
        pt_stored = [sem(f"pt_stored{i}") for i in range(2)]
        x_stored = sem("x_stored") if causal else None

        AHEAD = 2
        LQ = 6 if causal else 2
        LP = LQ + 3
        NSTAT = 2 if causal else 1
        N_CONST = 16 * (8 if causal else 4)

        block = ctx.enter_context(nc.Block())

        @block.sync
        def _(sp):
            for b in range(B):
                for c in range(NC):
                    t = slice(TC * c, TC * (c + 1))
                    sp.dma_start(X[:, NT * b + TC * c:NT * b + TC * (c + 1), :], src(b)[:, t, :])\
                      .then_inc(rows[NC if b else c], 16)
                    if causal:
                        sp.dma_start(AD[:, NT * b + TC * c:NT * b + TC * (c + 1), :], add(b)[:, t, :])\
                          .then_inc(rows[NC if b else c], 16)
            def store_rows(b):
                sp.wait_ge(sum_ready, NC * (b + 1))
                sp.dma_start(x_out(b), X[:, NT * b:NT * (b + 1), :]).then_inc(x_stored, 16)
                sp.wait_ge(y0_ready, NC * (b + 1))
                sp.dma_start(h_out(b), AD[:, NT * b:NT * (b + 1), :]).then_inc(x_stored, 16)

            for k in range(N // TC):
                b, c = divmod(k, NC)
                sp.wait_ge(pbd_ready, TC * (k + 1))
                sp.wait_ge(pba_ready, TC * (k + 1))
                sp.dma_start(pt[b].rearrange("n p t -> p n t")[:, :, c * QC:(c + 1) * QC], PB[:, k % 2, :, :])\
                  .then_inc(pt_stored[k % 2], 16)
                if causal and k in (0, NC):
                    store_rows(k // NC)
            for i in range(2):
                sp.wait_ge(pt_stored[i], 16 * (N // TC // 2))
            if causal:
                sp.wait_ge(x_stored, 32 * B)

        @block.gpsimd
        def _(pool):
            pool.memset(hT[:, :, :, 0:2], 0.0).then_inc(zeroed, 1)
            pool.memset(V[:, :, :, D:VW], 1.0).then_inc(zeroed, 1)
            pool.wait_ge(zeroed, 2)
            if causal:
                for k in range(B * NC):
                    t = slice(TC * k, TC * (k + 1))
                    if k < NC:
                        pool.wait_ge(rows[k], 32)
                    elif k == NC:
                        pool.wait_ge(rows[NC], 32 * NC)
                    pool.tensor_tensor(X[:, t, :], X[:, t, :], AD[:, t, :], ALU.add).then_inc(sum_ready, 1)

            def total(n):
                pool.wait_ge(ro_ready, n + 1)
                if n >= 2:
                    pool.wait_ge(hi_ready, n - 1)
                    pool.wait_ge(r1_ready, n - 1)
                pool.tensor_tensor(qk[:, n % 2, :], ra[:, n % 2, :], rb[:, n % 2, :], ALU.add).then_inc(qk_ready, 1)

            if causal:
                total(0)
            for n in range(N + 1):
                if n < N:
                    pool.wait_ge(hi_ready, n + 1)
                    if n >= 2:
                        pool.wait_ge(mid_ready, n - 1)
                        pool.wait_ge(lo_ready, n - 1)
                    pool.tensor_tensor(r1[:, n % 2, :], qk[:, n % 2, :], parts[:, n % 4, 0, :], ALU.subtract)\
                        .then_inc(r1_ready, 1)
                if causal and n + 1 < N:
                    total(n + 1)
                if n:
                    m = n - 1
                    pool.wait_ge(mid_ready, n)
                    pool.tensor_tensor(parts[:, m % 4, 2, :], r1[:, m % 2, :], parts[:, m % 4, 1, :], ALU.subtract)\
                        .then_inc(lo_ready, 1)

        @block.scalar
        def _(act):
            act.dma_start(IDF[:, :], identf).then_inc(consts, 16)
            act.dma_start(IDB[:, :], identb).then_inc(consts, 16)
            act.dma_start(W[:, :, :], w_dram).then_inc(consts, 16)
            if causal:
                act.dma_start(RC[:, :, :, :], rope_c).then_inc(consts, 16)
                act.dma_start(RS[:, :, :, :], rope_s).then_inc(consts, 16)
                act.dma_start(LW[:, :], ln_w).then_inc(consts, 16)
                act.dma_start(LB[:, :], ln_b).then_inc(consts, 16)
                act.dma_start(CW[:, :, :], conv_w).then_inc(consts, 16)
            else:
                act.dma_start(BI[:, :], bias).then_inc(consts, 16)

            def evacuate(n):
                b, i = divmod(n, NT)
                act.wait_ge(tp_done, n + 1)
                t = slice(2 + i * P, 2 + (i + 1) * P)
                if causal:
                    for c in range(CH):
                        last = act.activation(hT[:, c, b, t], pT[n % 2][:, c, :], ACT.Identity,
                                              scale=LW[:, c:c + 1], bias=LB[:, c:c + 1])
                else:
                    last = act.activation(hT[:, :, b, t], pT[n % 2], ACT.Copy)
                last.then_inc(ht_ready, 1)

            def high(n):
                if causal:
                    act.wait_ge(qkv_done, n + 1)
                    act.activation(V[:, n, :, 0:D], pV[n % 2].rearrange("p (h d) -> p h d", h=H), ACT.Copy).then_inc(v_ready, 1)
                act.wait_ge(qk_ready, n + 1)
                if n >= 4:
                    act.wait_ge(pt_done, n - 3)
                act.activation(parts[:, n % 4, 0, :], qk[:, n % 2, :], ACT.Copy).then_inc(hi_ready, 1)

            def middle(n):
                act.wait_ge(r1_ready, n + 1)
                act.activation(parts[:, n % 4, 1, :], r1[:, n % 2, :], ACT.Copy).then_inc(mid_ready, 1)

            def parts_out(n):
                k, i = divmod(n, TC)
                act.wait_ge(pt_done, n + 1)
                if k >= 2:
                    act.wait_ge(pt_stored[k % 2], 16 * (k // 2))
                act.activation(PB[:, k % 2, 6:12, i * P:(i + 1) * P], pP[1], ACT.Copy).then_inc(pba_ready, 1)

            def root(k, i):
                act.wait_ge(var_ready, NSTAT * k + i + 1)
                t = slice(TC * k, TC * (k + 1))
                act.activation(sd[:, t], ve[:, t], ACT.Sqrt).then_inc(sd_ready, 1)

            act.wait_ge(consts, N_CONST)
            for k in (0, 1):
                for i in range(NSTAT):
                    root(k, i)
            act.wait_ge(zeroed, 2)
            for s in range(N + LP + 1):
                if s < N:
                    evacuate(s)
                if 0 <= s - LQ < N:
                    high(s - LQ)
                if 0 <= s - LQ - 1 < N:
                    middle(s - LQ - 1)
                if 0 <= s - LP < N:
                    parts_out(s - LP)
                k, i = divmod(s + TC, TC)
                if k + 1 < B * NC and i in (0, 2) and i // 2 < NSTAT:
                    root(k + 1, i // 2)

        @block.vector
        def _(dve):
            chain = [0]

            def link(ins):
                chain[0] += 1
                ins.then_inc(dch, 1)
                dve.wait_ge(dch, chain[0])

            def variances(k, rows_):
                t = slice(TC * k, TC * (k + 1))
                for n in range(TC * k, TC * (k + 1)):
                    last = dve.bn_stats(st[:, n, :], rows_[:, n, :])
                link(last)
                for n in range(TC * k, TC * (k + 1)):
                    last = dve.bn_aggr(mv[:, n, :], st[:, n, :])
                link(last)
                dve.tensor_scalar(ve[:, t], mv[:, t, 1], EPS, None, ALU.add).then_inc(var_ready, 1)

            def statistics(k, j):
                t = slice(TC * k, TC * (k + 1))
                if j:
                    dve.wait_ge(sd_ready, NSTAT * k + j)
                    link(dve.reciprocal(rs[:, t], sd[:, t]))
                elif causal:
                    dve.wait_ge(sum_ready, k + 1)
                else:
                    dve.wait_ge(rows[min(k, NC)], 16 if k < NC else 16 * NC)
                if j == 0:
                    variances(k, X)
                elif j < NSTAT:
                    for n in range(TC * k, TC * (k + 1)):
                        last = dve.tensor_scalar(AD[:, n, :], X[:, n, :], mv[:, n, 0:1], rs[:, n:n + 1],
                                                 ALU.subtract, ALU.mult)
                    last.then_inc(y0_ready, 1)
                    dve.wait_ge(y0_ready, k + 1)
                    variances(k, AD)

            def normalise(n):
                if n >= 4:
                    dve.wait_ge(tp_done, n - 3)
                dve.tensor_scalar(hn[:, n % 4, :], (AD if causal else X)[:, n, :], mv[:, n, 0:1], rs[:, n:n + 1],
                                  ALU.subtract, ALU.mult).then_inc(hn_ready, 1)

            def convolve(k):
                b, q = divmod(k, NC)
                dve.wait_ge(ht_ready, TC * (k + 1))
                if k >= 2:
                    dve.wait_ge(qkv_done, TC * (k - 1))
                for tap in range(3):
                    for c in range(CH):
                        dst = hc[:, k % 2, c, :]
                        past = hT[:, c, b, q * QC + tap:(q + 1) * QC + tap]
                        if tap == 0:
                            last = dve.tensor_scalar(dst, past, CW[:, c, 0:1], None, ALU.mult)
                        else:
                            last = dve.scalar_tensor_tensor(out=dst, in0=past, scalar=CW[:, c, tap:tap + 1], in1=dst,
                                                            op0=ALU.mult, op1=ALU.add)
                    if tap < 2:
                        link(last)
                last.then_inc(hc_ready, 1)

            def rotate(n):
                i = n % NT
                dve.wait_ge(qkv_done, n + 1)
                s = pQ[n % 2]
                if causal:
                    if n >= 2:
                        dve.wait_ge(qk_ready, n - 1)
                    s4 = s.rearrange("p (a h d) -> p a h d", a=2, h=H)
                    ra4 = ra[:, n % 2, :].rearrange("p (a h d) -> p a h d", a=2, h=H)
                    rb4 = rb[:, n % 2, :].rearrange("p (a h d) -> p a h d", a=2, h=H)
                    half = D // 2
                    for lo in (0, half):
                        hi = half - lo
                        dve.tensor_tensor(rb4[:, :, :, lo:lo + half], s4[:, :, :, hi:hi + half],
                                          RS[:, i, :, lo:lo + half].unsqueeze(2).broadcast_to([P, 2, H, half]), ALU.mult)
                    dve.tensor_tensor(ra4, s4, RC[:, i, :, :].unsqueeze(2).broadcast_to([P, 2, H, D]), ALU.mult)\
                       .then_inc(ro_ready, 1)
                else:
                    if n >= 2:
                        dve.wait_ge(r1_ready, n - 1)
                    dve.scalar_tensor_tensor(out=qk[:, n % 2, 0:C], in0=s[:, 0:C], scalar=D ** -0.5,
                                             in1=BQ[:, :], op0=ALU.mult, op1=ALU.add)
                    dve.tensor_tensor(qk[:, n % 2, C:2 * C], s[:, C:2 * C], BI[:, C:2 * C], ALU.add)
                    dve.tensor_tensor(V[:, n, :, 0:D], pV[n % 2].rearrange("p (h d) -> p h d", h=H),
                                      BI[:, 2 * C:3 * C].rearrange("p (h d) -> p h d", h=H), ALU.add).then_inc(qk_ready, 1)

            def parts_out(n):
                k, i = divmod(n, TC)
                dve.wait_ge(pt_done, n + 1)
                if k >= 2:
                    dve.wait_ge(pt_stored[k % 2], 16 * (k // 2))
                dve.tensor_copy(PB[:, k % 2, 0:6, i * P:(i + 1) * P], pP[0]).then_inc(pbd_ready, 1)

            dve.wait_ge(consts, N_CONST)
            dve.wait_ge(zeroed, 2)
            if not causal:
                link(dve.tensor_scalar(BQ[:, :], BI[:, 0:C], D ** -0.5, None, ALU.mult))
            for j in range(NSTAT + 1):
                statistics(0, j)
            statistics(1, 0)
            for s in range(-AHEAD, N + LP):
                k, j = divmod(s + TC, TC)
                if j == 0 and NSTAT == 2 and k < B * NC:
                    statistics(k, 2)
                if j in (0, 2) and k + 1 < B * NC:
                    statistics(k + 1, j // 2)
                if s + AHEAD < N:
                    normalise(s + AHEAD)
                if causal and s % TC == 0 and 0 < s <= N:
                    convolve(s // TC - 1)
                if 0 <= s - LQ < N:
                    rotate(s - LQ)
                if 0 <= s - LP < N:
                    parts_out(s - LP)

        @block.tensor
        def _(pe):
            def transpose_rows(n):
                pe.wait_ge(hn_ready, n + 1)
                if n >= 2:
                    pe.wait_ge(ht_ready, n - 1)
                for c in range(CH):
                    last = pe.transpose(pT[n % 2][:, c, :], hn[:, n % 4, c * P:(c + 1) * P], IDF[:, :])
                last.then_inc(tp_done, 1)

            def project(n):
                k, i = divmod(n, TC)
                if causal:
                    pe.wait_ge(hc_ready, k + 1)
                else:
                    pe.wait_ge(ht_ready, n + 1)
                if n >= 2:
                    pe.wait_ge(ro_ready if causal else qk_ready, n - 1)
                    if causal:
                        pe.wait_ge(v_ready, n - 1)

                def rows_of(c):
                    if causal:
                        return hc[:, k % 2, c, i * P:(i + 1) * P]
                    return hT[:, c, n // NT, 2 + (n % NT) * P:2 + (n % NT + 1) * P]

                for c in range(CH):
                    pe.matmul(pQ[n % 2], rows_of(c), W[:, c, 0:2 * C], start=(c == 0), stop=(c == CH - 1))
                for c in range(CH):
                    last = pe.matmul(pV[n % 2], rows_of(c), W[:, c, 2 * C:3 * C], start=(c == 0), stop=(c == CH - 1))
                last.then_inc(qkv_done, 1)

            def transpose_parts(n):
                pe.wait_ge(lo_ready, n + 1)
                if n:
                    pe.wait_ge(pbd_ready, n)
                    pe.wait_ge(pba_ready, n)
                for k in range(12):
                    a, f = divmod(k, 4)
                    last = pe.transpose(pP[k // 6][:, k % 6, :], parts[:, n % 4, a, f * P:(f + 1) * P], IDB[:, :])
                last.then_inc(pt_done, 1)

            pe.wait_ge(consts, N_CONST)
            pe.wait_ge(zeroed, 2)
            for s in range(N + LP):
                if s < N:
                    transpose_rows(s)
                if 0 <= s - LQ < N:
                    project(s - LQ)
                if 0 <= s - LP < N:
                    transpose_parts(s - LP)


def attend_phase(nc, PS, V, causal, pt, mask_q, mask_k, identf, identb, m_dram, y_out, early=(), cleared=None):
    ctx = ExitStack()
    with ctx:
        ph = Phase(nc, ctx, "TB" if causal else "TA")
        sb, sem = ph.sb, ph.sem
        GG = B * NG
        E = HG if causal else 1
        if causal:
            STEPS = [(c, kt, max(0, kt - TC * c) * P) for c in range(NC) for kt in range(TC * (c + 1))]
        else:
            STEPS = [(c, TC * c + i, i * P) for c in range(NC) for i in range(TC)]
        NS = len(STEPS)
        START = [min(s for s in range(NS) if STEPS[s][0] == c) for c in range(NC)]
        LAST = [max(s for s in range(NS) if STEPS[s][0] == c) for c in range(NC)]
        PVLAG = 2
        LEAD = LEAD_B if causal else LEAD_A
        NPAR = 2 if causal else 3
        MC = 1 if causal else NC
        MT = TC * MC
        SC = 1 if causal else NC
        NY = 4 if causal else 2
        if causal:
            PAIRS = [[(i, k, p) for i in range(TC) for k in range(c + 1) for p in range(HG // 2)] for c in range(NC)]
        else:
            PAIRS = [[(i, 0, 0) for i in range(0, TC, 2)] for c in range(NC)]

        beside = {}

        def width(c, pair):
            i, k, p = pair
            return min(QC, P * (TC * c + i + 1) - QC * k) if causal else QC

        FIXED = 64
        work = [0]
        for c, kt, off in STEPS:
            work.append(work[-1] + (QC - off if causal else QC) + FIXED)
        units = sum(width(c, pair) + FIXED for c in range(NC) for pair in PAIRS[c])
        done = 0
        for g in range(GG):
            for c in range(NC):
                for pair in PAIRS[c]:
                    done += width(c, pair) + FIXED
                    turn, rest = divmod(done * work[-1] / units - LEAD * work[-1] / NS, work[-1])
                    at = NS * int(turn) + max(s for s in range(NS) if work[s] <= rest)
                    beside.setdefault(at, []).append(("scores", g, c, pair))
                if (c + 1) % MC == 0:
                    beside.setdefault(at + 1, []).append(("maxima", g, c, None))
                beside.setdefault(NS * g + LAST[c] + PVLAG + 2, []).append(("results", g, c, None))
        FIRST, END = min(beside), max(beside) + 1
        order = [item for s in range(FIRST, END) for item in beside.get(s, ())]
        bank, n = {}, 0
        for item in order:
            bank[item] = n
            n += 2 if item[0] == "scores" else 1

        stk = sb("stk", [P, NPAR, 2, HG, T], BF16)
        PR = sb("PR", [P, NP, QC], FP32)
        OT = sb("OT", [P, 2, QC], FP32)
        YO = sb("YO", [P, NY, TC * SC, HG * D], FP32)
        IDF = sb("IDF", [P, P], FP32)
        IDB = sb("IDB", [P, P], BF16)
        ZB = sb("ZB", [P, QC], BF16)
        ZR = sb("ZR", [P, XW], FP32)
        MQ = sb("MQ", [P, HG * P], BF16)
        MK = sb("MK", [P, HG * P], BF16)
        mx = sb("mx", [P, 2, HG * MT, NC if causal else 1], FP32)
        mm = sb("mm", [P, HG * MT], FP32)
        nmb = sb("nmb", [P, 2, HG * MT], BF16)
        nmr = sb("nmr", [HG * MT, 2, P], BF16)
        rden = sb("rden", [P, TC, HG], FP32)
        pM = [PS[:, i, :] for i in range(4)]
        pS = [PS[:, i, :] for i in (4, 5, 6)]
        pO = PS[:, 7, :]

        consts = sem("consts")
        zeroed = sem("zeroed")
        zr_ready = sem("zr_ready") if early else None
        dch = sem("dch")
        stk_loaded = [sem(f"stk_loaded{i}") for i in range(NPAR)]
        rest_loaded = [sem(f"rest_loaded{i}") for i in range(NPAR)]
        m_put = sem("m_put")
        m_got = sem("m_got")
        nm_ready = sem("nm_ready")
        nmr_ready = sem("nmr_ready")
        m_stored = sem("m_stored")
        m_loaded = sem("m_loaded")
        s_done = sem("s_done")
        e_done = sem("e_done")
        pv_done = sem("pv_done")
        ot_ready = sem("ot_ready")
        y_ready = sem("y_ready")
        y_stored = [sem(f"y_stored{i}") for i in range(NY)]
        early_done = sem("early_done") if early else None
        N_LOAD = 2 * NMAX * 2
        N_REST = 2 * (NTERM - NMAX) * 2
        N_STORE = 1 if causal else HG

        block = ctx.enter_context(nc.Block())

        @block.sync
        def _(sp):
            def load_stacks(g):
                b, hg = divmod(g, NG)
                half, r0 = divmod(hg * HG * D, P)
                if g >= NPAR:
                    sp.wait_ge(s_done, E * NS * (g - NPAR + 1))
                for n in range(NTERM):
                    for a in range(2):
                        rows = pt[b, 4 * TERMS[a][n] + 2 * a + half, r0:r0 + HG * D, :]\
                            .rearrange("(j x d) t -> x d j t", x=2, d=D)
                        for x in range(2):
                            r = FIRST_ROW[x] + n * D if n < NMAX else REST_ROW[x] + (n - NMAX) * D
                            sp.dma_start(stk[r:r + D, g % NPAR, a, x::2, :], rows[x])\
                              .then_inc((stk_loaded if n < NMAX else rest_loaded)[g % NPAR], 16)

            sp.dma_start(IDB[:, :], identb).then_inc(consts, 16)
            sp.dma_start(MQ[:, :], mask_q).then_inc(consts, 16)
            sp.dma_start(MK[:, :], mask_k).then_inc(consts, 16)
            sp.dma_start(IDF[:, :], identf).then_inc(consts, 16)
            load_stacks(0)
            for g in range(1, NPAR):
                load_stacks(g)
            later = list(early)
            if cleared is not None:
                step = NE // 5
                later += [(cleared[:, i:i + step, :], ZR[:, :].unsqueeze(1).broadcast_to([P, step, XW]))
                          for i in range(0, NE, step)]
                sp.wait_ge(zr_ready, 1)
            N_EARLY = len(later)
            for n in range(NC * GG):
                g, c = divmod(n, NC)
                if n and c < NC - 1 and later:
                    dst, rows = later.pop(0)
                    sp.dma_start(dst, rows).then_inc(early_done, 16)
                if c == NC - 1 and g + NPAR < GG:
                    load_stacks(g + NPAR)
                if (c + 1) % SC == 0:
                    sp.wait_ge(y_ready, n + 1)
                    k = n // SC
                    for j in range(N_STORE):
                        w = HG * D // N_STORE
                        sp.dma_start(y_out(g // NG, g % NG, c, j), YO[:, k % NY, :, j * w:(j + 1) * w])\
                          .then_inc(y_stored[k % NY], 16)
            if early:
                sp.wait_ge(early_done, 16 * N_EARLY)
            for i in range(NY):
                sp.wait_ge(y_stored[i], 16 * N_STORE * (NC * GG // SC // NY))

        @block.gpsimd
        def _(pool):
            pool.memset(ZB[:, :], 0.0).then_inc(zeroed, 1)
            odd = slice(M_ROW[1], HALF_ROWS)
            view = stk[:, :, :, :, :].rearrange("p g a j t -> p (g a j t)").bitcast(FP32)\
                .rearrange("p (g a j t) -> p g a j t", g=NPAR, a=2, j=HG)
            pool.wait_ge(zeroed, 1)
            for g in range(NPAR):
                pool.memset(view[odd, g, :, 1::2, :], 0.0).then_inc(zeroed, 1)
                pool.wait_ge(zeroed, 2 + 3 * g)
                for x in range(2):
                    pool.memset(view[M_ROW[x]:M_ROW[x] + 1, g, 1, x::2, :], ONES2).then_inc(zeroed, 1)
                    pool.wait_ge(zeroed, 3 + 3 * g + x)
            if cleared is not None:
                pool.memset(ZR[:, :], 0.0).then_inc(zr_ready, 1)
            for n in range(NC * GG // MC):
                g, c = divmod(n, NC // MC)
                pool.wait_ge(nmr_ready, n + 1)
                pool.dma_start(m_dram[n], nmr[:, n % 2, :]).then_inc(m_stored, 16)
                if g >= NPAR:
                    pool.wait_ge(s_done, E * NS * (g - NPAR + 1))
                pool.wait_ge(m_stored, 16 * (n + 1))
                m = m_dram[n].rearrange("(j x i) s -> x j (i s)", x=2, i=MT)
                for x in range(2):
                    pool.dma_start(stk[M_ROW[x]:M_ROW[x] + 1, g % NPAR, 0, x::2, c * MC * QC:(c + 1) * MC * QC],
                                   m[x].unsqueeze(0)).then_inc(m_loaded, 16)

        @block.scalar
        def _(act):
            act.wait_ge(zeroed, 1)
            for s in range(NS * GG + PVLAG + 2):
                for e in range(E):
                    if s < NS * GG:
                        off = STEPS[s % NS][2] if causal else 0
                        n = E * s + e
                        act.wait_ge(s_done, n + 1)
                        if n >= NP:
                            act.wait_ge(pv_done, (n - NP) // E + 1)
                        act.activation(PR[:, n % NP, off:QC], pS[n % 3][:, off:QC], ACT.Exp).then_inc(e_done, 1)
                    if e == 0:
                        g, r = divmod(s - PVLAG - 1, NS)
                        if r in LAST and g >= 0:
                            n = NC * g + LAST.index(r)
                            act.wait_ge(pv_done, NS * g + r + 1)
                            if n >= 2:
                                act.wait_ge(m_got, bank["results", (n - 2) // NC, (n - 2) % NC, None] + 1)
                            act.activation(OT[:, n % 2, :], pO, ACT.Copy).then_inc(ot_ready, 1)

        @block.vector
        def _(dve):
            chain = [0]

            def link(ins):
                chain[0] += 1
                ins.then_inc(dch, 1)
                dve.wait_ge(dch, chain[0])

            def take_scores(g, c, pair, n):
                i, k, p = pair
                par = (NC * g + c) // MC % 2
                for x in range(2):
                    dve.wait_ge(m_put, n + x + 1)
                    s = pM[(n + x) % 4]
                    if causal:
                        w = min(QC, P * (TC * c + i + 1) - QC * k)
                        dve.reduce_max(mx[:, par, TC * (2 * p + x) + i, k:k + 1], s[:, 0:w], AX.X).then_inc(m_got, 1)
                    else:
                        i += TC * c if x == 0 else 0
                        dst = mx[:, par, :, 0].rearrange("p (j x i) -> p x i j", x=2, i=MT)[:, x, i:i + 2, :]
                        dve.reduce_max(dst, s.rearrange("p (i j k) -> p i j k", i=2, j=2), AX.X).then_inc(m_got, 1)

            def take_maxima(g, c, n):
                dve.wait_ge(m_put, n + 1)
                q = (NC * g + c) // MC
                if q >= 2:
                    dve.wait_ge(m_stored, 16 * (q - 1))
                dve.tensor_copy(nmr[:, q % 2, :], pM[n % 4].bitcast(BF16)[0:HG * MT, 0:P]).then_inc(nmr_ready, 1)
                dve.wait_ge(nmr_ready, q + 1)
                dve.sem_inc(m_got, 1)

            def maxima(g, c, n):
                q = (NC * g + c) // MC
                dve.wait_ge(m_got, n)
                if causal:
                    link(dve.reduce_max(mm[:, :], mx[:, q % 2, :, 0:c + 1], AX.X))
                else:
                    link(dve.tensor_copy(mm[:, :], mx[:, q % 2, :, 0]))
                dve.tensor_scalar(nmb[:, q % 2, :], mm[:, :], -1.0, None, ALU.mult).then_inc(nm_ready, 1)
                dve.wait_ge(nm_ready, q + 1)

            def take_results(g, c, n):
                q = NC * g + c
                dve.wait_ge(m_put, n + 1)
                x = pM[n % 4].rearrange("p (i j w) -> p i j w", i=TC, j=HG)
                link(dve.reciprocal(rden[:, :, :], x[:, :, :, D]))
                k = q // SC
                if k >= NY and q % SC == 0:
                    dve.wait_ge(y_stored[k % NY], 16 * N_STORE * (k // NY))
                yo = YO[:, k % NY, q % SC * TC:(q % SC + 1) * TC, :]
                dve.tensor_tensor(yo.rearrange("p i (j d) -> p i j d", j=HG), x[:, :, :, 0:D],
                                  rden[:, :, :].unsqueeze(3).broadcast_to([P, TC, HG, D]), ALU.mult).then_inc(y_ready, 1)
                dve.wait_ge(y_ready, q + 1)
                dve.sem_inc(m_got, 1)

            left = {}
            for kind, g, c, pair in order:
                if kind == "scores":
                    left[g, c] = left.get((g, c), 0) + 1
            for item in order:
                kind, g, c, pair = item
                if kind == "scores":
                    take_scores(g, c, pair, bank[item])
                    left[g, c] -= 1
                    if not left[g, c] and (c + 1) % MC == 0:
                        maxima(g, c, bank[item] + 2)
                elif kind == "maxima":
                    take_maxima(g, c, bank[item])
                else:
                    take_results(g, c, bank[item])

        @block.tensor
        def _(pe):
            def score_max(g, c, pair, n):
                i, k, p = pair
                if n >= 3:
                    pe.wait_ge(m_got, n - 2)
                out = [pM[(n + x) % 4] for x in range(2)]
                if causal:
                    qt = TC * c + i
                    w = min(QC, P * (qt + 1) - QC * k)
                    diagonal = k == c
                    for x in range(2):
                        r = slice(FIRST_ROW[x], FIRST_ROW[x] + HALF_ROWS)
                        j = 2 * p + x
                        last = pe.matmul(out[x][:, 0:w], stk[r, g % NPAR, 0, j, qt * P:(qt + 1) * P],
                                         stk[r, g % NPAR, 1, j, k * QC:k * QC + w], start=True, stop=not diagonal)
                        if not diagonal:
                            last.then_inc(m_put, 1)
                    if diagonal:
                        for x in range(2):
                            pe.matmul(out[x][:, w - P:w], IDB[:, :], MQ[:, 0:P], start=False, stop=True).then_inc(m_put, 1)
                else:
                    for x in range(2):
                        pe.matmul(out[x], IDB[:, :], MQ[:, :], start=True, stop=False)
                    for k in range(4):
                        t, jj = divmod(k, 2)
                        qt = TC * c + i + t
                        for x in range(2):
                            r = slice(FIRST_ROW[x], FIRST_ROW[x] + HALF_ROWS)
                            last = pe.matmul(out[x][:, k * P:(k + 1) * P], stk[r, g % NPAR, 0, 2 * jj + x, qt * P:(qt + 1) * P],
                                             stk[r, g % NPAR, 1, 2 * jj + x, qt * P:(qt + 1) * P],
                                             start=False, stop=k == 3)
                            if k == 3:
                                last.then_inc(m_put, 1)

            def transposes(kind, g, c, n):
                q = NC * g + c
                if n >= 4:
                    pe.wait_ge(m_got, n - 3)
                if kind == "maxima":
                    k = q // MC
                    pe.wait_ge(nm_ready, k + 1)
                    last = pe.transpose(pM[n % 4].bitcast(BF16)[0:HG * MT, 0:P], nmb[:, k % 2, :], IDB[:, :])
                else:
                    pe.wait_ge(ot_ready, q + 1)
                    for i in range(TC):
                        last = pe.transpose(pM[n % 4][:, i * P:(i + 1) * P], OT[:, q % 2, i * P:(i + 1) * P], IDF[:, :])
                last.then_inc(m_put, 1)

            def score(s, e):
                g, r = divmod(s, NS)
                c, kt, off = STEPS[r]
                n = E * s + e
                if e == 0 and r in START and c % MC == 0:
                    pe.wait_ge(m_loaded, 32 * ((NC * g + c) // MC + 1))
                    if c == 0:
                        pe.wait_ge(rest_loaded[g % NPAR], 16 * N_REST * (g // NPAR + 1))
                    if g < NPAR and c == 0:
                        pe.wait_ge(zeroed, 1 + 3 * (g + 1))
                if n >= 3:
                    pe.wait_ge(e_done, n - 2)
                o = pS[n % 3]
                if causal:
                    rows = slice(0, ROWS[e % 2])
                    last = pe.matmul(o[:, off:QC], stk[rows, g % NPAR, 1, e, kt * P:(kt + 1) * P],
                                     stk[rows, g % NPAR, 0, e, c * QC + off:(c + 1) * QC], start=True, stop=kt < TC * c)
                    if kt >= TC * c:
                        last = pe.matmul(o[:, off:off + P], IDB[:, :], MK[:, 0:P], start=False, stop=True)
                else:
                    pe.matmul(o, IDB[:, :], MK[:, :], start=True, stop=False)
                    for j in range(HG):
                        rows = slice(0, ROWS[j % 2])
                        last = pe.matmul(o[:, j * P:(j + 1) * P], stk[rows, g % NPAR, 1, j, kt * P:(kt + 1) * P],
                                         stk[rows, g % NPAR, 0, j, kt * P:(kt + 1) * P], start=False, stop=j == HG - 1)
                last.then_inc(s_done, 1)

            def weigh(s):
                g, r = divmod(s, NS)
                b, hg = divmod(g, NG)
                c, kt, off = STEPS[r]
                pe.wait_ge(e_done, E * (s + 1))
                if r in START:
                    pe.wait_ge(ot_ready, NC * g + c)
                for j in range(HG):
                    if causal:
                        pr = PR[:, (E * s + j) % NP, off:QC]
                        o = pO[HD * j:HD * j + VW, off:QC]
                        first, end = kt == 0, r == LAST[c]
                    else:
                        pr = PR[:, s % NP, j * P:(j + 1) * P]
                        o = pO[HD * j:HD * j + VW, off:off + P]
                        first, end = True, True
                    last = pe.matmul(o, V[:, NT * b + kt, HG * hg + j, :], pr, start=first, stop=end)
                last.then_inc(pv_done, 1)

            pe.wait_ge(consts, 64)
            pe.wait_ge(zeroed, 1)
            pe.matmul(pO, ZB[:, 0:P], ZB[:, :], start=True, stop=True)
            loaded = set()
            for s in range(FIRST, max(END, NS * GG + PVLAG)):
                items = list(beside.get(s, ()))
                for e in range(E):
                    if 0 <= s < NS * GG:
                        score(s, e)
                    if e == min(1, E - 1) and 0 <= s - PVLAG < NS * GG:
                        weigh(s - PVLAG)
                    take = (len(items) + E - 1 - e) // (E - e)
                    for item in items[:take]:
                        kind, g, c, pair = item
                        if kind == "scores":
                            if g not in loaded:
                                loaded.add(g)
                                pe.wait_ge(stk_loaded[g % NPAR], 16 * N_LOAD * (g // NPAR + 1))
                            score_max(g, c, pair, bank[item])
                        else:
                            transposes(kind, g, c, bank[item])
                    items = items[take:]


def router_phase(nc, PS, mem, yB, y0d, x1d, projw, rw, ln2w, ln2b, identf):
    ctx = ExitStack()
    with ctx:
        ph = Phase(nc, ctx, "C")
        sb, sem = ph.sb, ph.sem
        RES, H2, LG = mem.RES, mem.H2, mem.LG
        PW = sb("PW", [P, CH, C], FP32)
        RW = sb("RW", [P, CH, E4], FP32)
        YY = sb("YY", [P, N, C], FP32)
        NR = 4
        yT = sb("yT", [P, NR, CH, P], FP32)
        st = sb("st", [P, N, 6], FP32)
        mv = sb("mv", [P, N, 2], FP32)
        ve = sb("ve", [P, N], FP32)
        sd = sb("sd", [P, N], FP32)
        rs = sb("rs", [P, N], FP32)
        pT = [PS[:, i, 0:C].rearrange("p (c t) -> p c t", c=CH) for i in (0, 1, 2, 3)]
        pP = [PS[:, i, 0:C] for i in (4, 5)]
        pL = PS[:, 6, 0:N * E4]
        NL = N // TC
        consts = sem("consts")
        y_loaded = [sem(f"y_loaded{i}") for i in range(NL)]
        y0_loaded = [sem(f"y0_loaded{i}") for i in range(NL)]
        x1_loaded = sem("x1_loaded")
        t_done = sem("t_done")
        T_ready = sem("T_ready")
        p_done = sem("p_done")
        dch = sem("dch")
        y1_ready = sem("y1_ready")
        var_ready = sem("var_ready")
        sd_ready = sem("sd_ready")
        hn_ready = sem("hn_ready")
        res_ready = sem("res_ready")
        l_done = sem("l_done")
        l_ready = sem("l_ready")
        block = ctx.enter_context(nc.Block())

        @block.sync
        def _(sp):
            sp.dma_start(mem.IDF[:, :], identf).then_inc(consts, 16)
            sp.dma_start(PW[:, :, :], projw).then_inc(consts, 16)
            for k in range(NL + 1):
                if k < NL:
                    t = slice(TC * k, TC * (k + 1))
                    sp.dma_start(YY[:, t, :], yB[:, t, :]).then_inc(y_loaded[k], 16)
                if k:
                    t = slice(TC * (k - 1), TC * k)
                    sp.dma_start(RES[:, t, :], y0d[:, t, :]).then_inc(y0_loaded[k - 1], 16)
            for k in range(NL):
                t = slice(TC * k, TC * (k + 1))
                sp.wait_ge(t_done, TC * (k + 1))
                sp.dma_start(YY[:, t, :], x1d[:, t, :]).then_inc(x1_loaded, 16)
            for dst, s in mem.loads:
                sp.dma_start(dst, s).then_inc(mem.loaded, 16)

        @block.scalar
        def _(act):
            act.dma_start(RW[:, :, :], rw).then_inc(consts, 16)
            act.dma_start(mem.LNW[:, :], ln2w).then_inc(consts, 16)
            act.dma_start(mem.LNB[:, :], ln2b).then_inc(consts, 16)
            act.wait_ge(consts, 80)
            for n in range(2 * N):
                if n == N:
                    act.wait_ge(var_ready, 1)
                    act.activation(sd[:, :], ve[:, :], ACT.Sqrt).then_inc(sd_ready, 1)
                act.wait_ge(t_done, n + 1)
                if n >= NR:
                    if n - NR < N:
                        act.wait_ge(p_done, n - NR + 1)
                    else:
                        act.wait_ge(l_done, n - NR - N + 1)
                if n < N:
                    last = act.activation(yT[:, n % NR, :, :], pT[n % NR], ACT.Copy)
                else:
                    for c in range(CH):
                        last = act.activation(yT[:, n % NR, c, :], pT[n % NR][:, c, :], ACT.Identity,
                                              scale=mem.LNW[:, c:c + 1], bias=mem.LNB[:, c:c + 1])
                last.then_inc(T_ready, 1)

        @block.vector
        def _(dve):
            chain = [0]

            def link(ins):
                chain[0] += 1
                ins.then_inc(dch, 1)
                dve.wait_ge(dch, chain[0])

            dve.wait_ge(consts, 80)
            for n in range(N + 1):
                if n < N:
                    dve.wait_ge(p_done, n + 1)
                    dve.wait_ge(y0_loaded[n // TC], 16)
                    dve.tensor_tensor(RES[:, n, :], pP[n % 2], RES[:, n, :], ALU.add).then_inc(y1_ready, 1)
                if n:
                    dve.wait_ge(y1_ready, n)
                    last = dve.bn_stats(st[:, n - 1, :], RES[:, n - 1, :])
            link(last)
            for n in range(N):
                last = dve.bn_aggr(mv[:, n, :], st[:, n, :])
            link(last)
            dve.tensor_scalar(ve[:, :], mv[:, :, 1], EPS, None, ALU.add).then_inc(var_ready, 1)
            dve.wait_ge(sd_ready, 1)
            link(dve.reciprocal(rs[:, :], sd[:, :]))
            for n in range(N + 1):
                if n < N:
                    dve.tensor_scalar(H2[:, n, :], RES[:, n, :], mv[:, n, 0:1], rs[:, n:n + 1], ALU.subtract, ALU.mult)\
                       .then_inc(hn_ready, 1)
                if n:
                    m = n - 1
                    if m == 0:
                        dve.wait_ge(x1_loaded, 16 * NL)
                    dve.wait_ge(hn_ready, m + 1)
                    dve.tensor_tensor(RES[:, m, :], RES[:, m, :], YY[:, m, :], ALU.add).then_inc(res_ready, 1)
            dve.wait_ge(l_done, N)
            dve.tensor_copy(LG[:, :, :].rearrange("p n e -> p (n e)"), pL).then_inc(l_ready, 1)
            dve.wait_ge(l_ready, 1)

        @block.tensor
        def _(pe):
            def transposes(n):
                m = n % N
                src = YY if n < N else H2
                if n < N:
                    pe.wait_ge(y_loaded[n // TC], 16)
                else:
                    pe.wait_ge(hn_ready, m + 1)
                if n >= NR:
                    pe.wait_ge(T_ready, n - NR + 1)
                for c in range(CH):
                    last = pe.transpose(pT[n % NR][:, c, :], src[:, m, c * P:(c + 1) * P], mem.IDF[:, :])
                last.then_inc(t_done, 1)

            def project(n):
                pe.wait_ge(T_ready, n + 1)
                if n >= 2:
                    pe.wait_ge(y1_ready, n - 1)
                for c in range(CH):
                    last = pe.matmul(pP[n % 2], yT[:, n % NR, c, :], PW[:, c, :], start=(c == 0), stop=(c == CH - 1))
                last.then_inc(p_done, 1)

            def route(n):
                pe.wait_ge(T_ready, N + n + 1)
                for c in range(CH):
                    last = pe.matmul(pL[:, E4 * n:E4 * (n + 1)], yT[:, (N + n) % NR, c, :], RW[:, c, :], start=(c == 0), stop=(c == CH - 1))
                last.then_inc(l_done, 1)

            pe.wait_ge(consts, 80)
            LAG = 2
            for n in range(N + LAG):
                if n < N:
                    transposes(n)
                if n >= LAG:
                    project(n - LAG)
            for n in range(N + LAG):
                if n < N:
                    transposes(N + n)
                if n >= LAG:
                    route(n - LAG)


def expert_phase(nc, PS, mem, wp, xs_dram, xs_tiles, out):
    ctx = ExitStack()
    with ctx:
        ph = Phase(nc, ctx, "D")
        sb, sem = ph.sb, ph.sem
        XR, LG, WV = mem.XR, mem.LG, mem.WV
        WP = sb("WP", [P, E4 * F * C // P], FP32)
        mxl = sb("mxl", [P, N], FP32)
        ge = sb("ge", [P, N, E4], FP32)
        oh = sb("oh", [P, E4, N], FP32)
        ohT = oh[:, :, :].rearrange("p e n -> p n e")
        oh2 = oh[:, :, :].rearrange("p e n -> p (e n)")
        inc_ = sb("inc_", [P, E4, N], FP32)
        tot = sb("tot", [P, E4, N], FP32)
        inc2 = inc_[:, :, :].rearrange("p e n -> p (e n)")
        tot2 = tot[:, :, :].rearrange("p e n -> p (e n)")
        ni = sb("ni", [P, E4], mybir.dt.int32)
        nf = sb("nf", [P, E4], FP32)
        ts = sb("ts", [P, E4], FP32)
        base = sb("base", [P, E4], FP32)
        slotf = sb("slotf", [P, N], FP32)
        slot = sb("slot", [P, N], mybir.dt.uint32)
        cmp_ = sb("cmp_", [1, NE, E4 - 1], FP32)
        eidf = sb("eidf", [1, NE], FP32)
        eid = sb("eid", [1, NE], mybir.dt.int32)
        NX = 3
        xs = sb("xs", [P, NX, XW], FP32)
        xT = sb("xT", [P, 2, CH, P], FP32)
        sg = sb("sg", [P, F], FP32)
        u = sb("u", [P, F], FP32)
        uT = sb("uT", [P, 2, F // P, P], FP32)
        yo = sb("yo", [P, 2, C], FP32)
        dst = sb("dst", [P, 2], mybir.dt.uint32)
        pG = PS[:, 0:4, :].rearrange("p a b -> p (a b)")
        pU = PS[:, 4:6, :].rearrange("p a (b t) -> p (a b) t", t=P)
        pX = PS[:, 6, 0:C].rearrange("p (c t) -> p c t", c=CH)
        pD = PS[:, 7, 0:C]
        pA = PS[:, 0, 0:E4 * N]
        pB = PS[:, 1, 0:E4 * N]
        dch = sem("dch")
        oh_ready = sem("oh_ready")
        cnt_done = sem("cnt_done")
        slot_ready = sem("slot_ready")
        eid_ready = sem("eid_ready")
        scattered = sem("scattered")
        wp_loaded = sem("wp_loaded")
        xs_loaded = [sem(f"xs_loaded{i}") for i in range(NX)]
        x_tr = sem("x_tr")
        xt_ready = sem("xt_ready")
        gate_done = sem("gate_done")
        g_done = sem("g_done")
        silu_done = sem("silu_done")
        u_ready = sem("u_ready")
        ut_done = sem("ut_done")
        ut_ready = sem("ut_ready")
        d_done = sem("d_done")
        yo_ready = sem("yo_ready")
        dst_ready = sem("dst_ready")
        o_stored = mem.o_stored
        block = ctx.enter_context(nc.Block())

        @block.sync
        def _(sp):
            for e in range(E4):
                step = F * C // P
                sp.dma_start(WP[:, e * step:(e + 1) * step].rearrange("p (f n) -> p f n", n=C), wp[e]).then_inc(wp_loaded, 16)
            sp.wait_ge(scattered, 16 * N)
            for j in range(NE):
                if j >= NX:
                    sp.wait_ge(x_tr, j - NX + 1)
                    sp.wait_ge(dst_ready, j - NX + 1)
                    sp.wait_ge(yo_ready, j - NX + 1)
                sp.dma_start(xs[:, j % NX, :], xs_tiles[j]).then_inc(xs_loaded[j % NX], 16)

        @block.gpsimd
        def _(pool):
            pool.wait_ge(slot_ready, 1)
            for n in range(N):
                pool.indirect_dma_start(xs_dram, bass.IndirectOffsetOnAxis(ap=slot[:, n:n + 1], axis=0),
                                        XR[:, n, :], None).then_inc(scattered, 16)
            for j in range(NE):
                pool.wait_ge(dst_ready, j + 1)
                pool.wait_ge(yo_ready, j + 1)
                pool.indirect_dma_start(out, bass.IndirectOffsetOnAxis(ap=dst[:, j % 2:j % 2 + 1], axis=0),
                                        yo[:, j % 2, :], None, bounds_check=B * T - 1, oob_is_err=False)\
                    .then_inc(o_stored[j % 2], 16)
            for i in range(2):
                pool.wait_ge(o_stored[i], 16 * ((NE - i + 1) // 2))

        @block.scalar
        def _(act):
            for j in range(NE):
                act.wait_ge(gate_done, j + 1)
                if j:
                    act.wait_ge(u_ready, j)
                act.activation(sg[:, :], pG[:, 0:F], ACT.Silu).then_inc(silu_done, 1)
                act.wait_ge(ut_done, j + 1)
                if j >= 2:
                    act.wait_ge(d_done, j - 1)
                act.activation(uT[:, j % 2, :, :], pU, ACT.Copy).then_inc(ut_ready, 1)

        @block.vector
        def _(dve):
            chain = [0]

            def link(ins):
                chain[0] += 1
                ins.then_inc(dch, 1)
                dve.wait_ge(dch, chain[0])

            dve.wait_ge(mem.loaded, 16 * mem.n_loads)
            link(dve.reduce_max(mxl[:, :], LG[:, :, :], AX.X))
            link(dve.tensor_tensor(ge[:, :, :], LG[:, :, :], mxl[:, :].unsqueeze(2).broadcast_to([P, N, E4]), ALU.is_ge))
            link(dve.tensor_tensor(ge[:, :, :], ge[:, :, :], mem.RANK[:, :].unsqueeze(1).broadcast_to([P, N, E4]), ALU.mult))
            link(dve.reduce_max(mxl[:, :], ge[:, :, :], AX.X))
            dve.tensor_tensor(ohT, ge[:, :, :], mxl[:, :].unsqueeze(2).broadcast_to([P, N, E4]), ALU.is_equal).then_inc(oh_ready, 1)
            dve.wait_ge(cnt_done, 1)
            link(dve.tensor_copy(tot2, pB))
            link(dve.tensor_tensor_scan(inc2, mem.RESET[:, :], tot2, 0.0, ALU.mult, ALU.add))
            link(dve.tensor_scalar(nf[:, :], inc_[:, :, N - 1], float(P - 1), None, ALU.add))
            link(dve.tensor_copy(ni[:, :], nf[:, :]))
            link(dve.tensor_scalar(ni[:, :], ni[:, :], 7, None, ALU.logical_shift_right))
            link(dve.tensor_copy(nf[:, :], ni[:, :]))
            link(dve.tensor_tensor_scan(ts[:, :], mem.ONE[:, 0:E4], nf[:, :], 0.0, ALU.mult, ALU.add))
            link(dve.tensor_tensor(ts[:, :], ts[:, :], nf[:, :], ALU.subtract))
            link(dve.tensor_scalar(base[:, :], ts[:, :], float(P), None, ALU.mult))
            link(dve.tensor_tensor(inc2, inc2, tot2, ALU.subtract))
            link(dve.tensor_tensor(inc2, inc2, pA, ALU.add))
            link(dve.tensor_tensor(inc_[:, :, :], inc_[:, :, :], base[:, :].unsqueeze(2).broadcast_to([P, E4, N]), ALU.add))
            link(dve.tensor_tensor(inc2, inc2, oh2, ALU.mult))
            link(dve.reduce_sum(slotf[:, :], inc_[:, :, :].rearrange("p e n -> p n e"), AX.X))
            link(dve.tensor_tensor(XR[:, :, 2 * C], mem.TOK[:, :], slotf[:, :], ALU.subtract))
            dve.tensor_copy(slot[:, :], slotf[:, :]).then_inc(slot_ready, 1)
            link(dve.tensor_tensor(cmp_[:, :, :], mem.TILE[:, :].unsqueeze(2).broadcast_to([1, NE, E4 - 1]),
                                   ts[0:1, 1:E4].unsqueeze(1).broadcast_to([1, NE, E4 - 1]), ALU.is_ge))
            link(dve.reduce_sum(eidf[:, :], cmp_[:, :, :], AX.X))
            dve.tensor_copy(eid[:, :], eidf[:, :]).then_inc(eid_ready, 1)

            def xT_out(j):
                dve.wait_ge(x_tr, j + 1)
                if j >= 2:
                    dve.wait_ge(g_done, j - 1)
                for c in range(CH):
                    last = dve.tensor_scalar(xT[:, j % 2, c, :], pX[:, c, :], mem.LNW[:, c:c + 1], mem.LNB[:, c:c + 1],
                                             ALU.mult, ALU.add)
                last.then_inc(xt_ready, 1)

            def y_out(j):
                dve.wait_ge(d_done, j + 1)
                dve.wait_ge(xs_loaded[j % NX], 16 * (j // NX + 1))
                if j >= 2:
                    dve.wait_ge(o_stored[j % 2], 16 * (j // 2))
                dve.tensor_tensor(dst[:, j % 2:j % 2 + 1], xs[:, j % NX, 2 * C:XW], mem.SLOT[:, j:j + 1], ALU.add).then_inc(dst_ready, 1)
                dve.tensor_tensor(yo[:, j % 2, :], pD, xs[:, j % NX, C:2 * C], ALU.add).then_inc(yo_ready, 1)

            xT_out(0)
            for j in range(NE):
                dve.wait_ge(silu_done, j + 1)
                dve.wait_ge(g_done, j + 1)
                if j:
                    dve.wait_ge(ut_done, j)
                dve.tensor_tensor(u[:, :], sg[:, :], pG[:, F:2 * F], ALU.mult).then_inc(u_ready, 1)
                if j + 1 < NE:
                    xT_out(j + 1)
                if j:
                    y_out(j - 1)
            y_out(NE - 1)

        @block.tensor
        def _(pe):
            pe.wait_ge(mem.loaded, 16 * mem.n_loads)
            pe.wait_ge(oh_ready, 1)
            pe.matmul(pA, mem.LOWER[:, :], oh2, start=True, stop=True)
            pe.matmul(pB, mem.ONE[:, :], oh2, start=True, stop=True).then_inc(cnt_done, 1)

            def rows_in(j):
                pe.wait_ge(xs_loaded[j % NX], 16 * (j // NX + 1))
                if j:
                    pe.wait_ge(xt_ready, j)
                for c in range(CH):
                    last = pe.transpose(pX[:, c, :], xs[:, j % NX, c * P:(c + 1) * P], mem.IDF[:, :])
                last.then_inc(x_tr, 1)

            def up(j, e):
                pe.wait_ge(xt_ready, j + 1)
                for k in range(2 * F // QC):
                    if j and k == 0:
                        pe.wait_ge(silu_done, j)
                    if j and k == F // QC:
                        pe.wait_ge(u_ready, j)
                    for c in range(CH):
                        last = pe.matmul(pG[:, k * QC:(k + 1) * QC], xT[:, j % 2, c, :],
                                         WV[:, bass.ds(e * (CH * 2 * F) + c * 2 * F + k * QC, QC)],
                                         start=(c == 0), stop=(c == CH - 1))
                    if k == F // QC - 1:
                        last.then_inc(gate_done, 1)
                last.then_inc(g_done, 1)

            def hidden(j):
                pe.wait_ge(u_ready, j + 1)
                if j:
                    pe.wait_ge(ut_ready, j)
                for f in range(F // P):
                    last = pe.transpose(pU[:, f, :], u[:, f * P:(f + 1) * P], mem.IDF[:, :])
                last.then_inc(ut_done, 1)

            def down(j, e):
                pe.wait_ge(ut_ready, j + 1)
                if j == 0:
                    pe.wait_ge(wp_loaded, 16 * E4)
                if j:
                    pe.wait_ge(yo_ready, j)
                for f in range(F // P):
                    last = pe.matmul(pD, uT[:, j % 2, f, :], WP[:, bass.ds(e * (F // P * C) + f * C, C)],
                                     start=(f == 0), stop=(f == F // P - 1))
                last.then_inc(d_done, 1)

            pe.wait_ge(eid_ready, 1)
            rows_in(0)
            before = None
            for j in range(NE):
                e = pe.value_load(eid[0:1, j:j + 1], min_val=0, max_val=E4 - 1)
                up(j, e)
                if j + 1 < NE:
                    rows_in(j + 1)
                if j:
                    down(j - 1, before)
                hidden(j)
                before = e
            down(NE - 1, before)


class Memory:
    pass


def expert_layer(nc, PS, WV, yB, y0d, x1d, projw, rw, ln2w, ln2b, wp, rank, reset, lower, tiles, one, tok, slots, identf, xs_rows, out, o_stored):
    ctx = ExitStack()
    with ctx:
        ph = Phase(nc, ctx, "M")
        mem = Memory()
        mem.XR = ph.sb("XR", [P, N, XW], FP32)
        mem.H2 = mem.XR[:, :, 0:C]
        mem.RES = mem.XR[:, :, C:2 * C]
        mem.TOK = ph.sb("TOK", [P, N], FP32)
        mem.SLOT = ph.sb("SLOT", [P, NE], FP32)
        mem.LNW = ph.sb("LNW", [P, CH], FP32)
        mem.LNB = ph.sb("LNB", [P, CH], FP32)
        mem.LG = ph.sb("LG", [P, N, E4], FP32)
        mem.WV = WV
        mem.o_stored = o_stored
        mem.IDF = ph.sb("IDF", [P, P], FP32)
        mem.RANK = ph.sb("RANK", [P, E4], FP32)
        mem.RESET = ph.sb("RESET", [P, E4 * N], FP32)
        mem.LOWER = ph.sb("LOWER", [P, P], FP32)
        mem.ONE = ph.sb("ONE", [P, P], FP32)
        mem.TILE = ph.sb("TILE", [1, NE], FP32)
        mem.loaded = ph.sem("loaded")
        loads = [(mem.RANK[:, :], rank), (mem.RESET[:, :], reset), (mem.LOWER[:, :], lower),
                 (mem.ONE[:, :], one), (mem.TILE[:, :], tiles), (mem.TOK[:, :], tok), (mem.SLOT[:, :], slots)]
        mem.n_loads = len(loads)
        mem.loads = loads

        def across(t):
            return t.rearrange("(n p) c -> p n c", p=P)

        router_phase(nc, PS, mem, across(yB), across(y0d), across(x1d), projw, rw, ln2w, ln2b, identf)
        expert_phase(nc, PS, mem, wp, xs_rows, xs_rows.rearrange("(n p) c -> n p c", p=P), out)


def build(nc, x, wA, bA, ln1w, ln1b, cw, wB, ropec, ropes, mqk, mkq, bqk, identf, identb, projw, rw, ln2w, ln2b, wv, wp,
          rank, reset, lower, tiles, one, tok, slots, ptA, ptB, mA, mB, att, x1d, y0d, yB, xs, out):
    with ExitStack() as ctx:
        PS = ctx.enter_context(nc.psum_tensor("PS", [P, 8, QC], FP32))

        o_stored = [ctx.enter_context(nc.semaphore(f"o_stored{i}")) for i in range(2)]

        def batch(t):
            r = t.rearrange("(b i p) c -> b p i c", b=B, p=P)
            return lambda b: r[b]

        att_heads = att.rearrange("r c -> (r c)").rearrange("(b g h i s d) -> b g h s i d", b=B, g=NG, h=HG, i=NT, d=D)
        y_rows = yB.rearrange("(b c i s) (g w) -> b g c s i w", b=B, c=NC, i=TC, g=NG)
        with nc.sbuf_tensor("V", [P, N, H, VW], FP32) as V:
            project_phase(nc, PS, V, False, batch(x), None, wA, bA, None, None, None, None, None, identf, identb, ptA, None, None)
            attend_phase(nc, PS, V, False, ptA, bqk, bqk, identf, identb, mA, lambda b, g, c, j: att_heads[b, g, j])
            project_phase(nc, PS, V, True, batch(x), batch(att), wB, None, ln1w, ln1b, cw, ropec, ropes, identf, identb,
                          ptB, batch(x1d), batch(y0d))
            WV = ctx.enter_context(nc.sbuf_tensor("WV", [P, E4 * CH * 2 * F], FP32, side="right"))
            step = CH * 2 * F
            early = [(WV[:, e * step:(e + 1) * step].rearrange("p (c n) -> p c n", c=CH), wv[e]) for e in range(E4)]
            attend_phase(nc, PS, V, True, ptB, mqk, mkq, identf, identb, mB, lambda b, g, c, j: y_rows[b, g, c],
                         early, xs.rearrange("(n p) c -> p n c", p=P))
        expert_layer(nc, PS, WV, yB, y0d, x1d, projw, rw, ln2w, ln2b, wp, rank, reset, lower, tiles, one, tok, slots, identf, xs, out, o_stored)


def kernel(**inputs):
    import ml_dtypes
    import numpy as np
    import concourse.bacc as bacc
    from concourse.bass_utils import run_bass_kernel_spmd as run

    def lay(name):
        return np.ascontiguousarray(inputs[name])

    def halves(w):
        return np.ascontiguousarray(w.reshape(CH, P, -1).transpose(1, 0, 2))

    def col(v):
        return np.ascontiguousarray(v.reshape(CH, P).T)

    inv = (1.0 / (10000.0 ** (np.arange(0, D, 2, dtype=np.float32) / np.float32(D)))).astype(np.float32)
    ang = (np.arange(T, dtype=np.float32)[:, None] * inv[None]).astype(np.float32)
    cos = np.concatenate([np.cos(ang)] * 2, -1).astype(np.float32)
    sin = np.concatenate([-np.sin(ang), np.sin(ang)], -1).astype(np.float32)

    def table(t):
        t = np.stack([t * np.float32(D ** -0.5), t], 1)
        return np.ascontiguousarray(t.reshape(NT, P, 2, D).transpose(1, 0, 2, 3).astype(np.float32))

    neg = np.float32(-1e30)
    r = np.arange(P)
    qk_mask = np.where(r[None] <= r[:, None], np.float32(0), neg)
    block_mask = np.where(r[None] // 32 == r[:, None] // 32, np.float32(0), neg)
    bf = ml_dtypes.bfloat16
    wq = lay("L0_attn_w_qkv")
    arrays = {
        "x": lay("L0_attn_hidden_states").reshape(B * T, C),
        "wA": halves(np.ascontiguousarray(wq.T)),
        "bA": np.ascontiguousarray(np.broadcast_to(lay("L0_attn_b_qkv")[None], (P, 3 * C))),
        "ln1w": col(lay("L0_ffn_ln1_w")), "ln1b": col(lay("L0_ffn_ln1_b")),
        "cw": halves(lay("L0_ffn_conv_w").reshape(C, 3)),
        "wB": halves(lay("L0_ffn_attn_w")),
        "ropec": table(cos), "ropes": table(sin),
        "mqk": np.tile(qk_mask, (1, HG)).astype(bf), "mkq": np.tile(qk_mask.T, (1, HG)).astype(bf),
        "bqk": np.tile(block_mask, (1, HG)).astype(bf),
        "identf": np.eye(P, dtype=np.float32), "identb": np.eye(P, dtype=np.float32).astype(bf),
    }
    arrays.update({
        "projw": halves(lay("L0_ffn_proj_w")), "rw": halves(lay("L0_ffn_router_w")),
        "ln2w": col(lay("L0_ffn_ln2_w")), "ln2b": col(lay("L0_ffn_ln2_b")),
        "wv": np.ascontiguousarray(lay("L0_ffn_expert_wv").reshape(E4, CH, P, 2 * F).transpose(0, 2, 1, 3)),
        "wp": np.ascontiguousarray(lay("L0_ffn_expert_proj").reshape(E4, F // P, P, C).transpose(0, 2, 1, 3)),
        "rank": np.ascontiguousarray(np.broadcast_to(np.arange(E4, 0, -1, dtype=np.float32)[None], (P, E4))),
        "reset": np.ascontiguousarray(np.broadcast_to((np.arange(E4 * N) % N != 0).astype(np.float32)[None], (P, E4 * N))),
        "lower": (r[:, None] < r[None]).astype(np.float32),
        "tiles": np.arange(NE, dtype=np.float32)[None],
        "one": np.ones((P, P), np.float32),
        "tok": np.ascontiguousarray(np.arange(B * T, dtype=np.float32).reshape(N, P).T) - np.float32(B * T),
        "slots": np.ascontiguousarray(np.arange(NE * P, dtype=np.float32).reshape(NE, P).T) + np.float32(B * T),
    })
    nc = bacc.Bacc("TRN2", target_bir_lowering=False, num_devices=1)
    args = [nc.dram_tensor(k + "_dram", a.shape, mybir.dt.from_np(a.dtype), kind="ExternalInput").ap() for k, a in arrays.items()]
    for k in ("ptA", "ptB"):
        args.append(nc.dram_tensor(k + "_dram", (B, 12, P, T), BF16, kind="Internal").ap())
    for k, n in (("mA", 1), ("mB", NC)):
        args.append(nc.dram_tensor(k + "_dram", (B * NG * n, HG * NT // n, P), BF16, kind="Internal").ap())
    for k, rows in (("att", B * T), ("x1d", B * T), ("y0d", B * T), ("yB", B * T), ("xs", NE * P)):
        args.append(nc.dram_tensor(k + "_dram", (rows, XW if k == "xs" else C), FP32, kind="Internal").ap())
    o = nc.dram_tensor("out_dram", (B * T, C), FP32, kind="ExternalOutput").ap()
    args.append(o)
    build(nc, *args)
    res = run(nc, [{k + "_dram": a for k, a in arrays.items()}], core_ids=[0])
    return res.results[0]["out_dram"].reshape(B, T, C)
```
